# Optimizing a Trainium2 kernel written in Bass

```python
import numpy as np
import jax
import jax.numpy as jnp

def _softmax(x, axis=-1):
    return jax.nn.softmax(x, axis=axis)

def _gelu(x):
    return jax.nn.gelu(x, approximate=True)

def _silu(x):
    return jax.nn.silu(x)

def _sigmoid(x):
    return jax.nn.sigmoid(x)

def _layernorm(x, axis=-1, eps=1e-05):
    m = jnp.mean(x, axis=axis, keepdims=True)
    v = jnp.var(x, axis=axis, keepdims=True)
    return (x - m) / jnp.sqrt(v + eps)

def _scatter_add(tgt, idx, src, axis=0):
    return tgt.at[idx].add(src)

def _segment_sum(src, seg, n):
    return jax.ops.segment_sum(src, seg, n)
kernel_name = 'mk_gps_d1_gnn_r8_a2d5f0'

def setup_inputs(seed: int=0):
    np.random.seed(seed)
    _w = jnp.asarray

    def _rec_inputs():
        import jax
        import jax.numpy as jnp
        _gk = jax.random.key(seed)
        x = -8.776e-05 + 1 * jax.random.normal(jax.random.fold_in(_gk, 1), (1250, 512), jnp.float32)
        src = jax.random.randint(jax.random.fold_in(_gk, 2), (20000,), 0, 1250, jnp.int32)
        dst = jnp.minimum((1250 * jax.random.uniform(jax.random.fold_in(_gk, 3), (20000,)) ** 2.0).astype(jnp.int32), 9999)
        _o = jnp.argsort(dst, stable=True)
        src = src[_o]
        dst = dst[_o]
        return (x, src, dst)
    x, src, dst = _rec_inputs()

    def _L0_gnn_setup():
        import jax, jax.numpy as jnp
        import numpy as np
        N_NODES = 1250

        def gnn_layer(x, W, b, src, dst):
            h = x @ W.T + b
            msgs = h[src]
            agg = jax.ops.segment_sum(msgs, dst, num_segments=N_NODES)
            return jax.nn.relu(agg)
        key = jax.random.key(seed)
        ks = jax.random.split(key, 6)
        d_in, d_hid, d_out = (512, 512, 512)
        E = 20000
        x = jax.random.normal(ks[0], (N_NODES, d_in), dtype=jnp.float32)
        edge_index = jax.random.randint(ks[1], (2, E), 0, N_NODES, dtype=jnp.int64)
        s_in = 1.0 / np.sqrt(d_in)
        s_hid = 1.0 / np.sqrt(d_hid)
        W1 = jax.random.uniform(ks[2], (d_hid, d_in), jnp.float32, -s_in, s_in)
        b1 = jax.random.uniform(ks[3], (d_hid,), jnp.float32, -s_in, s_in)
        W2 = jax.random.uniform(ks[4], (d_out, d_hid), jnp.float32, -s_hid, s_hid)
        b2 = jax.random.uniform(ks[5], (d_out,), jnp.float32, -s_hid, s_hid)
        return {'x': x, 'edge_index': edge_index, 'W1': W1, 'b1': b1, 'W2': W2, 'b2': b2}
    _L0_gnn_all = _L0_gnn_setup()
    _L0_gnn_in = {k: v for k, v in _L0_gnn_all.items() if k in ('W1', 'b1', 'W2', 'b2')}
    del _L0_gnn_all

    def _L0_mix_setup():
        import jax, jax.numpy as jnp
        import numpy as np
        B, N, C = (8, 512, 512)
        key = jax.random.key(seed)
        ks = jax.random.split(key, 6)
        s = 1.0 / np.sqrt(C)
        return {'x': jax.random.normal(ks[0], (B, N, C), jnp.float32), 'Wq': jax.random.normal(ks[1], (C, C), jnp.float32) * s, 'Wk': jax.random.normal(ks[2], (C, C), jnp.float32) * s, 'Wv': jax.random.normal(ks[3], (C, C), jnp.float32) * s, 'W1': jax.random.normal(ks[4], (C, C), jnp.float32) * s, 'W2': jax.random.normal(ks[5], (C, C), jnp.float32) * s}
    _L0_mix_all = _L0_mix_setup()
    _L0_mix_in = {k: v for k, v in _L0_mix_all.items() if k in ('Wq', 'Wk', 'Wv', 'W1', 'W2')}
    del _L0_mix_all

    def _L0_ffn_setup():
        import jax, jax.numpy as jnp
        import numpy as np
        EPS = 1e-06
        SINKHORN_ITERS = 8
        TEMPERATURE = 1.0
        B, N, D = (4, 1024, 512)
        E, OUT = (8, 512)
        H = 1

        def _sinkhorn(logits):
            t = jnp.log(jnp.clip(logits, EPS)) / TEMPERATURE
            for _ in range(SINKHORN_ITERS):
                t = t - jax.nn.logsumexp(t, axis=-2, keepdims=True)
                t = t - jax.nn.logsumexp(t, axis=-1, keepdims=True)
            return jnp.exp(t)
        key = jax.random.key(seed)
        k1, k2, k3 = jax.random.split(key, 3)
        x = jax.random.normal(k1, (B, N, D), dtype=jnp.float32)
        gate_weight = jax.random.normal(k2, (H, D, E), dtype=jnp.float32)
        experts = jax.random.normal(k3, (E, D, OUT), dtype=jnp.float32) * 0.02
        return {'x': x, 'gate_weight': gate_weight, 'experts': experts}
    _L0_ffn_all = _L0_ffn_setup()
    _L0_ffn_in = {k: v for k, v in _L0_ffn_all.items() if k in ('gate_weight', 'experts')}
    del _L0_ffn_all
    return {'x': x, 'src': src, 'dst': dst, 'L0_gnn_W1': _L0_gnn_in['W1'], 'L0_gnn_b1': _L0_gnn_in['b1'], 'L0_gnn_W2': _L0_gnn_in['W2'], 'L0_gnn_b2': _L0_gnn_in['b2'], 'L0_mix_Wq': _L0_mix_in['Wq'], 'L0_mix_Wk': _L0_mix_in['Wk'], 'L0_mix_Wv': _L0_mix_in['Wv'], 'L0_mix_W1': _L0_mix_in['W1'], 'L0_mix_W2': _L0_mix_in['W2'], 'L0_ffn_gate_weight': _L0_ffn_in['gate_weight'], 'L0_ffn_experts': _L0_ffn_in['experts']}

def reference(x, src, dst, L0_gnn_W1, L0_gnn_b1, L0_gnn_W2, L0_gnn_b2, L0_mix_Wq, L0_mix_Wk, L0_mix_Wv, L0_mix_W1, L0_mix_W2, L0_ffn_gate_weight, L0_ffn_experts):
    import jax
    import jax.numpy as jnp

    def _L0_gnn_ref(x, edge_index, W1, b1, W2, b2):
        import jax, jax.numpy as jnp
        import numpy as np
        N_NODES = 1250

        def gnn_layer(x, W, b, src, dst):
            h = x @ W.T + b
            msgs = h[src]
            agg = jax.ops.segment_sum(msgs, dst, num_segments=N_NODES)
            return jax.nn.relu(agg)
        src, dst = (edge_index[0], edge_index[1])
        h = gnn_layer(x, W1, b1, src, dst)
        out = gnn_layer(h, W2, b2, src, dst)
        return out

    def _L0_mix_ref(x, Wq, Wk, Wv, W1, W2):
        import jax, jax.numpy as jnp
        import numpy as np
        B, N, C = (8, 512, 512)
        q = x @ Wq.T
        k = x @ Wk.T
        v = x @ Wv.T
        dim = q.shape[-1]
        q = jax.nn.softmax(q, axis=-1) * dim ** (-0.5)
        k = jax.nn.softmax(k, axis=-2)
        context = jnp.einsum('bnd,bne->bde', k, v)
        attn = jnp.einsum('bnd,bde->bne', q, context)
        x = attn + x
        return x @ W1.T @ W2.T + x

    def _L0_ffn_ref(x, gate_weight, experts):
        import jax, jax.numpy as jnp
        import numpy as np
        EPS = 1e-06
        SINKHORN_ITERS = 8
        TEMPERATURE = 1.0
        B, N, D = (4, 1024, 512)
        E, OUT = (8, 512)
        H = 1

        def _sinkhorn(logits):
            t = jnp.log(jnp.clip(logits, EPS)) / TEMPERATURE
            for _ in range(SINKHORN_ITERS):
                t = t - jax.nn.logsumexp(t, axis=-2, keepdims=True)
                t = t - jax.nn.logsumexp(t, axis=-1, keepdims=True)
            return jnp.exp(t)
        b, n, d = x.shape
        e = experts.shape[0]
        m = n // e
        xh = x[:, None, :, :]
        gate_logits = jnp.einsum('bhnd,hde->bhne', xh, gate_weight)
        gates = _sinkhorn(gate_logits)
        g_t = jnp.swapaxes(gates, -1, -2)
        vals, idx = jax.lax.top_k(g_t, m)
        gate_values = jnp.transpose(vals, (2, 0, 1, 3))[..., None]
        routed = jnp.take_along_axis(xh[:, :, None, :, :], idx[..., None], axis=3)
        routed = jnp.transpose(routed, (2, 0, 1, 3, 4))
        expert_w = experts[:, None, :, :]
        outputs = jnp.einsum('ebhmi,ehio->ebhmo', routed, expert_w)
        outputs = outputs * gate_values
        bh_idx = idx.reshape(b, 1, e * m)
        bh_vals = jnp.transpose(outputs, (1, 2, 0, 3, 4)).reshape(b, 1, e * m, outputs.shape[-1])

        def scat(i1, v1):
            return jnp.zeros((n, v1.shape[-1]), dtype=v1.dtype).at[i1].set(v1)
        routed_back = jax.vmap(jax.vmap(scat))(bh_idx, bh_vals)
        return routed_back[:, 0]
    edge_index = jnp.stack([src, dst])
    xn = _layernorm(x, axis=-1)
    x = x + _L0_gnn_ref(xn, edge_index, L0_gnn_W1, L0_gnn_b1, L0_gnn_W2, L0_gnn_b2) + _L0_mix_ref(xn[None], L0_mix_Wq, L0_mix_Wk, L0_mix_Wv, L0_mix_W1, L0_mix_W2)[0]
    x = x + _L0_ffn_ref(_layernorm(x, axis=-1)[None], L0_ffn_gate_weight, L0_ffn_experts)[0]
    return x

_drawn_inputs = setup_inputs


def setup_inputs(seed=0):
    import zlib

    import numpy as np

    out = dict(_drawn_inputs(seed))
    spreads = {}
    factors = {'L0_mix_Wq': 8.0, 'L0_mix_Wk': 8.0, 'L0_mix_Wv': 8.0, 'L0_ffn_gate_weight': 2.889}
    for name, (base, spread) in spreads.items():
        noise = np.random.default_rng([zlib.crc32(name.encode()), seed]).standard_normal(out[name].shape)
        drawn = base * np.exp(spread * noise) if base else spread * noise
        out[name] = jnp.asarray(drawn.astype(out[name].dtype))
    for name, factor in factors.items():
        out[name] = (out[name] * factor).astype(out[name].dtype)
    return out
```

```python
from contextlib import ExitStack

import numpy as np

import concourse.bass as bass
from concourse import mybir

ALU = mybir.AluOpType
ACT = mybir.ActivationFunctionType
F32 = mybir.dt.float32
F32R = mybir.dt.float32r
BF16 = mybir.dt.bfloat16
F16 = mybir.dt.float16
I32 = mybir.dt.int32
U32 = mybir.dt.uint32
I8 = mybir.dt.int8
AX = mybir.AxisListType.X

N, D, E = 1250, 512, 20000
NE, TOPK = 8, 1250 // 8
TT = 125
NT = N // TT
C = D // 128
ET = 125
NG = E // (2 * ET)
DB = 64
NB = -(-N // DB)
NPAD = NB * DB
CHUNKS = [(0, 418), (418, 416), (834, 416)]
EXACT = 4096.0
LN_EPS, CLIP_EPS, SINKHORN = 1e-5, 1e-6, 8
SLOT = TOPK // 2
NS = NE * 2
RING = 4
SHIFTS = [27, 23, 19, 15, 11, 7, 3, 0]
KB = 1024


def psum_plan():
    uses, filled, readers, turn = {}, [0] * 8, [[] for _ in range(8)], {}

    def use(name, banks, *read_by):
        k = turn.get(banks, 0)
        turn[banks] = k + 1
        b = banks[k % len(banks)]
        uses[name] = (b, filled[b] + 1, readers[b])
        filled[b] += 1
        readers[b] = list(read_by)

    low, high, every = (0, 1, 2, 3), (4, 5, 6, 7), tuple(range(8))
    use("bounds", (7,), ("blen_ready", 1))
    use("bases", (6,), ("tab_ready", 1))
    for c in range(C):
        use(f"mp{c}", low, ("mt_ready", c + 1))
    for i in range(NT):
        use(f"xt{i}", high, ("xth_ready", i + 1), ("xtl_ready", i + 1))
    for i in range(NT):
        use(f"k{i}", low, ("k_stored", i + 1), ("kmax_step", i + 1))
    for i in range(NT):
        if i == 4:
            use("kmt", (4,), ("diag_ready", 1))
        if i == 7:
            use("kmb", (4,), ("k_shift", NT))
        use(f"q{i}", (5, 6, 7), ("rmax_ready", i + 1), ("q_exp", i + 1))
    for i in range(NT):
        use(f"xm{i}", low, ("xm_added", i + 1))
    for c in range(C):
        use(f"vp{c}", (5, 6, 7), ("vph_ready", c + 1), ("vpl_ready", c + 1))
    for c in range(C):
        use(f"tt{c}", low, ("th_ready", c + 1), ("tl_ready", c + 1))
    use("ks", (4,), ("krs_ready", 1))
    for c in range(C):
        use(f"cp{c}", low, ("cph_ready", c + 1), ("cpl_ready", c + 1))
    for b in high:
        uses[f"adj{b}"] = (b, None, readers[b])
        readers[b] = [("adj_hi", NB), ("adj_lo", NB)]
    for i in range(NT):
        use(f"qt{i}", (0, 1), ("qth_ready", i + 1), ("qtl_ready", i + 1))
        use(f"qp{i}", (2, 3), ("qp_added", i + 1))
    use("flag", (0,), ("flag_ready", 1))
    for layer in (1, 2):
        for ch in range(3):
            for f in range(C):
                n = ((layer - 1) * 3 + ch) * C + f + 1
                use(f"z{layer}_{ch}_{f}", every, ("zh_ready", n), ("zl_ready", n))
            if layer == 1:
                use(f"deg{ch}", every, ("degrow_ready", ch + 1))
        if layer == 1:
            use("degt", (7,), ("deg_ready", 1))
            for i in range(NT):
                use(f"h{i}", low, ("h1h_ready", i + 1), ("h1l_ready", i + 1))
    for i in range(NT):
        use(f"o{i}", low, ("x_final", i + 1))
    for i in range(NT):
        use(f"yt{i}", (4, 5), ("yt_ready", i + 1))
    use("logits", (6,), ("p_ready", 1))
    for r in range(SINKHORN):
        use(f"sink{r}", (3, 0), ("p_ready", r + 2))
    for h in range(3):
        use(f"gt{h}", (1, 2, 3), ("gt_ready", h + 1))
    for r in range(len(SHIFTS)):
        use(f"rad{r}", (0,), ("prefix_ready", r + 1))
    use("sel", (1,), ("rowtot_ready", 1))
    use("off", (2,), ("route_ready", 1))
    use("slots", (3,), ("idx_ready", 1))
    for j in range(NS):
        use(f"ft{j}", (0, 1), ("fth_ready", j + 1), ("ftl_ready", j + 1))
        use(f"fo{j}", (2, 3), ("fo_ready", j + 1))
    return uses


def gps_block(nc, x_in, src_t, dst_t, dst_in, gW1T, gb1, gW2T, gb2, WqT, WkT, Wv, mW1, mW2T,
              gate_w, experts, out):
    plan = psum_plan()
    scratch_y = nc.dram_tensor("scratch_y", [N, D], F32).ap()
    scratch_x = nc.dram_tensor("scratch_x", [N, D], F32).ap()

    with ExitStack() as ctx:
        base = nc.sbuf_base + (-nc.sbuf_base) % 32

        def at(name, shape, dt, off):
            return nc.alloc_sbuf_tensor_at(name, shape, dt, offset=base + int(off))

        areas = {"a": [int(162.5 * KB), 168 * KB], "b": [204 * KB, int(207.7 * KB)],
                 "c": [193 * KB, 204 * KB]}

        def small(name, shape, dt, area):
            size = int(np.prod(shape[1:])) * mybir.dt.size(dt)
            off = areas[area][0]
            areas[area][0] += size + (-size) % 32
            assert areas[area][0] <= areas[area][1], (name, areas[area])
            return at(name, shape, dt, off)

        def sem(name):
            return ctx.enter_context(nc.semaphore(name))

        X = at("X", [128, NT, D], F32, 0)
        XNH = at("XNH", [128, NT, D], F32R, 20 * KB)
        XNL = at("XNL", [128, NT, D], F32R, 40 * KB)
        H1H = at("H1H", [128, NT, D], F32R, 20 * KB)
        H1L = at("H1L", [128, NT, D], F32R, 40 * KB)
        W1H = at("W1H", [128, C, D], F32R, 60 * KB)
        W1L = at("W1L", [128, C, D], F32R, 68 * KB)
        W2H = at("W2H", [128, C, D], F32R, 76 * KB)
        W2L = at("W2L", [128, C, D], F32R, 84 * KB)
        MT = at("MT", [128, C, D], F32, 92 * KB)
        XTH = at("XTH", [128, C, N], F32R, 60 * KB)
        XTL = at("XTL", [128, C, N], F32R, 80 * KB)
        EH = at("EH", [128, 3, D], F32R, 60 * KB)
        EL = at("EL", [128, 3, D], F32R, 66 * KB)
        TH = at("TH", [128, C, D], F32R, 84 * KB)
        TL = at("TL", [128, C, D], F32R, 92 * KB)
        QTH = at("QTH", [128, 2, C, TT + 3], F32R, 60 * KB)
        QTL = at("QTL", [128, 2, C, TT + 3], F32R, 64 * KB)
        HOT_S = at("HOT_S", [128, 2, N], BF16, 68 * KB)
        HOT_D = at("HOT_D", [128, 2, DB], BF16, 73 * KB)
        zero16 = at("zero16", [128, 5 * DB], BF16, 74 * KB)
        ZH = at("ZH", [128, C, N], F32R, 60 * KB)
        ZL = at("ZL", [128, C, N], F32R, 80 * KB)
        XF = at("XF", [128, NT, D], F32, 100 * KB)
        K = at("K", [128, NT, D], F32, 100 * KB)
        WKH = at("WKH", [128, C, D], F32R, 120 * KB)
        WKL = at("WKL", [128, C, D], F32R, 128 * KB)
        WVH = at("WVH", [128, C, D], F32R, 120 * KB)
        WVL = at("WVL", [128, C, D], F32R, 128 * KB)
        WQH = at("WQH", [128, C, D], F32R, 136 * KB)
        WQL = at("WQL", [128, C, D], F32R, 144 * KB)
        VPH = at("VPH", [128, C, D], F32R, 136 * KB)
        VPL = at("VPL", [128, C, D], F32R, 144 * KB)
        RAW_C = at("RAW_C", [128, C, D], F32, 152 * KB)
        KMAX = at("KMAX", [128, D], F32, 160 * KB)
        ESUM = at("ESUM", [128, D], F32, 160 * KB)
        AT = at("AT", [128, NT, NPAD], F32R, 100 * KB)
        AL = at("AL", [128, NT, NPAD], I8, 150 * KB)
        RAW_A = at("RAW_A", [128, C, D], F32, 168 * KB)
        RAW_B = at("RAW_B", [128, C, D], F32, 176 * KB)
        DROW = at("DROW", [128, 2 * ET], I32, 40 * KB)
        EDGE = at("EDGE", [128, 2, 2 * NG], I32, 41 * KB)
        Q = at("Q", [128, NT, D], F32, 168 * KB)
        MPH = at("MPH", [128, C, D], F32R, 188 * KB)
        MPL = at("MPL", [128, C, D], F32R, 196 * KB)
        CPH = at("CPH", [128, C, D], F32R, 188 * KB)
        CPL = at("CPL", [128, C, D], F32R, 196 * KB)
        G1H = at("G1H", [128, C, D], F32R, 168 * KB)
        G1L = at("G1L", [128, C, D], F32R, 176 * KB)
        AC = at("AC", [128, 2, 418], F32R, 184 * KB)
        G2H = at("G2H", [128, C, D], F32R, 188 * KB)
        G2L = at("G2L", [128, C, D], F32R, 196 * KB)
        RAW_G1 = at("RAW_G1", [128, C, D], F32, 188 * KB)
        RAW_G2 = at("RAW_G2", [128, C, D], F32, 168 * KB)
        Y = at("Y", [128, NT, D], F32, 60 * KB)
        YT = at("YT", [128, 2, C, TT + 3], F32, 80 * KB)
        YG = at("YG", [128, NS, D], F32, 60 * KB)
        XG = at("XG", [128, NS, D], F32, 20 * KB)
        FTH = at("FTH", [128, 2, C, SLOT + 2], F32R, 92 * KB)
        FTL = at("FTL", [128, 2, C, SLOT + 2], F32R, 95 * KB)
        FO = at("FO", [128, 4, D], F32, 52 * KB)
        WEH = [at(f"WEH{s}", [128, C, D], F32R, (100 + 16 * s) * KB) for s in range(3)]
        WEL = [at(f"WEL{s}", [128, C, D], F32R, (108 + 16 * s) * KB) for s in range(3)]
        RAW_E = at("RAW_E", [128, C, D], F32, 148 * KB)
        GREP = at("GREP", [128, NT, 128], F32, 168 * KB)
        GT = at("GT", [128, N], F32, 173 * KB)
        RANK = at("RANK", [128, N], F32, 178 * KB)
        M_GT = at("M_GT", [128, N], BF16, 183 * KB)
        M_EQ = at("M_EQ", [128, N], BF16, 185.5 * KB)
        M_TIE = at("M_TIE", [128, N], BF16, 188 * KB)
        M_SEL = at("M_SEL", [128, N], BF16, 190.5 * KB)
        ROUTE = at("ROUTE", [128, NT, NS * SLOT], BF16, 168 * KB)

        ident = small("ident", [128, 128], F32, "a")
        ones = small("ones", [128, 128], F32, "a")
        tri = small("tri", [128, 128], F32, "a")
        iota = small("iota", [128, NPAD], F16, "a")
        srcf = small("srcf", [128, 2 * NG], F32, "a")
        dstf = small("dstf", [128, 2 * NG], F32, "a")
        diag = small("diag", [128, C, 128], F32, "b")
        bias = at("bias", [128, D], F32, 204 * KB)
        stat = small("stat", [128, NT, 6], F32, "b")
        mv = small("mv", [128, NT, 2], F32, "b")
        rstd = small("rstd", [128, 4, NT], F32, "b")
        rmax = small("rmax", [128, NT], F32, "b")
        rsum = small("rsum", [128, 2, NT], F32, "b")
        kmt = small("kmt", [128, C], F32, "b")
        krs = small("krs", [128, 2, C], F32, "b")
        degs = small("degs", [128, NT], F32, "b")
        onesr = small("onesr", [128, 2], F32R, "b")
        odeg = small("odeg", [128, 2, NB], F32, "b")
        many = small("many", [128, 2], F32, "b")
        flag = small("flag", [128, 1], I32, "b")
        tab = small("tab", [128, 2, NB + 2], I32, "b")
        drow = at("drow", [128, N], F32, 196 * KB)
        grp = at("grp", [128, 2], F32, 43 * KB)
        dg2 = at("dg2", [128, 2, NG], F32, 44 * KB)
        blk = at("blk", [128, 2], F32, 43 * KB + 32)
        gio = at("gio", [128, 2, NG], F32, 45 * KB)
        bw = at("bw", [128, 4, NG], F32, 46 * KB)
        blh = at("blh", [128, 6], F32, 43 * KB + 64)
        gw = small("gw", [128, C, NE], F32, "c")
        P8 = small("P8", [128, NT, NE], F32, "c")
        s8 = small("s8", [128, 2, NE], F32, "c")
        s10 = small("s10", [128, 4, NT], F32, "c")
        pick = small("pick", [128, NE], BF16, "c")
        blkones = small("blkones", [128, 128], F32, "c")
        ctab = small("ctab", [128, len(SHIFTS)], I32, "c")
        cb = small("cb", [128, 2], I32, "c")
        pre = small("pre", [128, 4], I32, "c")
        cnt = small("cnt", [128, 8], F32, "c")
        e1 = small("e1", [128, NT, NE], F32, "c")
        e156 = small("e156", [128, NE], F32, "c")
        fin = small("fin", [128, NE, NT], F32, "c")
        incl = small("incl", [128, NE, NT], F32, "c")
        reset = small("reset", [128, NE, NT], F32, "c")
        w8 = small("w8", [128, 2, NE, NT], F32, "c")
        tid = small("tid", [128, 2, NT], I32, "c")
        vals = small("vals", [128, NT, 6], BF16, "c")
        slot = small("slot", [128, NT], F32, "c")
        tokv = small("tokv", [128, 3, NS], F32, "c")
        idx = small("idx", [128, 2, NS], I32, "c")

        PS = [ctx.enter_context(nc.psum_tensor(f"ps{b}", [128, 512], F32)) for b in range(8)]

        def view(name, chunks=C):
            return PS[plan[name][0]].rearrange("p (c t) -> p c t", c=chunks)

        full = [sem(f"bank_full{b}") for b in range(8)]
        ld_x = [sem(f"ld_x{n}") for n in range(5)]
        loads = {n: sem(f"ld_{n}") for n in ("edges", "w1", "w2", "wk", "wq", "wv", "b1", "b2", "g1",
                                             "g2", "gate", "exp")}
        done = {n: sem(n) for n in (
            "consts rconsts w_hi w_lo dve_chain pool_chain var_ready sqrt_ready xf_ready xnh_ready "
            "xnl_ready xth_ready xtl_ready grp_ready blen_ready tab_ready mt_ready mph_ready mpl_ready "
            "k_stored kmax_step diag_ready rmax_ready q_exp q_ready k_shift k_exp eh_ready el_ready "
            "esum_ready krs_ready e_used xm_added vph_ready vpl_ready th_ready tl_ready cph_ready "
            "cpl_ready zero_ready adj_full adj_hi adj_lo qth_ready qtl_ready qp_added flag_in "
            "flag_ready zh_ready zl_ready ac_ready ac_used degrow_ready deg_ready t_ready h1h_ready "
            "h1l_ready x_final y_ready var2_ready sqrt2_ready yt_ready yt_used p_ready grep_ready "
            "gt_ready ind_ready prefix_ready msel_ready rowtot_ready route_ready idx_ready st_y st_x "
            "st_out gathered_x fth_ready ftl_ready fo_ready").split()}
        gathered_y = [sem(f"gathered_y{j}") for j in range(NS)]
        scattered = [sem(f"scattered{s}") for s in range(4)]
        hot = [sem(f"hot_ready{s}") for s in range(2)]
        hot_used = [sem(f"hot_used{s}") for s in range(2)]

        splits = [(RAW_A, W1H, W1L, "w1"), (RAW_B, W2H, W2L, "w2"), (RAW_C, WKH, WKL, "wk"),
                  (RAW_A, WQH, WQL, "wq"), (RAW_C, WVH, WVL, "wv"), (RAW_G1, G1H, G1L, "g1"),
                  (RAW_G2, G2H, G2L, "g2")]
        NW = len(splits)
        order = {s[3]: n + 1 for n, s in enumerate(splits)}

        def reads(eng, name):
            eng.wait_ge(full[plan[name][0]], plan[name][1])

        block = ctx.enter_context(nc.Block())

        @block.sync
        def _(sp):
            def rows(w):
                return w.rearrange("(c p) f -> p c f", p=128)

            def tiles(a, i, n=1):
                return a[TT * i:TT * (i + n), :].rearrange("(i p) f -> p i f", p=TT)

            sp.dma_start(DROW[0:NG, :], dst_in).then_inc(loads["edges"], 16)
            sp.dma_start(EDGE[0:ET, 0, :], src_t).then_inc(loads["edges"], 16)
            sp.dma_start(EDGE[0:ET, 1, :], dst_t).then_inc(loads["edges"], 16)
            sp.dma_start(RAW_A[:], rows(mW1)).then_inc(loads["w1"], 16)
            sp.dma_start(RAW_B[:], rows(mW2T)).then_inc(loads["w2"], 16)
            for n in range(5):
                sp.dma_start(X[0:TT, 2 * n:2 * n + 2, :], tiles(x_in, 2 * n, 2)).then_inc(ld_x[n], 16)
            sp.dma_start(RAW_C[:], rows(WkT)).then_inc(loads["wk"], 16)
            sp.wait_ge(done["w_hi"], order["w1"])
            sp.wait_ge(done["w_lo"], order["w1"])
            sp.dma_start(RAW_A[:], rows(WqT)).then_inc(loads["wq"], 16)
            sp.wait_ge(done["w_hi"], order["wk"])
            sp.wait_ge(done["w_lo"], order["wk"])
            sp.dma_start(RAW_C[:], rows(Wv)).then_inc(loads["wv"], 16)
            sp.wait_ge(done["qp_added"], NT)
            sp.dma_start(RAW_G1[:], rows(gW1T)).then_inc(loads["g1"], 16)
            sp.dma_start(bias[0:TT, :], gb1.rearrange("(a f) -> a f", a=1).broadcast_to([TT, D])).then_inc(loads["b1"], 16)
            reads(sp, f"h{NT - 1}")
            sp.dma_start(RAW_G2[:], rows(gW2T)).then_inc(loads["g2"], 16)
            sp.wait_ge(done["t_ready"], NT)
            sp.dma_start(bias[0:TT, :], gb2.rearrange("(a f) -> a f", a=1).broadcast_to([TT, D])).then_inc(loads["b2"], 16)
            reads(sp, f"z2_2_{C - 1}")
            for e in range(NE):
                if e >= 1:
                    sp.wait_ge(done["w_hi"], NW + e)
                    sp.wait_ge(done["w_lo"], NW + e)
                sp.dma_start(RAW_E[:], rows(experts[e])).then_inc(loads["exp"], 16)
                if e == 0:
                    reads(sp, f"o{NT - 1}")
                    sp.dma_start(gw[:], rows(gate_w[0])).then_inc(loads["gate"], 16)
                    for i in range(NT):
                        sp.wait_ge(done["x_final"], i + 1)
                        sp.dma_start(tiles(out, i), X[0:TT, i:i + 1, :]).then_inc(done["st_out"], 16)
                        sp.dma_start(tiles(scratch_x, i), X[0:TT, i:i + 1, :]).then_inc(done["st_x"], 16)
                    for i in range(NT):
                        sp.wait_ge(done["y_ready"], i + 1)
                        sp.dma_start(tiles(scratch_y, i), Y[0:TT, i:i + 1, :]).then_inc(done["st_y"], 16)
            sp.wait_ge(done["st_out"], 16 * NT)
            for s in range(4):
                sp.wait_ge(scattered[s], 16 * (NS // 4))

        @block.gpsimd
        def _(pool):
            count = [0]

            def link(ins):
                count[0] += 1
                ins.then_inc(done["pool_chain"], 1)
                pool.wait_ge(done["pool_chain"], count[0])

            link(nc.gpsimd.memset(ones[:], 1.0))
            link(nc.gpsimd.affine_select(out=ident[:], in_=ones[:], pattern=[[-1, 128]], compare_op=ALU.is_equal,
                                         fill=0.0, base=0, channel_multiplier=1))
            link(nc.gpsimd.affine_select(out=tri[:], in_=ones[:], pattern=[[1, 128]], compare_op=ALU.is_gt,
                                         fill=0.0, base=0, channel_multiplier=-1))
            link(nc.gpsimd.iota(gio[:, 0, :], [[1, NG]], base=1, channel_multiplier=0,
                                allow_small_or_imprecise_dtypes=True))
            link(nc.gpsimd.iota(gio[:, 1, :], [[-1, NG]], base=NG, channel_multiplier=0,
                                allow_small_or_imprecise_dtypes=True))
            link(nc.gpsimd.iota(blk[:, 0:1], [[0, 1]], base=0, channel_multiplier=DB,
                                allow_small_or_imprecise_dtypes=True))
            link(nc.gpsimd.iota(blk[:, 1:2], [[0, 1]], base=DB - 1, channel_multiplier=DB,
                                allow_small_or_imprecise_dtypes=True))
            nc.gpsimd.iota(iota[:], [[1, NPAD]], base=0, channel_multiplier=0,
                           allow_small_or_imprecise_dtypes=True).then_inc(done["consts"], 1)

            def split_lo(n, raw, hi, lo):
                pool.wait_ge(done["w_hi"], n)
                nc.gpsimd.tensor_tensor(lo[:], raw[:], hi[:].bitcast(F32), ALU.subtract).then_inc(done["w_lo"], 1)

            for n in range(2):
                split_lo(n + 1, *splits[n][:3])
            split_lo(3, *splits[2][:3])
            for i in range(NT):
                pool.wait_ge(done["xnh_ready"], i + 1)
                nc.gpsimd.tensor_tensor(XNL[0:TT, i, :], XF[0:TT, i, :], XNH[0:TT, i, :].bitcast(F32),
                                        ALU.subtract).then_inc(done["xnl_ready"], 1)
                if i == 2:
                    split_lo(4, *splits[3][:3])
            split_lo(5, *splits[4][:3])
            for i in range(NT):
                pool.wait_ge(done["k_exp"], i + 1)
                if i == 0:
                    link(nc.gpsimd.tensor_copy(ESUM[0:TT, :], K[0:TT, 0, :]))
                elif i < NT - 1:
                    link(nc.gpsimd.tensor_tensor(ESUM[0:TT, :], ESUM[0:TT, :], K[0:TT, i, :], ALU.add))
                else:
                    nc.gpsimd.tensor_tensor(ESUM[0:TT, :], ESUM[0:TT, :], K[0:TT, i, :],
                                            ALU.add).then_inc(done["esum_ready"], 1)
            split_lo(6, *splits[5][:3])
            split_lo(7, *splits[6][:3])

            reads(pool, f"o{NT - 1}")
            link(nc.gpsimd.affine_select(out=blkones[:].rearrange("p (e c) -> p e c", c=16),
                                         in_=ones[:].rearrange("p (e c) -> p e c", c=16),
                                         pattern=[[-16, NE], [0, 16]], compare_op=ALU.is_ge, fill=0.0,
                                         base=0, channel_multiplier=1))
            link(nc.gpsimd.affine_select(out=blkones[:].rearrange("p (e c) -> p e c", c=16),
                                         in_=blkones[:].rearrange("p (e c) -> p e c", c=16),
                                         pattern=[[16, NE], [0, 16]], compare_op=ALU.is_ge, fill=0.0,
                                         base=15, channel_multiplier=-1))
            link(nc.gpsimd.affine_select(out=pick[:], in_=ones[:, 0:NE], pattern=[[-16, NE]],
                                         compare_op=ALU.is_equal, fill=0.0, base=0, channel_multiplier=1))
            link(nc.gpsimd.iota(cb[:, 0:1], [[0, 1]], base=0, channel_multiplier=1))
            link(nc.gpsimd.iota(e1[:], [[0, NT], [1, NE]], base=1, channel_multiplier=0,
                                allow_small_or_imprecise_dtypes=True))
            link(nc.gpsimd.iota(e156[:], [[TOPK, NE]], base=0, channel_multiplier=0,
                                allow_small_or_imprecise_dtypes=True))
            link(nc.gpsimd.memset(reset[:], 1.0))
            link(nc.gpsimd.memset(reset[:, :, 0:1], 0.0))
            nc.gpsimd.iota(tid[:, 0, :], [[TT, NT]], base=1, channel_multiplier=1).then_inc(done["rconsts"], 1)

            def split_expert(e):
                if e >= 3:
                    reads(pool, f"fo{2 * (e - 3) + 1}")
                split_lo(NW + e + 1, RAW_E, WEH[e % 3], WEL[e % 3])

            for e in range(3):
                split_expert(e)
            reads(pool, "logits")
            pool.wait_ge(done["st_y"], 16 * NT)
            pool.wait_ge(done["st_x"], 16 * NT)
            pool.wait_ge(done["idx_ready"], 1)
            for j in range(NS):
                nc.gpsimd.indirect_dma_start(
                    out=YG[0:SLOT, j, :], out_offset=None, in_=scratch_y,
                    in_offset=bass.IndirectOffsetOnAxis(ap=idx[0:SLOT, 0, j:j + 1].bitcast(U32), axis=0)).then_inc(gathered_y[j], 16)
            for j in range(NS):
                nc.gpsimd.indirect_dma_start(
                    out=XG[0:SLOT, j, :], out_offset=None, in_=scratch_x,
                    in_offset=bass.IndirectOffsetOnAxis(ap=idx[0:SLOT, 0, j:j + 1].bitcast(U32), axis=0)).then_inc(done["gathered_x"], 16)
            pool.wait_ge(done["st_out"], 16 * NT)
            for j in range(NS):
                pool.wait_ge(done["fo_ready"], j + 1)
                nc.gpsimd.indirect_dma_start(
                    out=out, in_=FO[0:SLOT, j % 4, :], in_offset=None,
                    out_offset=bass.IndirectOffsetOnAxis(ap=idx[0:SLOT, 1, j:j + 1].bitcast(U32), axis=0),
                    bounds_check=N - 1, oob_is_err=False).then_inc(scattered[j % 4], 16)
                if j % 2 == 1 and j // 2 + 3 < NE:
                    split_expert(j // 2 + 3)

        @block.tensor
        def _(pe):
            def opens(name):
                for what, value in plan[name][2]:
                    pe.wait_ge(done[what], value)
                return PS[plan[name][0]]

            def closes(name, ins):
                ins.then_inc(full[plan[name][0]], 1)

            def product(name, ps, stationary, moving, chunks):
                pairs = [(a, b, c) for c in range(chunks) for a, b in ((0, 0), (0, 1), (1, 0))]
                for n, (a, b, c) in enumerate(pairs):
                    mm = pe.matmul(ps, stationary[a](c), moving[b](c), start=(n == 0), stop=(n == len(pairs) - 1))
                closes(name, mm)

            def block_of(t, f, w=128, off=0):
                return lambda c: t[:, c, f * w + off:(f + 1) * w + off]

            def rows_of(t):
                return lambda c: t[:, c, :]

            pe.wait_ge(done["consts"], 1)
            pe.wait_ge(done["grp_ready"], 1)
            ps = opens("bounds")
            pe.matmul(ps[0:NB, 0:NG], ones[0:NG, 0:NB], dg2[0:NG, 0, :], start=True, stop=True)
            closes("bounds", pe.matmul(ps[0:NB, NG:2 * NG], ones[0:NG, 0:NB], dg2[0:NG, 1, :], start=True, stop=True))
            pe.wait_ge(done["blen_ready"], 1)
            ps = opens("bases")
            pe.matmul(ps[0:1, 0:NB + 1], blh[0:NB, 0:1], tri[0:NB, 0:NB + 1], start=True, stop=True)
            closes("bases", pe.matmul(ps[0:1, 32:32 + NB], blh[0:NB, 1:2], ident[0:NB, 0:NB], start=True, stop=True))

            pe.wait_ge(done["w_lo"], order["w2"])
            for c in range(C):
                product(f"mp{c}", opens(f"mp{c}")[:], (block_of(W1H, c), block_of(W1L, c)), (rows_of(W2H), rows_of(W2L)), C)
            for i in range(NT):
                pe.wait_ge(done["xf_ready"], i + 1)
                opens(f"xt{i}")
                ps = view(f"xt{i}")
                for c in range(C):
                    mm = pe.transpose(ps[:, c, 0:TT], XF[0:TT, i, 128 * c:128 * (c + 1)], ident[0:TT, 0:TT])
                closes(f"xt{i}", mm)

            def tile_product(name, i, wh, wl):
                product(name, opens(name)[0:TT, :], (block_of(XTH, i, TT), block_of(XTL, i, TT)), (rows_of(wh), rows_of(wl)), C)

            pe.wait_ge(done["w_lo"], order["wk"])
            for i in range(NT):
                pe.wait_ge(done["xtl_ready"], i + 1)
                tile_product(f"k{i}", i, WKH, WKL)
            pe.wait_ge(done["w_lo"], order["wq"])
            for i in range(NT):
                if i == 4:
                    pe.wait_ge(done["kmax_step"], NT)
                    opens("kmt")
                    for c in range(C):
                        mm = pe.transpose(view("kmt")[:, c, 0:TT], KMAX[0:TT, 128 * c:128 * (c + 1)], ident[0:TT, 0:TT])
                    closes("kmt", mm)
                if i == 7:
                    pe.wait_ge(done["diag_ready"], 1)
                    closes("kmb", pe.matmul(opens("kmb")[0:TT, :], ones[:, 0:TT], diag[:].rearrange("p c f -> p (c f)"),
                                            start=True, stop=True))
                tile_product(f"q{i}", i, WQH, WQL)
            pe.wait_ge(done["mpl_ready"], C)
            for i in range(NT):
                tile_product(f"xm{i}", i, MPH, MPL)
            pe.wait_ge(done["w_lo"], order["wv"])
            for c in range(C):
                product(f"vp{c}", opens(f"vp{c}")[:], (block_of(WVH, c), block_of(WVL, c)), (rows_of(MPH), rows_of(MPL)), C)
            for i in range(NT):
                pe.wait_ge(done["el_ready"], i + 1)
                for c in range(C):
                    ps = opens(f"tt{c}") if i == 0 else PS[plan[f"tt{c}"][0]]
                    f = slice(128 * c, 128 * (c + 1))
                    pe.matmul(ps[:], XNH[0:TT, i, f], EH[0:TT, i % 3, :], start=(i == 0), stop=False)
                    pe.matmul(ps[:], XNH[0:TT, i, f], EL[0:TT, i % 3, :], start=False, stop=False)
                    mm = pe.matmul(ps[:], XNL[0:TT, i, f], EH[0:TT, i % 3, :], start=False, stop=(i == NT - 1))
                    if i == NT - 1:
                        closes(f"tt{c}", mm)
                    elif c == C - 1:
                        mm.then_inc(done["e_used"], 1)
            pe.wait_ge(done["esum_ready"], 1)
            ps = opens("ks")
            for c in range(C):
                mm = pe.matmul(ps[:, c:c + 1], ESUM[0:TT, 128 * c:128 * (c + 1)], ones[0:TT, 0:1], start=True, stop=True)
            closes("ks", mm)
            pe.wait_ge(done["tl_ready"], C)
            pe.wait_ge(done["vpl_ready"], C)
            for c in range(C):
                product(f"cp{c}", opens(f"cp{c}")[:], (block_of(TH, c), block_of(TL, c)), (rows_of(VPH), rows_of(VPL)), C)

            for b in range(4, 8):
                opens(f"adj{b}")
            pe.wait_ge(done["tab_ready"], 1)
            pe.wait_ge(done["zero_ready"], 1)
            pe.wait_ge(done["cpl_ready"], C)
            for s in range(2):
                pe.sem_inc(hot_used[s], 1)
            for b in range(NB):
                if b >= 2:
                    pe.wait_ge(done["adj_hi"], b - 1)
                    pe.wait_ge(done["adj_lo"], b - 1)
                half = [PS[4 + 2 * (b % 2) + h] for h in range(2)]
                for h in range(2):
                    pe.matmul(half[h][0:TT, 0:5 * DB], zero16[0:1, 0:TT], zero16[0:1, 0:5 * DB], start=True, stop=False,
                              skip_group_check=True)
                first = pe.value_load(tab[0:1, 0, b:b + 1], min_val=0, max_val=NB * NG)
                end = pe.value_load(tab[0:1, 0, b + 1:b + 2], min_val=1, max_val=NB * NG)
                with pe.Fori(first, end) as n:
                    for s in range(2):
                        pe.wait_ge(hot[s], n + 1)
                        for k in range(NT):
                            mm = pe.matmul(half[k // 5][0:TT, (k % 5) * DB:(k % 5 + 1) * DB], HOT_S[0:ET, s, TT * k:TT * (k + 1)],
                                           HOT_D[0:ET, s, :], start=False, stop=False, skip_group_check=True)
                        mm.then_inc(hot_used[s], 1)
                for h in range(2):
                    mm = pe.matmul(half[h][0:TT, 0:5 * DB], zero16[0:1, 0:TT], zero16[0:1, 0:5 * DB], start=False,
                                   stop=True, skip_group_check=True)
                mm.then_inc(done["adj_full"], 1)
                i = b // 2
                if b % 2 == 0:
                    pe.wait_ge(done["q_ready"], i + 1)
                    opens(f"qt{i}")
                    for c in range(C):
                        mm = pe.transpose(view(f"qt{i}")[:, c, 0:TT], Q[0:TT, i, 128 * c:128 * (c + 1)], ident[0:TT, 0:TT])
                    closes(f"qt{i}", mm)
                else:
                    pe.wait_ge(done["qtl_ready"], i + 1)
                    product(f"qp{i}", opens(f"qp{i}")[0:TT, :],
                            (lambda c: QTH[:, i % 2, c, 0:TT], lambda c: QTL[:, i % 2, c, 0:TT]), (rows_of(CPH), rows_of(CPL)), C)

            pe.wait_ge(done["flag_in"], 1)
            closes("flag", pe.matmul(opens("flag")[0:1, 0:1], many[0:TT, 1:2], ones[0:TT, 0:1], start=True, stop=True))
            pe.wait_ge(done["flag_ready"], 1)
            large = pe.value_load(flag[0:1, 0:1], min_val=0, max_val=1)

            def aggregate(layer, hi, lo):
                for ch, (c0, w) in enumerate(CHUNKS):
                    names = [f"z{layer}_{ch}_{f}" for f in range(C)] + ([f"deg{ch}"] if layer == 1 else [])

                    def operands(k, f):
                        if f == C:
                            return [onesr[0:TT, :]]
                        return [t[0:TT, k, 128 * f:128 * (f + 1)] for t in (hi, lo)]

                    def place(f):
                        return PS[plan[names[f]][0]][0:(2 if f == C else 128), 0:w]

                    for f, name in enumerate(names):
                        opens(name)
                        for n, a in enumerate(operands(0, f)):
                            pe.matmul(place(f), a, AT[0:TT, 0, c0:c0 + w], start=(n == 0), stop=False)
                    with pe.If(large > 0):
                        for k in range(NT):
                            pe.wait_ge(done["ac_ready"], ((layer - 1) * 3 + ch) * NT + k + 1)
                            for f in range(len(names)):
                                for a in operands(k, f):
                                    mm = pe.matmul(place(f), a, AC[0:TT, k % 2, 0:w], start=False, stop=False)
                            mm.then_inc(done["ac_used"], 1)
                    with pe.Else():
                        pe.nop()
                    for f, name in enumerate(names):
                        for k in range(1, NT):
                            for n, a in enumerate(operands(k, f)):
                                last = k == NT - 1 and n == len(operands(k, f)) - 1
                                mm = pe.matmul(place(f), a, AT[0:TT, k, c0:c0 + w], start=False, stop=last)
                        closes(name, mm)

            def dense(name, i, wh, wl):
                product(name, opens(name)[0:TT, :], (block_of(ZH, i, TT), block_of(ZL, i, TT)), (rows_of(wh), rows_of(wl)), C)

            aggregate(1, XNH, XNL)
            pe.wait_ge(done["degrow_ready"], 3)
            ps = opens("degt")
            for i in range(NT):
                mm = pe.matmul(ps[0:TT, i:i + 1], drow[0:1, TT * i:TT * (i + 1)], ones[0:1, 0:1], start=True, stop=True)
            closes("degt", mm)
            pe.wait_ge(done["w_lo"], order["g1"])
            pe.wait_ge(done["zl_ready"], 3 * C)
            for i in range(NT):
                dense(f"h{i}", i, G1H, G1L)
            pe.wait_ge(done["h1l_ready"], NT)
            aggregate(2, H1H, H1L)
            pe.wait_ge(done["w_lo"], order["g2"])
            pe.wait_ge(done["zl_ready"], 6 * C)
            for i in range(NT):
                dense(f"o{i}", i, G2H, G2L)

            pe.wait_ge(loads["gate"], 16)
            opens("logits")
            for i in range(NT + 1):
                if i < NT:
                    pe.wait_ge(done["y_ready"], i + 1)
                    opens(f"yt{i}")
                    for c in range(C):
                        mm = pe.transpose(view(f"yt{i}")[:, c, 0:TT], Y[0:TT, i, 128 * c:128 * (c + 1)], ident[0:TT, 0:TT])
                    closes(f"yt{i}", mm)
                if i:
                    pe.wait_ge(done["yt_ready"], i)
                    for c in range(C):
                        mm = pe.matmul(PS[plan["logits"][0]][0:TT, NE * (i - 1):NE * i], YT[:, (i - 1) % 2, c, 0:TT], gw[:, c, :],
                                       start=(c == 0), stop=(c == C - 1))
                    if i == NT:
                        closes("logits", mm)
                    else:
                        mm.then_inc(done["yt_used"], 1)
            for r in range(SINKHORN):
                pe.wait_ge(done["p_ready"], r + 1)
                closes(f"sink{r}", pe.matmul(opens(f"sink{r}")[0:TT, 0:NT * NE], ones[0:TT, 0:TT],
                                             P8[0:TT].rearrange("p i e -> p (i e)"), start=True, stop=True))
            pe.wait_ge(done["grep_ready"], 1)
            for h in range(3):
                opens(f"gt{h}")
                for i in range(4 * h, min(4 * h + 4, NT)):
                    mm = pe.transpose(view(f"gt{h}")[:, i % 4, 0:TT], GREP[0:TT, i, :], ident[0:TT, 0:TT])
                closes(f"gt{h}", mm)
            pe.wait_ge(done["rconsts"], 1)
            for r in range(len(SHIFTS)):
                pe.wait_ge(done["ind_ready"], r + 1)
                closes(f"rad{r}", pe.matmul(opens(f"rad{r}")[:, 0:1], blkones[:], cnt[:, 1:2], start=True, stop=True))
            pe.wait_ge(done["msel_ready"], 1)
            ps = opens("sel")
            for i in range(NT):
                mm = pe.matmul(ps[0:TT, NE * i:NE * (i + 1)], M_SEL[:, TT * i:TT * (i + 1)], pick[:], start=True, stop=True)
            closes("sel", mm)
            pe.wait_ge(done["rowtot_ready"], 1)
            closes("off", pe.matmul(opens("off")[0:TT, 0:NE], tri[0:TT, 0:TT], s8[0:TT, 1, :], start=True, stop=True))
            ps = opens("slots")
            pe.wait_ge(done["route_ready"], NT)
            for j in range(NS):
                for i in range(NT):
                    mm = pe.matmul(ps[0:SLOT, 6 * j:6 * (j + 1)], ROUTE[0:TT, i, SLOT * j:SLOT * (j + 1)], vals[0:TT, i, :],
                                   start=(i == 0), stop=(i == NT - 1))
            closes("slots", mm)

            for j in range(NS + 1):
                if j < NS:
                    pe.wait_ge(gathered_y[j], 16)
                    opens(f"ft{j}")
                    for c in range(C):
                        mm = pe.transpose(view(f"ft{j}")[:, c, 0:SLOT], YG[0:SLOT, j, 128 * c:128 * (c + 1)], ident[0:SLOT, 0:SLOT])
                    closes(f"ft{j}", mm)
                if j:
                    t = j - 1
                    e = t // 2
                    pe.wait_ge(done["w_lo"], NW + e + 1)
                    pe.wait_ge(done["ftl_ready"], t + 1)
                    product(f"fo{t}", opens(f"fo{t}")[0:SLOT, :],
                            (lambda c: FTH[:, t % 2, c, 0:SLOT], lambda c: FTL[:, t % 2, c, 0:SLOT]),
                            (rows_of(WEH[e % 3]), rows_of(WEL[e % 3])), C)

        @block.scalar
        def _(act):
            def copy(o, i, **kw):
                return nc.scalar.activation(o, i, ACT.Copy, **kw)

            def split_hi(n, raw, hi, load, value=16):
                act.wait_ge(loads[load], value)
                copy(hi[:], raw[:]).then_inc(done["w_hi"], 1)

            for n in range(2):
                split_hi(n, splits[n][0], splits[n][1], splits[n][3])
            act.wait_ge(done["var_ready"], 1)
            nc.scalar.activation(rstd[0:TT, 1, :], rstd[0:TT, 0, :], ACT.Sqrt).then_inc(done["sqrt_ready"], 1)
            split_hi(2, splits[2][0], splits[2][1], splits[2][3])
            for i in range(NT):
                act.wait_ge(done["xf_ready"], i + 1)
                copy(XNH[0:TT, i, :], XF[0:TT, i, :]).then_inc(done["xnh_ready"], 1)
                if i == 1:
                    for c in range(C):
                        act.wait_ge(done["mt_ready"], c + 1)
                        copy(MPH[:, c, :], MT[:, c, :]).then_inc(done["mph_ready"], 1)
                    split_hi(3, splits[3][0], splits[3][1], splits[3][3])
            for i in range(NT):
                reads(act, f"xt{i}")
                copy(XTH[:, :, TT * i:TT * (i + 1)], view(f"xt{i}")[:, :, 0:TT]).then_inc(done["xth_ready"], 1)
            for i in range(NT):
                reads(act, f"k{i}")
                if i == 0:
                    act.wait_ge(done["xnl_ready"], NT)
                ps = PS[plan[f"k{i}"][0]]
                copy(K[0:TT, i, :], ps[0:TT, :]).then_inc(done["k_stored"], 1)
            act.wait_ge(loads["wv"], 16)
            reads(act, f"k{NT - 1}")
            split_hi(4, splits[4][0], splits[4][1], splits[4][3])
            for i in range(NT):
                ps = PS[plan[f"q{i}"][0]]
                act.wait_ge(done["rmax_ready"], i + 1)
                if i == 0:
                    act.wait_ge(done["w_lo"], order["wq"])
                nc.scalar.activation(Q[0:TT, i, :], ps[0:TT, :], ACT.Exp, bias=rmax[0:TT, i:i + 1],
                                     accum_out=rsum[0:TT, 0, i:i + 1]).then_inc(done["q_exp"], 1)
            for i in range(NT):
                act.wait_ge(done["k_shift"], i + 1)
                nc.scalar.activation(K[0:TT, i, :], K[0:TT, i, :], ACT.Exp).then_inc(done["k_exp"], 1)
                if i == 0:
                    reads(act, f"xm{NT - 1}")
                if i >= 3:
                    act.wait_ge(done["e_used"], i - 2)
                act.wait_ge(done["k_exp"], i + 1)
                copy(EH[0:TT, i % 3, :], K[0:TT, i, :]).then_inc(done["eh_ready"], 1)
                if 1 <= i <= C:
                    c = i - 1
                    reads(act, f"vp{c}")
                    copy(VPH[:, c, :], PS[plan[f"vp{c}"][0]][:]).then_inc(done["vph_ready"], 1)
            for c in range(C):
                reads(act, f"tt{c}")
                copy(TH[:, c, :], PS[plan[f"tt{c}"][0]][:]).then_inc(done["th_ready"], 1)
            act.wait_ge(done["krs_ready"], 1)
            for c in range(C):
                reads(act, f"cp{c}")
                copy(CPH[:, c, :], PS[plan[f"cp{c}"][0]][:], scale=krs[:, 1, c:c + 1]).then_inc(done["cph_ready"], 1)
            for b in range(NB):
                act.wait_ge(done["adj_full"], b + 1)
                if b == 0:
                    act.wait_ge(done["cph_ready"], C)
                for h in range(2):
                    src = PS[4 + 2 * (b % 2) + h][0:TT, 0:5 * DB].rearrange("p (k d) -> p k d", k=5)
                    ins = nc.scalar.activation(AT[0:TT, 5 * h:5 * h + 5, DB * b:DB * (b + 1)], src, ACT.Copy,
                                               accum_out=odeg[0:TT, h, b:b + 1])
                ins.then_inc(done["adj_hi"], 1)
                i = b // 2
                if b % 2 == 0:
                    reads(act, f"qt{i}")
                    if i >= 2:
                        reads(act, f"qp{i - 2}")
                    copy(QTH[:, i % 2, :, 0:TT], view(f"qt{i}")[:, :, 0:TT]).then_inc(done["qth_ready"], 1)
            reads(act, f"qp{NT - 1}")
            split_hi(5, splits[5][0], splits[5][1], "g1")

            def z_hi(layer):
                for ch, (c0, w) in enumerate(CHUNKS):
                    for f in range(C):
                        name = f"z{layer}_{ch}_{f}"
                        reads(act, name)
                        if layer == 2 and ch == f == 0:
                            reads(act, f"h{NT - 1}")
                        copy(ZH[:, f, c0:c0 + w], PS[plan[name][0]][:, 0:w]).then_inc(done["zh_ready"], 1)

            z_hi(1)
            for i in range(NT):
                act.wait_ge(done["t_ready"], i + 1)
                nc.scalar.activation(H1H[0:TT, i, :], PS[plan[f"h{i}"][0]][0:TT, :], ACT.Relu).then_inc(done["h1h_ready"], 1)
            act.wait_ge(done["w_lo"], order["g1"])
            split_hi(6, splits[6][0], splits[6][1], "g2")
            z_hi(2)

            def split_expert(e):
                if e >= 3:
                    reads(act, f"fo{2 * (e - 3) + 1}")
                split_hi(NW + e, RAW_E, WEH[e % 3], "exp", 16 * (e + 1))

            split_expert(0)
            act.wait_ge(done["var2_ready"], 1)
            nc.scalar.activation(rstd[0:TT, 1, :], rstd[0:TT, 0, :], ACT.Sqrt).then_inc(done["sqrt2_ready"], 1)
            for i in range(NT):
                reads(act, f"yt{i}")
                if i >= 2:
                    act.wait_ge(done["yt_used"], i - 1)
                ins = copy(YT[:, i % 2, :, 0:TT], view(f"yt{i}")[:, :, 0:TT])
                ins.then_inc(done["yt_ready"], 1)
            split_expert(1)
            for h in range(3):
                reads(act, f"gt{h}")
                n = min(4, NT - 4 * h)
                copy(GT[:, TT * 4 * h:TT * (4 * h + n)].rearrange("p (i t) -> p i t", i=n),
                     view(f"gt{h}")[:, 0:n, 0:TT]).then_inc(done["gt_ready"], 1)
            split_expert(2)
            for j in range(NS):
                reads(act, f"ft{j}")
                if j >= 2:
                    reads(act, f"fo{j - 2}")
                copy(FTH[:, j % 2, :, 0:SLOT], view(f"ft{j}")[:, :, 0:SLOT]).then_inc(done["fth_ready"], 1)
                if j % 2 == 1 and j // 2 + 2 < NE and j >= 3:
                    split_expert(j // 2 + 2)

        @block.vector
        def _(dve):
            V = nc.vector
            count = [0]

            def link(ins):
                count[0] += 1
                ins.then_inc(done["dve_chain"], 1)
                dve.wait_ge(done["dve_chain"], count[0])

            def after(name, value):
                dve.wait_ge(done[name], value)

            def ps_of(name):
                return PS[plan[name][0]]

            dve.wait_ge(loads["edges"], 48)
            V.tensor_reduce(grp[0:NG, 0:1], DROW[0:NG, :], AX, ALU.min)
            link(V.tensor_reduce(grp[0:NG, 1:2], DROW[0:NG, :], AX, ALU.max))
            after("consts", 1)
            V.tensor_copy(onesr[:], ones[:, 0:2])
            V.tensor_scalar(dg2[0:NG, 0, :], ident[0:NG, 0:NG], grp[0:NG, 0:1], None, ALU.mult)
            V.tensor_scalar(dg2[0:NG, 1, :], ident[0:NG, 0:NG], grp[0:NG, 1:2], None, ALU.mult).then_inc(done["grp_ready"], 1)
            V.tensor_copy(srcf[0:ET, :], EDGE[0:ET, 0, :])
            V.tensor_copy(dstf[0:ET, :], EDGE[0:ET, 1, :])
            reads(dve, "bounds")
            ps = ps_of("bounds")
            b_ = slice(0, NB)
            link(V.tensor_scalar(bw[b_, 0, :], ps[b_, 0:NG], blk[b_, 1:2], None, ALU.is_le))
            link(V.scalar_tensor_tensor(bw[b_, 1, :], ps[b_, NG:2 * NG], blk[b_, 0:1], bw[b_, 0, :], ALU.is_ge, ALU.mult))
            V.tensor_tensor(bw[b_, 2, :], bw[b_, 1, :], gio[b_, 0, :], ALU.mult)
            link(V.tensor_tensor(bw[b_, 3, :], bw[b_, 1, :], gio[b_, 1, :], ALU.mult))
            V.tensor_reduce(blh[b_, 2:3], bw[b_, 2, :], AX, ALU.max)
            link(V.tensor_reduce(blh[b_, 3:4], bw[b_, 3, :], AX, ALU.max))
            link(V.tensor_scalar(blh[b_, 4:5], blh[b_, 3:4], -1.0, float(NG), ALU.mult, ALU.add))
            link(V.tensor_scalar(blh[b_, 1:2], blh[b_, 4:5], float(NG - 1), None, ALU.min))
            link(V.scalar_tensor_tensor(blh[b_, 5:6], blh[b_, 1:2], 1.0, blh[b_, 2:3], ALU.add, ALU.max))
            V.tensor_tensor(blh[b_, 0:1], blh[b_, 5:6], blh[b_, 1:2], ALU.subtract).then_inc(done["blen_ready"], 1)
            reads(dve, "bases")
            ps = ps_of("bases")
            link(V.tensor_copy(tab[0:1, 0, 0:NB + 1], ps[0:1, 0:NB + 1]))
            V.tensor_tensor(tab[0:1, 1, 0:NB], ps[0:1, 32:32 + NB], tab[0:1, 0, 0:NB], ALU.subtract).then_inc(done["tab_ready"], 1)
            after("tab_ready", 1)

            def inverse_deviation(sqrt_done, root_ready):
                t = slice(0, TT)
                V.tensor_scalar(rstd[t, 0, :], mv[t, :, 1], LN_EPS, None, ALU.add).then_inc(done[root_ready], 1)
                after(sqrt_done, 1)
                link(V.reciprocal(rstd[t, 2, :], rstd[t, 1, :]))
                link(V.tensor_tensor(rstd[t, 3, :], rstd[t, 2, :], rstd[t, 2, :], ALU.mult))
                link(V.tensor_tensor(rstd[t, 3, :], rstd[t, 3, :], rstd[t, 0, :], ALU.mult))
                link(V.tensor_scalar(rstd[t, 3, :], rstd[t, 3, :], -0.5, 1.5, ALU.mult, ALU.add))
                link(V.tensor_tensor(rstd[t, 2, :], rstd[t, 2, :], rstd[t, 3, :], ALU.mult))

            for i in range(NT):
                if i % 2 == 0:
                    dve.wait_ge(ld_x[i // 2], 16)
                ins = V.bn_stats(stat[0:TT, i, :], X[0:TT, i, :])
            link(ins)
            for i in range(NT):
                ins = V.bn_aggr(mv[0:TT, i, :], stat[0:TT, i, :])
            link(ins)
            inverse_deviation("sqrt_ready", "var_ready")
            for i in range(NT):
                V.tensor_scalar(XF[0:TT, i, :], X[0:TT, i, :], mv[0:TT, i, 0:1], rstd[0:TT, 2, i:i + 1],
                                ALU.subtract, ALU.mult).then_inc(done["xf_ready"], 1)
            for c in range(C):
                reads(dve, f"mp{c}")
                link(V.tensor_copy(MT[:, c, :], ps_of(f"mp{c}")[:]))
                V.tensor_tensor(MT[:, c, 128 * c:128 * (c + 1)], ps_of(f"mp{c}")[:, 128 * c:128 * (c + 1)], ident[:],
                                ALU.add).then_inc(done["mt_ready"], 1)
            for c in range(C):
                after("mph_ready", c + 1)
                V.tensor_tensor(MPL[:, c, :], MT[:, c, :], MPH[:, c, :].bitcast(F32), ALU.subtract).then_inc(done["mpl_ready"], 1)
            after("mpl_ready", C)
            for i in range(NT):
                after("xth_ready", i + 1)
                V.tensor_tensor(XTL[:, :, TT * i:TT * (i + 1)], view(f"xt{i}")[:, :, 0:TT],
                                XTH[:, :, TT * i:TT * (i + 1)].bitcast(F32), ALU.subtract).then_inc(done["xtl_ready"], 1)

            for i in range(NT):
                after("k_stored", i + 1)
                ps = ps_of(f"k{i}")[0:TT, :]
                if i == 0:
                    after("w_lo", order["wk"])
                    V.tensor_copy(KMAX[0:TT, :], ps).then_inc(done["kmax_step"], 1)
                else:
                    after("kmax_step", i)
                    V.tensor_tensor(KMAX[0:TT, :], ps, KMAX[0:TT, :], ALU.max).then_inc(done["kmax_step"], 1)

            def q_scale(i):
                after("q_exp", i + 1)
                link(V.reciprocal(rsum[0:TT, 1, i:i + 1], rsum[0:TT, 0, i:i + 1]))
                V.tensor_scalar(Q[0:TT, i, :], Q[0:TT, i, :], rsum[0:TT, 1, i:i + 1], None, ALU.mult).then_inc(done["q_ready"], 1)

            def shift(i):
                if i == 0:
                    reads(dve, "kmb")
                after("k_stored", i + 1)
                V.tensor_tensor(K[0:TT, i, :], K[0:TT, i, :], ps_of("kmb")[0:TT, :], ALU.subtract).then_inc(done["k_shift"], 1)

            for i in range(NT):
                reads(dve, f"q{i}")
                V.tensor_reduce(rmax[0:TT, i:i + 1], ps_of(f"q{i}")[0:TT, :], AX, ALU.max, negate=True).then_inc(done["rmax_ready"], 1)
                if i == 3:
                    reads(dve, "kmt")
                    link(V.tensor_reduce(kmt[:], view("kmt")[:, :, 0:TT], AX, ALU.max))
                    for c in range(C):
                        ins = V.tensor_scalar(diag[:, c, :], ident[:], kmt[:, c:c + 1], None, ALU.mult)
                    ins.then_inc(done["diag_ready"], 1)
                if i >= 1:
                    q_scale(i - 1)
                if i >= 8:
                    shift(i - 8)
            q_scale(NT - 1)
            for i in range(NT):
                if i + 2 < NT:
                    shift(i + 2)
                reads(dve, f"xm{i}")
                after("xf_ready", i + 1)
                V.tensor_tensor(X[0:TT, i, :], ps_of(f"xm{i}")[0:TT, :], X[0:TT, i, :], ALU.add).then_inc(done["xm_added"], 1)
            for i in range(NT):
                after("eh_ready", i + 1)
                V.tensor_tensor(EL[0:TT, i % 3, :], K[0:TT, i, :], EH[0:TT, i % 3, :].bitcast(F32), ALU.subtract).then_inc(done["el_ready"], 1)
                if 1 <= i <= C:
                    c = i - 1
                    after("vph_ready", c + 1)
                    V.tensor_tensor(VPL[:, c, :], ps_of(f"vp{c}")[:], VPH[:, c, :].bitcast(F32), ALU.subtract).then_inc(done["vpl_ready"], 1)
            for c in range(C):
                after("th_ready", c + 1)
                V.tensor_tensor(TL[:, c, :], ps_of(f"tt{c}")[:], TH[:, c, :].bitcast(F32), ALU.subtract).then_inc(done["tl_ready"], 1)
            reads(dve, "ks")
            link(V.reciprocal(krs[:, 0, :], ps_of("ks")[:, 0:C]))
            V.tensor_scalar(krs[:, 1, :], krs[:, 0, :], float(D) ** -0.5, None, ALU.mult).then_inc(done["krs_ready"], 1)
            for c in range(C):
                after("cph_ready", c + 1)
                V.scalar_tensor_tensor(CPL[:, c, :], ps_of(f"cp{c}")[:], krs[:, 1, c:c + 1], CPH[:, c, :].bitcast(F32),
                                       ALU.mult, ALU.subtract).then_inc(done["cpl_ready"], 1)

            V.memset(zero16[:], 0.0).then_inc(done["zero_ready"], 1)

            def counts_left(b):
                after("adj_hi", b + 1)
                for h in range(2):
                    src = PS[4 + 2 * (b % 2) + h][0:TT, 0:5 * DB].rearrange("p (k d) -> p k d", k=5)
                    ins = V.tensor_tensor(AL[0:TT, 5 * h:5 * h + 5, DB * b:DB * (b + 1)], src,
                                          AT[0:TT, 5 * h:5 * h + 5, DB * b:DB * (b + 1)].bitcast(F32), ALU.subtract)
                ins.then_inc(done["adj_lo"], 1)

            def add_attention(i):
                reads(dve, f"qp{i}")
                V.tensor_tensor(X[0:TT, i, :], ps_of(f"qp{i}")[0:TT, :], X[0:TT, i, :], ALU.add).then_inc(done["qp_added"], 1)

            after("xm_added", NT)
            for b in range(NB):
                first = dve.value_load(tab[0:1, 0, b:b + 1], min_val=0, max_val=NB * NG)
                end = dve.value_load(tab[0:1, 0, b + 1:b + 2], min_val=1, max_val=NB * NG)
                behind = dve.value_load(tab[0:1, 1, b:b + 1], min_val=-NB * NG, max_val=NG)
                with dve.Fori(first, end) as n:
                    for s in range(2):
                        col = nc.s_assert_within(2 * (n + behind) + s, 0, 2 * NG - 1,
                                                 skip_runtime_bounds_check_because="lo <= n + lo - first < hi")
                        dve.wait_ge(hot_used[s], n + 1)
                        V.tensor_scalar(HOT_S[0:ET, s, :], iota[0:ET, 0:N], srcf[0:ET, bass.ds(col, 1)], None, ALU.is_equal)
                        V.tensor_scalar(HOT_D[0:ET, s, :], iota[0:ET, DB * b:DB * (b + 1)], dstf[0:ET, bass.ds(col, 1)], None,
                                        ALU.is_equal).then_inc(hot[s], 1)
                if b >= 1:
                    counts_left(b - 1)
                if b % 2 == 1:
                    i = b // 2
                    after("qth_ready", i + 1)
                    V.tensor_tensor(QTL[:, i % 2, :, 0:TT], view(f"qt{i}")[:, :, 0:TT], QTH[:, i % 2, :, 0:TT].bitcast(F32),
                                    ALU.subtract).then_inc(done["qtl_ready"], 1)
                    if i >= 1:
                        add_attention(i - 1)
            counts_left(NB - 1)
            add_attention(NT - 1)

            link(V.tensor_reduce(many[0:TT, 0:1], odeg[0:TT], mybir.AxisListType.XY, ALU.add))
            V.tensor_scalar(many[0:TT, 1:2], many[0:TT, 0:1], EXACT, None, ALU.is_gt).then_inc(done["flag_in"], 1)
            reads(dve, "flag")
            V.tensor_scalar(flag[0:1, 0:1], ps_of("flag")[0:1, 0:1], 0.5, None, ALU.is_gt).then_inc(done["flag_ready"], 1)
            after("flag_ready", 1)
            large = dve.value_load(flag[0:1, 0:1], min_val=0, max_val=1)

            def aggregate(layer):
                for ch, (c0, w) in enumerate(CHUNKS):
                    with dve.If(large > 0):
                        for k in range(NT):
                            n = ((layer - 1) * 3 + ch) * NT + k
                            if n >= 2:
                                after("ac_used", n - 1)
                            V.tensor_copy(AC[0:TT, k % 2, 0:w], AL[0:TT, k, c0:c0 + w]).then_inc(done["ac_ready"], 1)
                    with dve.Else():
                        dve.nop()
                    for f in range(C):
                        n = ((layer - 1) * 3 + ch) * C + f + 1
                        after("zh_ready", n)
                        V.tensor_tensor(ZL[:, f, c0:c0 + w], ps_of(f"z{layer}_{ch}_{f}")[:, 0:w], ZH[:, f, c0:c0 + w].bitcast(F32),
                                        ALU.subtract).then_inc(done["zl_ready"], 1)
                    if layer == 1:
                        reads(dve, f"deg{ch}")
                        V.tensor_copy(drow[0:1, c0:c0 + w], ps_of(f"deg{ch}")[0:1, 0:w]).then_inc(done["degrow_ready"], 1)

            aggregate(1)
            reads(dve, "degt")
            V.tensor_copy(degs[0:TT, :], ps_of("degt")[0:TT, 0:NT]).then_inc(done["deg_ready"], 1)
            after("deg_ready", 1)
            dve.wait_ge(loads["b1"], 16)
            for i in range(NT + 1):
                if i < NT:
                    reads(dve, f"h{i}")
                    ps = ps_of(f"h{i}")[0:TT, :]
                    V.scalar_tensor_tensor(ps, bias[0:TT, :], degs[0:TT, i:i + 1], ps, ALU.mult, ALU.add).then_inc(done["t_ready"], 1)
                if i:
                    after("h1h_ready", i)
                    V.scalar_tensor_tensor(H1L[0:TT, i - 1, :], ps_of(f"h{i - 1}")[0:TT, :], 0.0, H1H[0:TT, i - 1, :].bitcast(F32),
                                           ALU.max, ALU.subtract).then_inc(done["h1l_ready"], 1)
            aggregate(2)
            dve.wait_ge(loads["b2"], 16)
            for i in range(NT):
                reads(dve, f"o{i}")
                ps = ps_of(f"o{i}")[0:TT, :]
                link(V.scalar_tensor_tensor(ps, bias[0:TT, :], degs[0:TT, i:i + 1], ps, ALU.mult, ALU.add))
                V.scalar_tensor_tensor(X[0:TT, i, :], ps, 0.0, X[0:TT, i, :], ALU.max, ALU.add).then_inc(done["x_final"], 1)
                after("x_final", i + 1)
                ins = V.bn_stats(stat[0:TT, i, :], X[0:TT, i, :])
            link(ins)
            for i in range(NT):
                ins = V.bn_aggr(mv[0:TT, i, :], stat[0:TT, i, :])
            link(ins)
            inverse_deviation("sqrt2_ready", "var2_ready")
            for i in range(NT):
                V.tensor_scalar(Y[0:TT, i, :], X[0:TT, i, :], mv[0:TT, i, 0:1], rstd[0:TT, 2, i:i + 1],
                                ALU.subtract, ALU.mult).then_inc(done["y_ready"], 1)

            t = slice(0, TT)
            after("rconsts", 1)
            for r, s in enumerate(SHIFTS):
                V.tensor_scalar(ctab[:, r:r + 1], cb[:, 0:1], 15 if s else 7, s, ALU.bitwise_and, ALU.logical_shift_left)
            V.memset(pre[:, 0:1], 0)
            reads(dve, "logits")
            V.tensor_scalar(P8[t], ps_of("logits")[t, 0:NT * NE].rearrange("p (i e) -> p i e", e=NE), CLIP_EPS, None,
                            ALU.max).then_inc(done["p_ready"], 1)
            for r in range(SINKHORN):
                reads(dve, f"sink{r}")
                sums = ps_of(f"sink{r}")[t, 0:NT * NE].rearrange("p (i e) -> p e i", e=NE)
                link(V.tensor_reduce(s8[t, 0, :], sums, AX, ALU.add))
                link(V.reciprocal(s8[t, 1, :], s8[t, 0, :]))
                link(V.tensor_tensor(P8[t], P8[t], s8[t, 1:2, :].broadcast_to([TT, NT, NE]), ALU.mult))
                link(V.tensor_reduce(s10[t, 0, :], P8[t], AX, ALU.add))
                link(V.reciprocal(s10[t, 1, :], s10[t, 0, :]))
                V.tensor_tensor(P8[t], P8[t], s10[t, 1, :].unsqueeze(2).broadcast_to([TT, NT, NE]), ALU.mult).then_inc(done["p_ready"], 1)
            after("p_ready", SINKHORN + 1)
            V.tensor_copy(GREP[t].rearrange("p i (e c) -> p (i e) c", c=16),
                          P8[t].rearrange("p i e -> p (i e)").unsqueeze(2).broadcast_to([TT, NT * NE, 16])).then_inc(done["grep_ready"], 1)

            after("gt_ready", 3)
            for r, s in enumerate(SHIFTS):
                link(V.tensor_tensor(pre[:, 1:2], pre[:, 0:1], ctab[:, r:r + 1], ALU.bitwise_or))
                link(V.tensor_scalar(M_GT[:], GT[:], pre[:, 1:2].bitcast(F32), None, ALU.is_ge, ALU.add, accum_out=cnt[:, 0:1]))
                V.tensor_scalar(cnt[:, 1:2], cnt[:, 0:1], float(TOPK), None, ALU.is_ge).then_inc(done["ind_ready"], 1)
                reads(dve, f"rad{r}")
                twice = 1 if s else 2
                link(V.tensor_scalar(pre[:, 2:3], ps_of(f"rad{r}")[:, 0:1], float(2 ** s) / twice, -float(2 ** s), ALU.mult, ALU.add))
                V.tensor_tensor(pre[:, 0:1], pre[:, 0:1], pre[:, 2:3], ALU.bitwise_or).then_inc(done["prefix_ready"], 1)
                after("prefix_ready", r + 1)
            kth = pre[:, 0:1].bitcast(F32)
            V.tensor_scalar(M_GT[:], GT[:], kth, None, ALU.is_gt, ALU.add, accum_out=cnt[:, 2:3])
            link(V.tensor_scalar(M_EQ[:], GT[:], kth, None, ALU.is_equal))
            V.tensor_scalar(cnt[:, 3:4], cnt[:, 2:3], -1.0, float(TOPK), ALU.mult, ALU.add)
            link(V.tensor_tensor_scan(RANK[:], M_EQ[:], M_EQ[:], 0.0, ALU.add, ALU.max))
            link(V.scalar_tensor_tensor(M_TIE[:], RANK[:], cnt[:, 3:4], M_EQ[:], ALU.is_le, ALU.mult))
            V.tensor_tensor(M_SEL[:], M_GT[:], M_TIE[:], ALU.add).then_inc(done["msel_ready"], 1)

            V.tensor_scalar(tid[t, 1, :], tid[t, 0, :], 31, None, ALU.bitwise_and)
            reads(dve, "sel")
            link(V.tensor_tensor(w8[t, 0].rearrange("p e i -> p (e i)"), ps_of("sel")[t, 0:NT * NE],
                                 e1[t].rearrange("p i e -> p (i e)"), ALU.mult))
            taken = w8[t, 0].rearrange("p e i -> p (e i)").rearrange("p (i e) -> p i e", e=NE)
            link(V.tensor_reduce(s10[t, 0, :], taken, AX, ALU.max))
            last = w8[t, 1].rearrange("p e i -> p (e i)").rearrange("p (i e) -> p i e", e=NE)
            link(V.tensor_tensor(last, taken, s10[t, 0, :].unsqueeze(2).broadcast_to([TT, NT, NE]), ALU.is_equal))
            by_token = fin[t].rearrange("p e i -> p i e")
            link(V.scalar_tensor_tensor(by_token, taken, 0.0, last, ALU.is_gt, ALU.mult))
            link(V.tensor_tensor_scan(incl[t].rearrange("p e i -> p (e i)"), reset[t].rearrange("p e i -> p (e i)"),
                                      fin[t].rearrange("p e i -> p (e i)"), 0.0, ALU.mult, ALU.add))
            V.tensor_copy(s8[t, 1, :], incl[t, :, NT - 1]).then_inc(done["rowtot_ready"], 1)
            V.tensor_tensor(w8[t, 0], fin[t], P8[t].rearrange("p i e -> p e i"), ALU.mult)
            V.tensor_copy(vals[t, :, 1], tid[t, 1, :])
            link(V.tensor_tensor(vals[t, :, 0], tid[t, 0, :], tid[t, 1, :], ALU.subtract))
            link(V.tensor_reduce(s10[t, 1, :], w8[t, 0].rearrange("p e i -> p i e"), AX, ALU.add))
            link(V.tensor_copy(vals[t, :, 2], s10[t, 1, :]))
            link(V.tensor_tensor(s10[t, 2, :], s10[t, 1, :], vals[t, :, 2], ALU.subtract))
            link(V.tensor_copy(vals[t, :, 3], s10[t, 2, :]))
            V.tensor_tensor(vals[t, :, 4], s10[t, 2, :], vals[t, :, 3], ALU.subtract)
            V.memset(vals[t, :, 5], 0.0)
            reads(dve, "off")
            link(V.tensor_tensor(w8[t, 0], incl[t], ps_of("off")[t, 0:NE].unsqueeze(2).broadcast_to([TT, NE, NT]), ALU.add))
            link(V.tensor_tensor(w8[t, 1], w8[t, 0], e156[t].unsqueeze(2).broadcast_to([TT, NE, NT]), ALU.add))
            link(V.tensor_tensor(w8[t, 0], w8[t, 1], fin[t], ALU.mult))
            link(V.tensor_reduce(s10[t, 3, :], w8[t, 0].rearrange("p e i -> p i e"), AX, ALU.add))
            link(V.tensor_scalar(slot[t, :], s10[t, 3, :], -1.0, None, ALU.add))
            for i in range(NT):
                V.tensor_scalar(ROUTE[t, i, :], iota[t, 0:NS * SLOT], slot[t, i:i + 1], None, ALU.is_equal).then_inc(done["route_ready"], 1)
            reads(dve, "slots")
            u = slice(0, SLOT)
            ps = ps_of("slots")[u, 0:6 * NS].rearrange("p (j c) -> p j c", c=6)
            V.tensor_reduce(tokv[u, 1, :], ps[:, :, 2:5], AX, ALU.add)
            link(V.tensor_reduce(tokv[u, 0, :], ps[:, :, 0:2], AX, ALU.add))
            V.tensor_scalar(idx[u, 0, :], tokv[u, 0, :], -1.0, 0.0, ALU.add, ALU.max)
            link(V.tensor_scalar(tokv[u, 2, :], tokv[u, 0, :], 0.0, 8192.0, ALU.is_equal, ALU.mult))
            V.scalar_tensor_tensor(idx[u, 1, :], tokv[u, 0, :], -1.0, tokv[u, 2, :], ALU.add, ALU.add).then_inc(done["idx_ready"], 1)

            after("idx_ready", 1)
            for j in range(NS + 1):
                if j < NS:
                    after("fth_ready", j + 1)
                    V.tensor_tensor(FTL[:, j % 2, :, 0:SLOT], view(f"ft{j}")[:, :, 0:SLOT], FTH[:, j % 2, :, 0:SLOT].bitcast(F32),
                                    ALU.subtract).then_inc(done["ftl_ready"], 1)
                if j:
                    n = j - 1
                    reads(dve, f"fo{n}")
                    after("gathered_x", 16 * NS)
                    if n >= 4:
                        dve.wait_ge(scattered[n % 4], 16 * (n // 4))
                    V.scalar_tensor_tensor(FO[u, n % 4, :], ps_of(f"fo{n}")[u, :], tokv[u, 1, n:n + 1], XG[u, n, :],
                                           ALU.mult, ALU.add).then_inc(done["fo_ready"], 1)


_OUT = ((N, D), "float32")


def kernel(**inputs):
    import numpy as _np
    import concourse.bacc as _bacc
    from concourse import mybir as _mybir
    from concourse.bass_utils import run_bass_kernel_spmd as _run

    def tr(name):
        return _np.ascontiguousarray(_np.asarray(inputs[name]).T)

    def edges(name):
        return _np.ascontiguousarray(_np.asarray(inputs[name]).reshape(2 * NG, ET).T)

    host = {
        "x": _np.asarray(inputs["x"]), "src_t": edges("src"), "dst_t": edges("dst"),
        "dst_rows": _np.asarray(inputs["dst"]).reshape(NG, 2 * ET),
        "gW1T": tr("L0_gnn_W1"), "gb1": _np.asarray(inputs["L0_gnn_b1"]),
        "gW2T": tr("L0_gnn_W2"), "gb2": _np.asarray(inputs["L0_gnn_b2"]),
        "WqT": tr("L0_mix_Wq"), "WkT": tr("L0_mix_Wk"), "Wv": _np.asarray(inputs["L0_mix_Wv"]),
        "mW1": _np.asarray(inputs["L0_mix_W1"]), "mW2T": tr("L0_mix_W2"),
        "gate": _np.asarray(inputs["L0_ffn_gate_weight"]), "experts": _np.asarray(inputs["L0_ffn_experts"]),
    }
    nc = _bacc.Bacc("TRN2", target_bir_lowering=False, num_devices=1)
    arrays, args = {}, []
    for name, a in host.items():
        a = _np.ascontiguousarray(a)
        arrays[f"in_{name}"] = a
        args.append(nc.dram_tensor(f"in_{name}", a.shape, _mybir.dt.from_np(a.dtype), kind="ExternalInput").ap())
    out = nc.dram_tensor("out_x", _OUT[0], _mybir.dt.float32, kind="ExternalOutput").ap()
    gps_block(nc, *args, out)
    r = _run(nc, [arrays], core_ids=[0])
    return r.results[0]["out_x"]
```

```python
from contextlib import ExitStack

import numpy as np

import concourse.bass as bass
from concourse import mybir

ALU = mybir.AluOpType
ACT = mybir.ActivationFunctionType
F32 = mybir.dt.float32
F32R = mybir.dt.float32r
BF16 = mybir.dt.bfloat16
F16 = mybir.dt.float16
I32 = mybir.dt.int32
U32 = mybir.dt.uint32
I8 = mybir.dt.int8
AX = mybir.AxisListType.X

N, D, E = 1250, 512, 20000
NE, TOPK = 8, 1250 // 8
TT = 125
NT = N // TT
C = D // 128
ET = 125
NE_T = E // ET
UN = 3
DB = 98
NB = -(-N // DB)
NPAD = NB * DB
SPANS = [(0, 4), (4, 8), (8, NB)]
EXACT = 4096.0
LN_EPS, CLIP_EPS, SINKHORN = 1e-5, 1e-6, 8
SLOT = TOPK // 2
NS = NE * 2
SHIFTS = [27, 23, 19, 15, 11, 7, 3, 0]
KB = 1024
BEHIND = ([[("context", 2 * b), ("context", 2 * b + 1)] for b in range(5)]
          + [[], [("values", 0)]]
          + [[("attend", i) for i in part] for part in ((0, 1), (2, 3), (4, 5), (6, 7), (8,), (9,))])


def psum_plan():
    uses, filled, readers, turn = {}, [0] * 8, [[] for _ in range(8)], {}

    def use(name, banks, *read_by):
        k = turn.get(banks, 0)
        turn[banks] = k + 1
        b = banks[k % len(banks)]
        uses[name] = (b, filled[b] + 1, readers[b])
        filled[b] += 1
        readers[b] = list(read_by)

    low, high, every = (0, 1, 2, 3), (4, 5, 6, 7), tuple(range(8))
    for i in range(NT):
        use(f"xt{i}", high, ("xth_ready", i + 1), ("xtl_ready", i + 1))
    use("bounds", (3,), ("blen_ready", 1))
    for i in range(NT):
        if i == 2:
            use("bases", (2,), ("tab_ready", 1))
        use(f"k{i}", low, ("k_stored", i + 1), ("kmax_step", i + 1))
    for i in range(NT):
        if i == 4:
            use("kmt", (4,), ("diag_ready", 1))
        if i == 7:
            use("kmb", (4,), ("k_shift", NT))
        use(f"q{i}", (5, 6, 7), ("rmax_ready", i + 1), ("q_exp", i + 1))
    for c in range(C):
        use(f"mp{c}", low, ("mph_ready", c + 1), ("mpl_ready", c + 1))
    for i in range(NT):
        use(f"xm{i}", low, ("xm_added", i + 1))
    for c in range(C):
        use(f"vp{c}", (5, 6, 7), ("vph_ready", c + 1), ("vpl_ready", c + 1))
    for c in range(C):
        use(f"tt{c}", low, ("th_ready", c + 1), ("tl_ready", c + 1))
    for b in high:
        uses[f"adj{b}"] = (b, None, readers[b])
        readers[b] = [("adj_hi", NB), ("adj_lo", NB)]
    use("ks", (0,), ("krs_ready", 1))
    for c in range(C):
        use(f"cp{c}", (1, 2, 3), ("cph_ready", c + 1), ("cpl_ready", c + 1))
    for i in range(NT):
        use(f"qt{i}", (0, 1), ("qth_ready", i + 1), ("qtl_ready", i + 1))
        use(f"qp{i}", (2, 3), ("qp_added", i + 1))
    use("flag", (0,), ("flag_ready", 1))
    for layer in (1, 2):
        for ch in range(3):
            for f in range(C):
                n = ((layer - 1) * 3 + ch) * C + f + 1
                use(f"z{layer}_{ch}_{f}", every, ("zh_ready", n), ("zl_ready", n))
            if layer == 1:
                use(f"deg{ch}", every, ("degrow_ready", ch + 1))
        if layer == 1:
            use("degt", (7,), ("deg_ready", 1))
            for i in range(NT):
                use(f"h{i}", low, ("h1h_ready", i + 1), ("h1l_ready", i + 1))
    for i in range(NT):
        use(f"o{i}", low, ("x_final", i + 1))
        use(f"yt{i}", (4, 5, 6), ("yt_ready", i + 1))
    use("logits", (7,), ("p_ready", 1))
    for r in range(SINKHORN):
        use(f"sink{r}", (3, 0), *([("p_ready", r + 2)] if r + 1 < SINKHORN else [("grep_ready", 1)]))
    for h in range(3):
        use(f"gt{h}", (1, 2, 3), ("gt_ready", h + 1))
    for r in range(len(SHIFTS)):
        use(f"rad{r}", (0,), ("prefix_ready", r + 1))
    use("sel", (1,), ("rowtot_ready", 1))
    use("off", (2,), ("route_ready", 1))
    use("slots", (3,), ("idx_ready", 1))
    for j in range(NS):
        use(f"ft{j}", (0, 1), ("fth_ready", j + 1), ("ftl_ready", j + 1))
        use(f"fo{j}", (2, 3), ("fo_ready", j + 1))
    return uses


def gps_block(nc, x_in, src_t, dst_t, dst_in, gW1T, gb1, gW2T, gb2, WqT, WkT, Wv, mW1, mW2T,
              gate_w, experts, out):
    plan = psum_plan()
    scratch = nc.dram_tensor("scratch", [N, 2 * D], F32).ap()

    with ExitStack() as ctx:
        base = nc.sbuf_base + (-nc.sbuf_base) % 32

        def at(name, shape, dt, off):
            return nc.alloc_sbuf_tensor_at(name, shape, dt, offset=base + int(off))

        areas = {"a": [int(162.5 * KB), 168 * KB], "b": [204 * KB, int(207.8 * KB)],
                 "c": [148 * KB, 160 * KB]}

        def small(name, shape, dt, area):
            size = int(np.prod(shape[1:])) * mybir.dt.size(dt)
            off = areas[area][0]
            areas[area][0] += size + (-size) % 32
            assert areas[area][0] <= areas[area][1], (name, areas[area])
            return at(name, shape, dt, off)

        def sem(name):
            return ctx.enter_context(nc.semaphore(name))

        X = at("X", [128, NT, D], F32, 0)
        XNH = at("XNH", [128, NT, D], F32R, 20 * KB)
        XNL = at("XNL", [128, NT, D], F32R, 40 * KB)
        H1H = at("H1H", [128, NT, D], F32R, 20 * KB)
        H1L = at("H1L", [128, NT, D], F32R, 40 * KB)
        XTH = at("XTH", [128, C, N], F32R, 60 * KB)
        XTL = at("XTL", [128, C, N], F32R, 80 * KB)
        EH = at("EH", [128, 4, D], F32R, 60 * KB)
        EL = at("EL", [128, 4, D], F32R, 68 * KB)
        TH = at("TH", [128, C, D], F32R, 60 * KB)
        TL = at("TL", [128, C, D], F32R, 68 * KB)
        QTH = at("QTH", [128, 2, C, TT + 3], F32R, 60 * KB)
        QTL = at("QTL", [128, 2, C, TT + 3], F32R, 64 * KB)
        VPH = at("VPH", [128, C, D], F32R, 76 * KB)
        VPL = at("VPL", [128, C, D], F32R, 84 * KB)
        HOT_S = at("HOT_S", [128, UN, N], BF16, 92 * KB)
        HOT_D = at("HOT_D", [128, UN, DB], BF16, 99.375 * KB)
        ZH = at("ZH", [128, C, N], F32R, 60 * KB)
        ZL = at("ZL", [128, C, N], F32R, 80 * KB)
        WKH = at("WKH", [128, C, D], F32R, 100 * KB)
        WKL = at("WKL", [128, C, D], F32R, 108 * KB)
        W1H = at("W1H", [128, C, D], F32R, 100 * KB)
        W1L = at("W1L", [128, C, D], F32R, 108 * KB)
        WVH = at("WVH", [128, C, D], F32R, 100 * KB)
        WVL = at("WVL", [128, C, D], F32R, 108 * KB)
        WQH = at("WQH", [128, C, D], F32R, 116 * KB)
        WQL = at("WQL", [128, C, D], F32R, 124 * KB)
        MPH = at("MPH", [128, C, D], F32R, 116 * KB)
        MPL = at("MPL", [128, C, D], F32R, 124 * KB)
        XF = at("XF", [128, NT, D], F32, 132 * KB)
        K = at("K", [128, NT, D], F32, 132 * KB)
        RAW_C = at("RAW_C", [128, C, D], F32, 152 * KB)
        AT = at("AT", [128, NB, NT, DB], F32R, 100 * KB)
        AL = at("AL", [128, NB, NT, DB], I8, 150 * KB)
        RAW_A = at("RAW_A", [128, C, D], F32, 168 * KB)
        RAW_B = at("RAW_B", [128, C, D], F32, 176 * KB)
        KMAX = at("KMAX", [128, D], F32, 186 * KB)
        Q = at("Q", [128, NT, D], F32, 168 * KB)
        W2H = at("W2H", [128, C, D], F32R, 188 * KB)
        W2L = at("W2L", [128, C, D], F32R, 196 * KB)
        CPH = at("CPH", [128, C, D], F32R, 188 * KB)
        CPL = at("CPL", [128, C, D], F32R, 196 * KB)
        DROW = at("DROW", [128, 2, ET], I32, 188 * KB)
        EDGE = at("EDGE", [128, 2, NE_T], I32, 189 * KB)
        grp = at("grp", [128, 2, 2], F32, 191 * KB)
        blk = at("blk", [128, 2], F32, 191 * KB + 32)
        blh = at("blh", [128, 7], F32, 191 * KB + 64)
        dg2 = at("dg2", [128, 2, NE_T], F32, 192 * KB)
        gio = at("gio", [128, 3, NE_T], F32, 194 * KB)
        bw = at("bw", [128, 4, NE_T], F32, 196 * KB)
        G1H = at("G1H", [128, C, D], F32R, 168 * KB)
        G1L = at("G1L", [128, C, D], F32R, 176 * KB)
        AC = at("AC", [128, 2, 5, DB], F32R, 184 * KB)
        G2H = at("G2H", [128, C, D], F32R, 188 * KB)
        G2L = at("G2L", [128, C, D], F32R, 196 * KB)
        RAW_G1 = at("RAW_G1", [128, C, D], F32, 188 * KB)
        drow = at("drow", [128, N], F32, 196 * KB)
        RAW_G2 = at("RAW_G2", [128, C, D], F32, 168 * KB)
        Y = at("Y", [128, NT, D], F32, 100 * KB)
        YT = at("YT", [128, 2, C, TT + 3], F32, 144 * KB)
        YX = at("YX", [128, 12, 2, D], F32, 60 * KB)
        FTH = at("FTH", [128, 2, C, SLOT + 2], F32R, 112 * KB)
        FTL = at("FTL", [128, 2, C, SLOT + 2], F32R, 115 * KB)
        FO = at("FO", [128, 4, D], F32, 52 * KB)
        WEH = [at(f"WEH{s}", [128, C, D], F32R, o * KB) for s, o in enumerate((20, 36, 120))]
        WEL = [at(f"WEL{s}", [128, C, D], F32R, (o + 8) * KB) for s, o in enumerate((20, 36, 120))]
        RAW_E = at("RAW_E", [128, C, D], F32, 136 * KB)
        GREP = at("GREP", [128, NT, 128], F32, 168 * KB)
        GT = at("GT", [128, N], F32, 173 * KB)
        RANK = at("RANK", [128, N], F32, 178 * KB)
        M_GT = at("M_GT", [128, N], BF16, 183 * KB)
        M_EQ = at("M_EQ", [128, N], BF16, 185.5 * KB)
        M_TIE = at("M_TIE", [128, N], BF16, 188 * KB)
        M_SEL = at("M_SEL", [128, N], BF16, 190.5 * KB)
        ROUTE = at("ROUTE", [128, NT, NS * SLOT], BF16, 168 * KB)

        ident = small("ident", [128, 128], F32, "a")
        ones = small("ones", [128, 128], F32, "a")
        tri = small("tri", [128, 128], F32, "a")
        iota = small("iota", [128, NPAD], F16, "a")
        srcf = small("srcf", [128, NE_T + UN], F32, "a")
        dstf = small("dstf", [128, NE_T + UN], F32, "a")
        diag = small("diag", [128, C, 128], F32, "b")
        ESUM = at("ESUM", [128, D], F32, 204 * KB)
        bias = at("bias", [128, D], F32, 204 * KB)
        stat = small("stat", [128, NT, 6], F32, "b")
        mv = small("mv", [128, NT, 2], F32, "b")
        rstd = small("rstd", [128, 4, NT], F32, "b")
        rmax = small("rmax", [128, NT], F32, "b")
        rsum = small("rsum", [128, 2, NT], F32, "b")
        kmt = small("kmt", [128, C], F32, "b")
        krs = small("krs", [128, 2, C], F32, "b")
        degs = small("degs", [128, NT], F32, "b")
        onesr = small("onesr", [128, 2], F32R, "b")
        odeg = small("odeg", [128, 2, NB], F32, "b")
        many = small("many", [128, 2], F32, "b")
        flag = small("flag", [128, 1], I32, "b")
        tab = small("tab", [128, 2, NB + 2], I32, "b")
        zero = small("zero", [128, TT + 3], BF16, "b")
        gw = small("gw", [128, C, NE], F32, "c")
        P8 = small("P8", [128, NT, NE], F32, "c")
        s8 = small("s8", [128, 2, NE], F32, "c")
        s10 = small("s10", [128, 4, NT], F32, "c")
        pick = small("pick", [128, NE], BF16, "c")
        blkones = small("blkones", [128, 128], F32, "c")
        ctab = small("ctab", [128, len(SHIFTS)], I32, "c")
        cb = small("cb", [128, 2], I32, "c")
        pre = small("pre", [128, 4], I32, "c")
        cnt = small("cnt", [128, 8], F32, "c")
        e1 = small("e1", [128, NT, NE], F32, "c")
        e156 = small("e156", [128, NE], F32, "c")
        fin = small("fin", [128, NE, NT], F32, "c")
        incl = small("incl", [128, NE, NT], F32, "c")
        reset = small("reset", [128, NE, NT], F32, "c")
        w8 = small("w8", [128, 2, NE, NT], F32, "c")
        tid = small("tid", [128, 2, NT], I32, "c")
        vals = small("vals", [128, NT, 6], BF16, "c")
        slot = small("slot", [128, NT], F32, "c")
        tokv = small("tokv", [128, 3, NS], F32, "c")
        idx = small("idx", [128, 2, NS], I32, "c")

        PS = [ctx.enter_context(nc.psum_tensor(f"ps{b}", [128, 512], F32)) for b in range(8)]

        def view(name, chunks=C):
            return PS[plan[name][0]].rearrange("p (c t) -> p c t", c=chunks)

        full = [sem(f"bank_full{b}") for b in range(8)]
        ld_x = [sem(f"ld_x{n}") for n in range(5)]
        loads = {n: sem(f"ld_{n}") for n in ("edges", "w1", "w2", "wk", "wq", "wv", "b1", "b2", "g1",
                                             "g2", "gate", "exp")}
        done = {n: sem(n) for n in (
            "consts rconsts w_hi w_lo el_split dve_chain pool_chain var_ready sqrt_ready xf_ready xnh_ready "
            "xnl_ready xth_ready xtl_ready grp_ready blen_ready tab_ready mph_ready mpl_ready "
            "k_stored kmax_step diag_ready rmax_ready q_exp q_ready k_shift k_exp eh_ready el_ready "
            "esum_ready krs_ready e_used xm_added vph_ready vpl_ready th_ready tl_ready cph_ready "
            "cpl_ready zero_ready adj_full adj_hi adj_lo qth_ready qtl_ready qp_added flag_in "
            "flag_ready zh_ready zl_ready ac_ready ac_used degrow_ready deg_ready t_ready h1h_ready "
            "h1l_ready x_final y_ready var2_ready sqrt2_ready yt_ready yt_used p_ready grep_ready "
            "gt_ready ind_ready prefix_ready msel_ready rowtot_ready route_ready idx_ready st_scratch "
            "st_out fth_ready ftl_ready fo_ready").split()}
        gathered = [sem(f"gathered{j}") for j in range(NS)]
        scattered = [sem(f"scattered{s}") for s in range(4)]
        hot = [sem(f"hot{s}") for s in range(UN)]
        hot_used = [sem(f"hot_used{s}") for s in range(UN)]

        splits = [(RAW_A, WKH, WKL, "wk"), (RAW_B, WQH, WQL, "wq"), (RAW_C, W2H, W2L, "w2"),
                  (RAW_C, W1H, W1L, "w1"), (RAW_C, WVH, WVL, "wv"), (RAW_G1, G1H, G1L, "g1"),
                  (RAW_G2, G2H, G2L, "g2")]
        NW = len(splits)
        order = {s[3]: n + 1 for n, s in enumerate(splits)}

        def reads(eng, name):
            eng.wait_ge(full[plan[name][0]], plan[name][1])

        block = ctx.enter_context(nc.Block())

        @block.sync
        def _(sp):
            def rows(w):
                return w.rearrange("(c p) f -> p c f", p=128)

            def tiles(a, i, n=1):
                return a[TT * i:TT * (i + n), :].rearrange("(i p) f -> p i f", p=TT)

            for n in range(5):
                sp.dma_start(X[0:TT, 2 * n:2 * n + 2, :], tiles(x_in, 2 * n, 2)).then_inc(ld_x[n], 16)
            sp.dma_start(RAW_A[:], rows(WkT)).then_inc(loads["wk"], 16)
            sp.dma_start(DROW[0:NE_T // 2], dst_in).then_inc(loads["edges"], 16)
            sp.dma_start(EDGE[0:ET, 0, :], src_t).then_inc(loads["edges"], 16)
            sp.dma_start(EDGE[0:ET, 1, :], dst_t).then_inc(loads["edges"], 16)
            sp.dma_start(RAW_B[:], rows(WqT)).then_inc(loads["wq"], 16)
            sp.dma_start(RAW_C[:], rows(mW2T)).then_inc(loads["w2"], 16)
            for last, name, w in (("w2", "w1", mW1), ("w1", "wv", Wv)):
                sp.wait_ge(done["w_hi"], order[last])
                sp.wait_ge(done["w_lo"], order[last])
                sp.dma_start(RAW_C[:], rows(w)).then_inc(loads[name], 16)
            sp.wait_ge(done["qp_added"], NT)
            sp.dma_start(RAW_G1[:], rows(gW1T)).then_inc(loads["g1"], 16)
            sp.dma_start(bias[0:TT, :], gb1.rearrange("(a f) -> a f", a=1).broadcast_to([TT, D])).then_inc(loads["b1"], 16)
            reads(sp, f"h{NT - 1}")
            sp.dma_start(RAW_G2[:], rows(gW2T)).then_inc(loads["g2"], 16)
            sp.wait_ge(done["t_ready"], NT)
            sp.dma_start(bias[0:TT, :], gb2.rearrange("(a f) -> a f", a=1).broadcast_to([TT, D])).then_inc(loads["b2"], 16)
            reads(sp, f"z2_2_{C - 1}")
            sp.dma_start(gw[:], rows(gate_w[0])).then_inc(loads["gate"], 16)
            sp.dma_start(RAW_E[:], rows(experts[0])).then_inc(loads["exp"], 16)
            for i in range(NT):
                sp.wait_ge(done["x_final"], i + 1)
                sp.dma_start(tiles(out, i), X[0:TT, i:i + 1, :]).then_inc(done["st_out"], 16)
                sp.dma_start(tiles(scratch, i)[:, :, D:2 * D], X[0:TT, i:i + 1, :]).then_inc(done["st_scratch"], 16)
                if i >= 3:
                    sp.wait_ge(done["y_ready"], i - 2)
                    sp.dma_start(tiles(scratch, i - 3)[:, :, 0:D], Y[0:TT, i - 3:i - 2, :]).then_inc(done["st_scratch"], 16)
            for i in range(NT - 3, NT):
                sp.wait_ge(done["y_ready"], i + 1)
                sp.dma_start(tiles(scratch, i)[:, :, 0:D], Y[0:TT, i:i + 1, :]).then_inc(done["st_scratch"], 16)
            for e in range(1, NE):
                sp.wait_ge(done["w_hi"], NW + e)
                if e <= 3:
                    sp.wait_ge(done["w_lo"], NW + e)
                else:
                    sp.wait_ge(done["el_split"], e - 3)
                sp.dma_start(RAW_E[:], rows(experts[e])).then_inc(loads["exp"], 16)
            sp.wait_ge(done["st_out"], 16 * NT)
            for s in range(4):
                sp.wait_ge(scattered[s], 16 * (NS // 4))

        @block.gpsimd
        def _(pool):
            count = [0]

            def link(ins):
                count[0] += 1
                ins.then_inc(done["pool_chain"], 1)
                pool.wait_ge(done["pool_chain"], count[0])

            link(nc.gpsimd.memset(ones[:], 1.0))
            link(nc.gpsimd.affine_select(out=ident[:], in_=ones[:], pattern=[[-1, 128]], compare_op=ALU.is_equal,
                                         fill=0.0, base=0, channel_multiplier=1))
            link(nc.gpsimd.affine_select(out=tri[:], in_=ones[:], pattern=[[1, 128]], compare_op=ALU.is_gt,
                                         fill=0.0, base=0, channel_multiplier=-1))
            for n, (step, base) in enumerate(((1, 1), (-1, NE_T))):
                link(nc.gpsimd.iota(gio[:, n, :].rearrange("p (h g) -> p h g", h=2), [[step, 2], [2 * step, NE_T // 2]],
                                    base=base, channel_multiplier=0, allow_small_or_imprecise_dtypes=True))
            link(nc.gpsimd.iota(gio[:, 2, :], [[UN, NE_T]], base=0, channel_multiplier=0,
                                allow_small_or_imprecise_dtypes=True))
            link(nc.gpsimd.iota(blk[:, 0:1], [[0, 1]], base=0, channel_multiplier=DB,
                                allow_small_or_imprecise_dtypes=True))
            link(nc.gpsimd.iota(blk[:, 1:2], [[0, 1]], base=DB - 1, channel_multiplier=DB,
                                allow_small_or_imprecise_dtypes=True))
            nc.gpsimd.iota(iota[:], [[1, NPAD]], base=0, channel_multiplier=0,
                           allow_small_or_imprecise_dtypes=True).then_inc(done["consts"], 1)

            def split_lo(n, raw, hi, lo):
                pool.wait_ge(done["w_hi"], n)
                nc.gpsimd.tensor_tensor(lo[:], raw[:], hi[:].bitcast(F32), ALU.subtract).then_inc(done["w_lo"], 1)

            for i in range(NT):
                if i == 0:
                    split_lo(order["wk"], *splits[0][:3])
                pool.wait_ge(done["xnh_ready"], i + 1)
                nc.gpsimd.tensor_tensor(XNL[0:TT, i, :], XF[0:TT, i, :], XNH[0:TT, i, :].bitcast(F32),
                                        ALU.subtract).then_inc(done["xnl_ready"], 1)
            for n in (order["wq"], order["w2"], order["w1"], order["wv"]):
                split_lo(n, *splits[n - 1][:3])

            def add_exp(i):
                pool.wait_ge(done["k_exp"], i + 1)
                if i == 0:
                    link(nc.gpsimd.tensor_copy(ESUM[0:TT, :], K[0:TT, 0, :]))
                elif i < NT - 1:
                    link(nc.gpsimd.tensor_tensor(ESUM[0:TT, :], ESUM[0:TT, :], K[0:TT, i, :], ALU.add))
                else:
                    nc.gpsimd.tensor_tensor(ESUM[0:TT, :], ESUM[0:TT, :], K[0:TT, i, :],
                                            ALU.add).then_inc(done["esum_ready"], 1)

            for i in range(NT):
                add_exp(i)
            split_lo(6, *splits[5][:3])
            split_lo(7, *splits[6][:3])

            reads(pool, f"z2_2_{C - 1}")
            link(nc.gpsimd.affine_select(out=blkones[:].rearrange("p (e c) -> p e c", c=16),
                                         in_=ones[:].rearrange("p (e c) -> p e c", c=16),
                                         pattern=[[-16, NE], [0, 16]], compare_op=ALU.is_ge, fill=0.0,
                                         base=0, channel_multiplier=1))
            link(nc.gpsimd.affine_select(out=blkones[:].rearrange("p (e c) -> p e c", c=16),
                                         in_=blkones[:].rearrange("p (e c) -> p e c", c=16),
                                         pattern=[[16, NE], [0, 16]], compare_op=ALU.is_ge, fill=0.0,
                                         base=15, channel_multiplier=-1))
            link(nc.gpsimd.affine_select(out=pick[:], in_=ones[:, 0:NE], pattern=[[-16, NE]],
                                         compare_op=ALU.is_equal, fill=0.0, base=0, channel_multiplier=1))
            link(nc.gpsimd.iota(cb[:, 0:1], [[0, 1]], base=0, channel_multiplier=1))
            link(nc.gpsimd.iota(e1[:], [[0, NT], [1, NE]], base=1, channel_multiplier=0,
                                allow_small_or_imprecise_dtypes=True))
            link(nc.gpsimd.iota(e156[:], [[TOPK, NE]], base=0, channel_multiplier=0,
                                allow_small_or_imprecise_dtypes=True))
            link(nc.gpsimd.memset(reset[:], 1.0))
            link(nc.gpsimd.memset(reset[:, :, 0:1], 0.0))
            nc.gpsimd.iota(tid[:, 0, :], [[TT, NT]], base=1, channel_multiplier=1).then_inc(done["rconsts"], 1)

            for e in range(3):
                split_lo(NW + e + 1, RAW_E, WEH[e], WEL[e])

            pool.wait_ge(done["st_scratch"], 2 * 16 * NT)
            pool.wait_ge(done["idx_ready"], 1)

            def gather(j):
                nc.gpsimd.indirect_dma_start(
                    out=YX[0:SLOT, j % 12].rearrange("p a f -> p (a f)"), out_offset=None, in_=scratch,
                    in_offset=bass.IndirectOffsetOnAxis(ap=idx[0:SLOT, 0, j:j + 1].bitcast(U32), axis=0)).then_inc(gathered[j], 16)

            for j in range(12):
                gather(j)
            pool.wait_ge(done["st_out"], 16 * NT)
            for j in range(NS):
                pool.wait_ge(done["fo_ready"], j + 1)
                nc.gpsimd.indirect_dma_start(
                    out=out, in_=FO[0:SLOT, j % 4, :], in_offset=None,
                    out_offset=bass.IndirectOffsetOnAxis(ap=idx[0:SLOT, 1, j:j + 1].bitcast(U32), axis=0),
                    bounds_check=N - 1, oob_is_err=False).then_inc(scattered[j % 4], 16)
                if j + 12 < NS:
                    gather(j + 12)

        @block.tensor
        def _(pe):
            def opens(name):
                for what, value in plan[name][2]:
                    pe.wait_ge(done[what], value)
                return PS[plan[name][0]]

            def closes(name, ins):
                ins.then_inc(full[plan[name][0]], 1)

            def product(name, ps, stationary, moving, chunks, between=None):
                pairs = [(a, b, c) for c in range(chunks) for a, b in ((0, 0), (0, 1), (1, 0))]
                for n, (a, b, c) in enumerate(pairs):
                    if n == 1 and between is not None:
                        between()
                    mm = pe.matmul(ps, stationary[a](c), moving[b](c), start=(n == 0), stop=(n == len(pairs) - 1))
                closes(name, mm)

            def block_of(t, f, w=128, off=0):
                return lambda c: t[:, c, f * w + off:(f + 1) * w + off]

            def rows_of(t):
                return lambda c: t[:, c, :]

            pe.wait_ge(done["consts"], 1)
            for i in range(NT):
                if i == 4:
                    pe.wait_ge(done["grp_ready"], 1)
                    ps = opens("bounds")
                    for n in range(2):
                        mm = pe.matmul(ps[0:NB, NE_T * n:NE_T * (n + 1)], ones[0:NE_T // 2, 0:NB], dg2[0:NE_T // 2, n, :], start=True, stop=True)
                    closes("bounds", mm)
                pe.wait_ge(done["xf_ready"], i + 1)
                opens(f"xt{i}")
                ps = view(f"xt{i}")
                for c in range(C):
                    mm = pe.transpose(ps[:, c, 0:TT], XF[0:TT, i, 128 * c:128 * (c + 1)], ident[0:TT, 0:TT])
                closes(f"xt{i}", mm)

            def tile_product(name, i, wh, wl):
                product(name, opens(name)[0:TT, :], (block_of(XTH, i, TT), block_of(XTL, i, TT)), (rows_of(wh), rows_of(wl)), C)

            pe.wait_ge(done["w_lo"], order["wk"])
            for i in range(NT):
                if i == 2:
                    pe.wait_ge(done["blen_ready"], 1)
                    ps = opens("bases")
                    pe.matmul(ps[0:1, 0:NB + 1], blh[0:NB, 0:1], tri[0:NB, 0:NB + 1], start=True, stop=True)
                    closes("bases", pe.matmul(ps[0:1, 32:32 + NB], blh[0:NB, 1:2], ident[0:NB, 0:NB], start=True, stop=True))
                pe.wait_ge(done["xtl_ready"], i + 1)
                tile_product(f"k{i}", i, WKH, WKL)
            pe.wait_ge(done["w_lo"], order["wq"])
            for i in range(NT):
                if i == 4:
                    pe.wait_ge(done["kmax_step"], NT)
                    opens("kmt")
                    for c in range(C):
                        mm = pe.transpose(view("kmt")[:, c, 0:TT], KMAX[0:TT, 128 * c:128 * (c + 1)], ident[0:TT, 0:TT])
                    closes("kmt", mm)
                if i == 7:
                    pe.wait_ge(done["diag_ready"], 1)
                    closes("kmb", pe.matmul(opens("kmb")[0:TT, :], ones[:, 0:TT], diag[:].rearrange("p c f -> p (c f)"),
                                            start=True, stop=True))
                tile_product(f"q{i}", i, WQH, WQL)
            pe.wait_ge(done["w_lo"], order["w1"])
            for c in range(C):
                ps = opens(f"mp{c}")
                product(f"mp{c}", ps[:], (block_of(W1H, c), block_of(W1L, c)), (rows_of(W2H), rows_of(W2L)), C,
                        between=lambda: pe.matmul(ps[:, 128 * c:128 * (c + 1)], ident[:], ident[:], start=False, stop=False))
            pe.wait_ge(done["mpl_ready"], C)
            for i in range(NT):
                tile_product(f"xm{i}", i, MPH, MPL)
            pe.wait_ge(done["w_lo"], order["wv"])
            for c in range(C):
                product(f"vp{c}", opens(f"vp{c}")[:], (block_of(WVH, c), block_of(WVL, c)), (rows_of(MPH), rows_of(MPL)), C)
            def context(i):
                pe.wait_ge(done["el_ready"], i + 1)
                for c in range(C):
                    ps = opens(f"tt{c}") if i == 0 else PS[plan[f"tt{c}"][0]]
                    f = slice(128 * c, 128 * (c + 1))
                    pe.matmul(ps[:], XNH[0:TT, i, f], EH[0:TT, i % 4, :], start=(i == 0), stop=False)
                    pe.matmul(ps[:], XNH[0:TT, i, f], EL[0:TT, i % 4, :], start=False, stop=False)
                    mm = pe.matmul(ps[:], XNL[0:TT, i, f], EH[0:TT, i % 4, :], start=False, stop=(i == NT - 1))
                    if i == NT - 1:
                        closes(f"tt{c}", mm)
                    elif c == C - 1:
                        mm.then_inc(done["e_used"], 1)

            def values(_):
                pe.wait_ge(done["esum_ready"], 1)
                ps = opens("ks")
                for c in range(C):
                    mm = pe.matmul(ps[:, c:c + 1], ESUM[0:TT, 128 * c:128 * (c + 1)], ones[0:TT, 0:1], start=True, stop=True)
                closes("ks", mm)
                pe.wait_ge(done["tl_ready"], C)
                pe.wait_ge(done["vpl_ready"], C)
                for c in range(C):
                    product(f"cp{c}", opens(f"cp{c}")[:], (block_of(TH, c), block_of(TL, c)), (rows_of(VPH), rows_of(VPL)), C)
                turn_q(0)

            def turn_q(i):
                pe.wait_ge(done["q_ready"], i + 1)
                opens(f"qt{i}")
                for c in range(C):
                    mm = pe.transpose(view(f"qt{i}")[:, c, 0:TT], Q[0:TT, i, 128 * c:128 * (c + 1)], ident[0:TT, 0:TT])
                closes(f"qt{i}", mm)

            def attend(i):
                if i + 1 < NT:
                    turn_q(i + 1)
                pe.wait_ge(done["qtl_ready"], i + 1)
                if i == 0:
                    pe.wait_ge(done["cpl_ready"], C)
                product(f"qp{i}", opens(f"qp{i}")[0:TT, :],
                        (lambda c: QTH[:, i % 2, c, 0:TT], lambda c: QTL[:, i % 2, c, 0:TT]), (rows_of(CPH), rows_of(CPL)), C)

            for b in range(4, 8):
                opens(f"adj{b}")
            pe.wait_ge(done["tab_ready"], 1)
            pe.wait_ge(done["zero_ready"], 1)
            for s in range(UN):
                pe.sem_inc(hot_used[s], 1)
            for b in range(NB):
                if b >= 2:
                    pe.wait_ge(done["adj_hi"], b - 1)
                    pe.wait_ge(done["adj_lo"], b - 1)
                half = [PS[4 + 2 * (b % 2) + h] for h in range(2)]

                def add_zero(h, **flags):
                    return pe.matmul(half[h][0:TT, 0:5 * DB], zero[0:1, 0:TT], iota[0:1, 0:5 * DB], skip_group_check=True, **flags)

                for h in range(2):
                    add_zero(h, start=True, stop=False)
                first = pe.value_load(tab[0:1, 0, b:b + 1], min_val=0, max_val=NB * NE_T)
                end = pe.value_load(tab[0:1, 0, b + 1:b + 2], min_val=1, max_val=NB * NE_T)
                with pe.Fori(first, end) as n:
                    for s in range(UN):
                        pe.wait_ge(hot[s], n + 1)
                        for k in range(NT):
                            mm = pe.matmul(half[k // 5][0:TT, (k % 5) * DB:(k % 5 + 1) * DB], HOT_S[0:ET, s, TT * k:TT * (k + 1)],
                                           HOT_D[0:ET, s, :], start=False, stop=False, skip_group_check=True)
                        mm.then_inc(hot_used[s], 1)
                for h in range(2):
                    mm = add_zero(h, start=False, stop=True)
                mm.then_inc(done["adj_full"], 1)
                for what, i in BEHIND[b]:
                    {"context": context, "values": values, "attend": attend}[what](i)

            pe.wait_ge(done["flag_in"], 1)
            closes("flag", pe.matmul(opens("flag")[0:1, 0:1], many[0:TT, 1:2], ones[0:TT, 0:1], start=True, stop=True))
            pe.wait_ge(done["flag_ready"], 1)
            large = pe.value_load(flag[0:1, 0:1], min_val=0, max_val=1)

            def aggregate(layer, hi, lo):
                for ch, (b0, b1) in enumerate(SPANS):
                    w = (b1 - b0) * DB
                    names = [f"z{layer}_{ch}_{f}" for f in range(C)] + ([f"deg{ch}"] if layer == 1 else [])

                    def operands(k, f):
                        if f == C:
                            return [onesr[0:TT, :]]
                        return [t[0:TT, k, 128 * f:128 * (f + 1)] for t in (hi, lo)]

                    def place(f):
                        return PS[plan[names[f]][0]][0:(2 if f == C else 128), 0:w]

                    for f, name in enumerate(names):
                        opens(name)
                        for n, a in enumerate(operands(0, f)):
                            pe.matmul(place(f), a, AT[0:TT, b0:b1, 0, :], start=(n == 0), stop=False)
                    with pe.If(large > 0):
                        for k in range(NT):
                            pe.wait_ge(done["ac_ready"], ((layer - 1) * 3 + ch) * NT + k + 1)
                            for f in range(len(names)):
                                for a in operands(k, f):
                                    mm = pe.matmul(place(f), a, AC[0:TT, k % 2, 0:b1 - b0, :], start=False, stop=False)
                            mm.then_inc(done["ac_used"], 1)
                    with pe.Else():
                        pe.nop()
                    for f, name in enumerate(names):
                        for k in range(1, NT):
                            for n, a in enumerate(operands(k, f)):
                                last = k == NT - 1 and n == len(operands(k, f)) - 1
                                mm = pe.matmul(place(f), a, AT[0:TT, b0:b1, k, :], start=False, stop=last)
                        closes(name, mm)

            def dense(name, i, wh, wl):
                product(name, opens(name)[0:TT, :], (block_of(ZH, i, TT), block_of(ZL, i, TT)), (rows_of(wh), rows_of(wl)), C)

            aggregate(1, XNH, XNL)
            pe.wait_ge(done["degrow_ready"], 3)
            ps = opens("degt")
            for i in range(NT):
                mm = pe.matmul(ps[0:TT, i:i + 1], drow[0:1, TT * i:TT * (i + 1)], ones[0:1, 0:1], start=True, stop=True)
            closes("degt", mm)
            pe.wait_ge(done["w_lo"], order["g1"])
            pe.wait_ge(done["zl_ready"], 3 * C)
            for i in range(NT):
                dense(f"h{i}", i, G1H, G1L)
            pe.wait_ge(done["h1l_ready"], NT)
            aggregate(2, H1H, H1L)
            pe.wait_ge(done["w_lo"], order["g2"])
            pe.wait_ge(done["zl_ready"], 6 * C)
            pe.wait_ge(loads["gate"], 16)

            def turn_y(i):
                pe.wait_ge(done["y_ready"], i + 1)
                opens(f"yt{i}")
                for c in range(C):
                    mm = pe.transpose(view(f"yt{i}")[:, c, 0:TT], Y[0:TT, i, 128 * c:128 * (c + 1)], ident[0:TT, 0:TT])
                closes(f"yt{i}", mm)

            def logits(i):
                pe.wait_ge(done["yt_ready"], i + 1)
                for c in range(C):
                    mm = pe.matmul(PS[plan["logits"][0]][0:TT, NE * i:NE * (i + 1)], YT[:, i % 2, c, 0:TT], gw[:, c, :],
                                   start=(c == 0), stop=(c == C - 1))
                if i == NT - 1:
                    closes("logits", mm)
                else:
                    mm.then_inc(done["yt_used"], 1)

            opens("logits")
            for i in range(NT + 6):
                if i < NT:
                    dense(f"o{i}", i, G2H, G2L)
                if 5 <= i < NT + 5:
                    turn_y(i - 5)
                if i >= 6:
                    logits(i - 6)

            for r in range(SINKHORN):
                pe.wait_ge(done["p_ready"], r + 1)
                closes(f"sink{r}", pe.matmul(opens(f"sink{r}")[0:TT, 0:NE], ones[0:TT, 0:TT], s8[0:TT, 0, :],
                                             start=True, stop=True))
            pe.wait_ge(done["grep_ready"], 1)
            for h in range(3):
                opens(f"gt{h}")
                for i in range(4 * h, min(4 * h + 4, NT)):
                    mm = pe.transpose(view(f"gt{h}")[:, i % 4, 0:TT], GREP[0:TT, i, :], ident[0:TT, 0:TT])
                closes(f"gt{h}", mm)
            pe.wait_ge(done["rconsts"], 1)
            for r in range(len(SHIFTS)):
                pe.wait_ge(done["ind_ready"], r + 1)
                closes(f"rad{r}", pe.matmul(opens(f"rad{r}")[:, 0:1], blkones[:], cnt[:, 1:2], start=True, stop=True))
            pe.wait_ge(done["msel_ready"], 1)
            ps = opens("sel")
            for i in range(NT):
                mm = pe.matmul(ps[0:TT, NE * i:NE * (i + 1)], M_SEL[:, TT * i:TT * (i + 1)], pick[:], start=True, stop=True)
            closes("sel", mm)
            pe.wait_ge(done["rowtot_ready"], 1)
            closes("off", pe.matmul(opens("off")[0:TT, 0:NE], tri[0:TT, 0:TT], s8[0:TT, 1, :], start=True, stop=True))
            ps = opens("slots")
            pe.wait_ge(done["route_ready"], NT)
            for j in range(NS):
                for i in range(NT):
                    mm = pe.matmul(ps[0:SLOT, 6 * j:6 * (j + 1)], ROUTE[0:TT, i, SLOT * j:SLOT * (j + 1)], vals[0:TT, i, :],
                                   start=(i == 0), stop=(i == NT - 1))
            closes("slots", mm)

            for j in range(NS + 1):
                if j < NS:
                    pe.wait_ge(gathered[j], 16)
                    opens(f"ft{j}")
                    for c in range(C):
                        mm = pe.transpose(view(f"ft{j}")[:, c, 0:SLOT], YX[0:SLOT, j % 12, 0, 128 * c:128 * (c + 1)], ident[0:SLOT, 0:SLOT])
                    closes(f"ft{j}", mm)
                if j:
                    t = j - 1
                    e = t // 2
                    if e < 3:
                        pe.wait_ge(done["w_lo"], NW + e + 1)
                    else:
                        pe.wait_ge(done["el_split"], e - 2)
                    pe.wait_ge(done["ftl_ready"], t + 1)
                    product(f"fo{t}", opens(f"fo{t}")[0:SLOT, :],
                            (lambda c: FTH[:, t % 2, c, 0:SLOT], lambda c: FTL[:, t % 2, c, 0:SLOT]),
                            (rows_of(WEH[e % 3]), rows_of(WEL[e % 3])), C)

        @block.scalar
        def _(act):
            def copy(o, i, **kw):
                return nc.scalar.activation(o, i, ACT.Copy, **kw)

            def split_hi(n, raw, hi, load, value=16):
                act.wait_ge(loads[load], value)
                copy(hi[:], raw[:]).then_inc(done["w_hi"], 1)

            def split_named(name):
                n = order[name] - 1
                split_hi(n, splits[n][0], splits[n][1], name)

            act.wait_ge(done["var_ready"], 1)
            nc.scalar.activation(rstd[0:TT, 1, :], rstd[0:TT, 0, :], ACT.Sqrt).then_inc(done["sqrt_ready"], 1)
            split_named("wk")
            for i in range(NT):
                act.wait_ge(done["xf_ready"], i + 1)
                copy(XNH[0:TT, i, :], XF[0:TT, i, :]).then_inc(done["xnh_ready"], 1)
                reads(act, f"xt{i}")
                copy(XTH[:, :, TT * i:TT * (i + 1)], view(f"xt{i}")[:, :, 0:TT]).then_inc(done["xth_ready"], 1)
            split_named("wq")
            for i in range(NT):
                if i == 3:
                    reads(act, "bases")
                    split_named("w2")
                reads(act, f"k{i}")
                act.wait_ge(done["xnl_ready"], i + 1)
                ps = PS[plan[f"k{i}"][0]]
                copy(K[0:TT, i, :], ps[0:TT, :]).then_inc(done["k_stored"], 1)
            split_named("w1")
            for i in range(NT):
                ps = PS[plan[f"q{i}"][0]]
                act.wait_ge(done["rmax_ready"], i + 1)
                if i == 0:
                    act.wait_ge(done["w_lo"], order["wq"])
                nc.scalar.activation(Q[0:TT, i, :], ps[0:TT, :], ACT.Exp, bias=rmax[0:TT, i:i + 1],
                                     accum_out=rsum[0:TT, 0, i:i + 1]).then_inc(done["q_exp"], 1)
            for c in range(C):
                reads(act, f"mp{c}")
                copy(MPH[:, c, :], PS[plan[f"mp{c}"][0]][:]).then_inc(done["mph_ready"], 1)
            split_named("wv")
            for i in range(NT):
                act.wait_ge(done["k_shift"], i + 1)
                nc.scalar.activation(K[0:TT, i, :], K[0:TT, i, :], ACT.Exp).then_inc(done["k_exp"], 1)
            def round_exp(i):
                act.wait_ge(done["k_exp"], i + 1)
                if i >= 4:
                    act.wait_ge(done["e_used"], i - 3)
                copy(EH[0:TT, i % 4, :], K[0:TT, i, :]).then_inc(done["eh_ready"], 1)

            def block_counts(b):
                act.wait_ge(done["adj_full"], b + 1)
                for h in range(2):
                    src = PS[4 + 2 * (b % 2) + h][0:TT, 0:5 * DB]
                    ins = nc.scalar.activation(AT[0:TT, b, 5 * h:5 * h + 5, :].rearrange("p k d -> p (k d)"), src, ACT.Copy,
                                               accum_out=odeg[0:TT, h, b:b + 1])
                ins.then_inc(done["adj_hi"], 1)

            def round_q(i):
                reads(act, f"qt{i}")
                if i >= 2:
                    reads(act, f"qp{i - 2}")
                copy(QTH[:, i % 2, :, 0:TT], view(f"qt{i}")[:, :, 0:TT]).then_inc(done["qth_ready"], 1)

            for c in range(C):
                reads(act, f"vp{c}")
                copy(VPH[:, c, :], PS[plan[f"vp{c}"][0]][:]).then_inc(done["vph_ready"], 1)
                round_exp(c)
            for b in range(NB):
                if b >= 1:
                    block_counts(b - 1)
                if 1 <= b < 4:
                    round_exp(2 * b + 2)
                    round_exp(2 * b + 3)
                if b == 5:
                    reads(act, f"tt{C - 1}")
                    for c in range(C):
                        reads(act, f"tt{c}")
                        copy(TH[:, c, :], PS[plan[f"tt{c}"][0]][:]).then_inc(done["th_ready"], 1)
                if b == 6:
                    act.wait_ge(done["krs_ready"], 1)
                    for c in range(C):
                        reads(act, f"cp{c}")
                        copy(CPH[:, c, :], PS[plan[f"cp{c}"][0]][:], scale=krs[:, 1, c:c + 1]).then_inc(done["cph_ready"], 1)
                    round_q(0)
                for what, i in BEHIND[b]:
                    if what == "attend" and i + 1 < NT:
                        round_q(i + 1)
            block_counts(NB - 1)
            reads(act, f"qp{NT - 1}")
            split_named("g1")

            def z_hi(layer):
                for ch, (b0, b1) in enumerate(SPANS):
                    c0, w = b0 * DB, min(b1 * DB, N) - b0 * DB
                    for f in range(C):
                        name = f"z{layer}_{ch}_{f}"
                        reads(act, name)
                        if layer == 2 and ch == f == 0:
                            reads(act, f"h{NT - 1}")
                        copy(ZH[:, f, c0:c0 + w], PS[plan[name][0]][:, 0:w]).then_inc(done["zh_ready"], 1)

            z_hi(1)
            for i in range(NT):
                act.wait_ge(done["t_ready"], i + 1)
                nc.scalar.activation(H1H[0:TT, i, :], PS[plan[f"h{i}"][0]][0:TT, :], ACT.Relu).then_inc(done["h1h_ready"], 1)
            act.wait_ge(done["w_lo"], order["g1"])
            split_named("g2")
            z_hi(2)

            def split_expert(e):
                if e >= 3:
                    reads(act, f"fo{2 * (e - 3) + 1}")
                split_hi(NW + e, RAW_E, WEH[e % 3], "exp", 16 * (e + 1))

            def copy_yt(i):
                reads(act, f"yt{i}")
                if i >= 2:
                    act.wait_ge(done["yt_used"], i - 1)
                copy(YT[:, i % 2, :, 0:TT], view(f"yt{i}")[:, :, 0:TT]).then_inc(done["yt_ready"], 1)

            split_expert(0)
            for p in range(NT // 2):
                for i in range(max(2 * p - 7, 0), 2 * p - 5):
                    copy_yt(i)
                act.wait_ge(done["var2_ready"], p + 1)
                nc.scalar.activation(rstd[0:TT, 1, 2 * p:2 * p + 2], rstd[0:TT, 0, 2 * p:2 * p + 2],
                                     ACT.Sqrt).then_inc(done["sqrt2_ready"], 1)
            for i in range(NT - 7, NT):
                copy_yt(i)
            split_expert(1)
            split_expert(2)
            for h in range(3):
                reads(act, f"gt{h}")
                n = min(4, NT - 4 * h)
                copy(GT[:, TT * 4 * h:TT * (4 * h + n)].rearrange("p (i t) -> p i t", i=n),
                     view(f"gt{h}")[:, 0:n, 0:TT]).then_inc(done["gt_ready"], 1)
            for j in range(NS):
                reads(act, f"ft{j}")
                if j >= 2:
                    reads(act, f"fo{j - 2}")
                copy(FTH[:, j % 2, :, 0:SLOT], view(f"ft{j}")[:, :, 0:SLOT]).then_inc(done["fth_ready"], 1)
                if j % 2 == 1 and j // 2 + 2 < NE and j >= 3:
                    split_expert(j // 2 + 2)

        @block.vector
        def _(dve):
            V = nc.vector
            count = [0]

            def link(ins):
                count[0] += 1
                ins.then_inc(done["dve_chain"], 1)
                dve.wait_ge(done["dve_chain"], count[0])

            def after(name, value):
                dve.wait_ge(done[name], value)

            def ps_of(name):
                return PS[plan[name][0]]

            t = slice(0, TT)

            def variance(w, signal):
                V.tensor_scalar(rstd[t, 0, w], mv[t, w, 1], LN_EPS, None, ALU.add).then_inc(done[signal], 1)

            def inverse_root(w):
                link(V.reciprocal(rstd[t, 2, w], rstd[t, 1, w]))
                link(V.tensor_tensor(rstd[t, 3, w], rstd[t, 2, w], rstd[t, 2, w], ALU.mult))
                link(V.tensor_tensor(rstd[t, 3, w], rstd[t, 3, w], rstd[t, 0, w], ALU.mult))
                link(V.tensor_scalar(rstd[t, 3, w], rstd[t, 3, w], -0.5, 1.5, ALU.mult, ALU.add))
                link(V.tensor_tensor(rstd[t, 2, w], rstd[t, 2, w], rstd[t, 3, w], ALU.mult))

            for i in range(NT):
                if i % 2 == 0:
                    dve.wait_ge(ld_x[i // 2], 16)
                ins = V.bn_stats(stat[0:TT, i, :], X[0:TT, i, :])
            link(ins)
            for i in range(NT):
                ins = V.bn_aggr(mv[0:TT, i, :], stat[0:TT, i, :])
            link(ins)
            variance(slice(0, NT), "var_ready")
            after("sqrt_ready", 1)
            inverse_root(slice(0, NT))
            for i in range(NT):
                V.tensor_scalar(XF[0:TT, i, :], X[0:TT, i, :], mv[0:TT, i, 0:1], rstd[0:TT, 2, i:i + 1],
                                ALU.subtract, ALU.mult).then_inc(done["xf_ready"], 1)

            G = NE_T // 2
            dve.wait_ge(loads["edges"], 48)
            V.tensor_reduce(grp[0:G, 0, :], DROW[0:G], AX, ALU.min)
            link(V.tensor_reduce(grp[0:G, 1, :], DROW[0:G], AX, ALU.max))
            after("consts", 1)
            V.tensor_copy(onesr[:], ones[:, 0:2])
            V.memset(zero[:], 0.0).then_inc(done["zero_ready"], 1)
            for n in range(2):
                for h in range(2):
                    ins = V.tensor_scalar(dg2[0:G, n, G * h:G * (h + 1)], ident[0:G, 0:G], grp[0:G, n, h:h + 1], None, ALU.mult)
            ins.then_inc(done["grp_ready"], 1)
            V.memset(srcf[0:ET, NE_T:NE_T + UN], -1.0)
            V.memset(dstf[0:ET, NE_T:NE_T + UN], -1.0)
            V.tensor_copy(srcf[0:ET, 0:NE_T], EDGE[0:ET, 0, :])
            V.tensor_copy(dstf[0:ET, 0:NE_T], EDGE[0:ET, 1, :])
            for i in range(NT):
                if i == 2:
                    reads(dve, "bounds")
                    ps = ps_of("bounds")
                    b_ = slice(0, NB)
                    link(V.tensor_scalar(bw[b_, 0, :], ps[b_, 0:NE_T], blk[b_, 1:2], None, ALU.is_le))
                    link(V.scalar_tensor_tensor(bw[b_, 1, :], ps[b_, NE_T:2 * NE_T], blk[b_, 0:1], bw[b_, 0, :], ALU.is_ge, ALU.mult))
                    V.tensor_tensor(bw[b_, 2, :], bw[b_, 1, :], gio[b_, 0, :], ALU.mult)
                    link(V.tensor_tensor(bw[b_, 3, :], bw[b_, 1, :], gio[b_, 1, :], ALU.mult))
                    V.tensor_reduce(blh[b_, 2:3], bw[b_, 2, :], AX, ALU.max)
                    link(V.tensor_reduce(blh[b_, 3:4], bw[b_, 3, :], AX, ALU.max))
                    link(V.tensor_scalar(blh[b_, 4:5], blh[b_, 3:4], -1.0, float(NE_T), ALU.mult, ALU.add))
                    link(V.tensor_scalar(blh[b_, 1:2], blh[b_, 4:5], float(NE_T - 1), None, ALU.min))
                    link(V.scalar_tensor_tensor(blh[b_, 5:6], blh[b_, 1:2], 1.0, blh[b_, 2:3], ALU.add, ALU.max))
                    link(V.tensor_tensor(blh[b_, 6:7], blh[b_, 5:6], blh[b_, 1:2], ALU.subtract))
                    V.tensor_scalar(bw[b_, 0, :], gio[b_, 2, :], blh[b_, 6:7], None, ALU.is_lt, ALU.add,
                                    accum_out=blh[b_, 0:1]).then_inc(done["blen_ready"], 1)
                after("xth_ready", i + 1)
                V.tensor_tensor(XTL[:, :, TT * i:TT * (i + 1)], view(f"xt{i}")[:, :, 0:TT],
                                XTH[:, :, TT * i:TT * (i + 1)].bitcast(F32), ALU.subtract).then_inc(done["xtl_ready"], 1)
            reads(dve, "bases")
            ps = ps_of("bases")
            link(V.tensor_copy(tab[0:1, 0, 0:NB + 1], ps[0:1, 0:NB + 1]))
            V.scalar_tensor_tensor(tab[0:1, 1, 0:NB], tab[0:1, 0, 0:NB], -float(UN), ps[0:1, 32:32 + NB], ALU.mult,
                                   ALU.add).then_inc(done["tab_ready"], 1)
            after("tab_ready", 1)

            for i in range(NT):
                after("k_stored", i + 1)
                ps = ps_of(f"k{i}")[0:TT, :]
                if i == 0:
                    V.tensor_copy(KMAX[0:TT, :], ps).then_inc(done["kmax_step"], 1)
                else:
                    after("kmax_step", i)
                    V.tensor_tensor(KMAX[0:TT, :], ps, KMAX[0:TT, :], ALU.max).then_inc(done["kmax_step"], 1)

            def q_scale(i):
                after("q_exp", i + 1)
                link(V.reciprocal(rsum[0:TT, 1, i:i + 1], rsum[0:TT, 0, i:i + 1]))
                V.tensor_scalar(Q[0:TT, i, :], Q[0:TT, i, :], rsum[0:TT, 1, i:i + 1], None, ALU.mult).then_inc(done["q_ready"], 1)

            def shift(i):
                if i == 0:
                    reads(dve, "kmb")
                after("k_stored", i + 1)
                V.tensor_tensor(K[0:TT, i, :], K[0:TT, i, :], ps_of("kmb")[0:TT, :], ALU.subtract).then_inc(done["k_shift"], 1)

            for i in range(NT):
                reads(dve, f"q{i}")
                V.tensor_reduce(rmax[0:TT, i:i + 1], ps_of(f"q{i}")[0:TT, :], AX, ALU.max, negate=True).then_inc(done["rmax_ready"], 1)
                if i == 3:
                    reads(dve, "kmt")
                    link(V.tensor_reduce(kmt[:], view("kmt")[:, :, 0:TT], AX, ALU.max))
                    for c in range(C):
                        ins = V.tensor_scalar(diag[:, c, :], ident[:], kmt[:, c:c + 1], None, ALU.mult)
                    ins.then_inc(done["diag_ready"], 1)
                if i >= 1:
                    q_scale(i - 1)
                if i >= 8:
                    shift(i - 8)
            q_scale(NT - 1)
            for c in range(C):
                after("mph_ready", c + 1)
                V.tensor_tensor(MPL[:, c, :], ps_of(f"mp{c}")[:], MPH[:, c, :].bitcast(F32), ALU.subtract).then_inc(done["mpl_ready"], 1)
            for i in range(NT):
                if i + 2 < NT:
                    shift(i + 2)
                reads(dve, f"xm{i}")
                after("xf_ready", i + 1)
                V.tensor_tensor(X[0:TT, i, :], ps_of(f"xm{i}")[0:TT, :], X[0:TT, i, :], ALU.add).then_inc(done["xm_added"], 1)
            def exp_left(i):
                after("eh_ready", i + 1)
                V.tensor_tensor(EL[0:TT, i % 4, :], K[0:TT, i, :], EH[0:TT, i % 4, :].bitcast(F32), ALU.subtract).then_inc(done["el_ready"], 1)

            for c in range(C):
                after("vph_ready", c + 1)
                V.tensor_tensor(VPL[:, c, :], ps_of(f"vp{c}")[:], VPH[:, c, :].bitcast(F32), ALU.subtract).then_inc(done["vpl_ready"], 1)
                exp_left(c)


            def counts_left(b):
                after("adj_hi", b + 1)
                for h in range(2):
                    src = PS[4 + 2 * (b % 2) + h][0:TT, 0:5 * DB].rearrange("p (k d) -> p k d", k=5)
                    ins = V.tensor_tensor(AL[0:TT, NB - 1 - b, 5 * h:5 * h + 5, :], src,
                                          AT[0:TT, b, 5 * h:5 * h + 5, :].bitcast(F32), ALU.subtract)
                ins.then_inc(done["adj_lo"], 1)

            def add_attention(i):
                reads(dve, f"qp{i}")
                V.tensor_tensor(X[0:TT, i, :], ps_of(f"qp{i}")[0:TT, :], X[0:TT, i, :], ALU.add).then_inc(done["qp_added"], 1)

            def q_left(i):
                after("qth_ready", i + 1)
                V.tensor_tensor(QTL[:, i % 2, :, 0:TT], view(f"qt{i}")[:, :, 0:TT], QTH[:, i % 2, :, 0:TT].bitcast(F32),
                                ALU.subtract).then_inc(done["qtl_ready"], 1)

            after("xm_added", NT)
            for b in range(NB):
                first = dve.value_load(tab[0:1, 0, b:b + 1], min_val=0, max_val=NB * NE_T)
                end = dve.value_load(tab[0:1, 0, b + 1:b + 2], min_val=1, max_val=NB * NE_T)
                behind = dve.value_load(tab[0:1, 1, b:b + 1], min_val=-UN * NB * NE_T, max_val=NE_T)
                with dve.Fori(first, end) as n:
                    for s in range(UN):
                        col = nc.s_assert_within(UN * n + behind + s, 0, NE_T + UN - 1,
                                                 skip_runtime_bounds_check_because="lo + UN (n - first) < hi + UN")
                        dve.wait_ge(hot_used[s], n + 1)
                        V.tensor_scalar(HOT_D[0:ET, s, :], iota[0:ET, DB * b:DB * (b + 1)], dstf[0:ET, bass.ds(col, 1)], None,
                                        ALU.is_equal)
                        V.tensor_scalar(HOT_S[0:ET, s, :], iota[0:ET, 0:N], srcf[0:ET, bass.ds(col, 1)], None,
                                        ALU.is_equal).then_inc(hot[s], 1)
                if b >= 1:
                    counts_left(b - 1)
                if 1 <= b < 4:
                    exp_left(2 * b + 2)
                    exp_left(2 * b + 3)
                if b == 5:
                    for c in range(C):
                        after("th_ready", c + 1)
                        V.tensor_tensor(TL[:, c, :], ps_of(f"tt{c}")[:], TH[:, c, :].bitcast(F32), ALU.subtract).then_inc(done["tl_ready"], 1)
                if b == 6:
                    reads(dve, "ks")
                    link(V.reciprocal(krs[:, 0, :], ps_of("ks")[:, 0:C]))
                    V.tensor_scalar(krs[:, 1, :], krs[:, 0, :], float(D) ** -0.5, None, ALU.mult).then_inc(done["krs_ready"], 1)
                    for c in range(C):
                        after("cph_ready", c + 1)
                        V.scalar_tensor_tensor(CPL[:, c, :], ps_of(f"cp{c}")[:], krs[:, 1, c:c + 1], CPH[:, c, :].bitcast(F32),
                                               ALU.mult, ALU.subtract).then_inc(done["cpl_ready"], 1)
                    q_left(0)
                for what, i in BEHIND[b]:
                    if what == "attend":
                        if i + 1 < NT:
                            q_left(i + 1)
                        if i >= 1:
                            add_attention(i - 1)
            counts_left(NB - 1)
            add_attention(NT - 1)

            link(V.tensor_reduce(many[0:TT, 0:1], odeg[0:TT], mybir.AxisListType.XY, ALU.add))
            V.tensor_scalar(many[0:TT, 1:2], many[0:TT, 0:1], EXACT, None, ALU.is_gt).then_inc(done["flag_in"], 1)
            reads(dve, "flag")
            V.tensor_scalar(flag[0:1, 0:1], ps_of("flag")[0:1, 0:1], 0.5, None, ALU.is_gt).then_inc(done["flag_ready"], 1)
            after("flag_ready", 1)
            large = dve.value_load(flag[0:1, 0:1], min_val=0, max_val=1)

            def aggregate(layer):
                for ch, (b0, b1) in enumerate(SPANS):
                    c0, w = b0 * DB, min(b1 * DB, N) - b0 * DB
                    with dve.If(large > 0):
                        for k in range(NT):
                            n = ((layer - 1) * 3 + ch) * NT + k
                            if n >= 2:
                                after("ac_used", n - 1)
                            for b in range(b0, b1):
                                ins = V.tensor_copy(AC[0:TT, k % 2, b - b0, :], AL[0:TT, NB - 1 - b, k, :])
                            ins.then_inc(done["ac_ready"], 1)
                    with dve.Else():
                        dve.nop()
                    for f in range(C):
                        n = ((layer - 1) * 3 + ch) * C + f + 1
                        after("zh_ready", n)
                        V.tensor_tensor(ZL[:, f, c0:c0 + w], ps_of(f"z{layer}_{ch}_{f}")[:, 0:w], ZH[:, f, c0:c0 + w].bitcast(F32),
                                        ALU.subtract).then_inc(done["zl_ready"], 1)
                    if layer == 1:
                        reads(dve, f"deg{ch}")
                        V.tensor_copy(drow[0:1, c0:c0 + w], ps_of(f"deg{ch}")[0:1, 0:w]).then_inc(done["degrow_ready"], 1)

            aggregate(1)
            reads(dve, "degt")
            V.tensor_copy(degs[0:TT, :], ps_of("degt")[0:TT, 0:NT]).then_inc(done["deg_ready"], 1)
            after("deg_ready", 1)
            dve.wait_ge(loads["b1"], 16)
            for i in range(NT + 1):
                if i < NT:
                    reads(dve, f"h{i}")
                    ps = ps_of(f"h{i}")[0:TT, :]
                    V.scalar_tensor_tensor(ps, bias[0:TT, :], degs[0:TT, i:i + 1], ps, ALU.mult, ALU.add).then_inc(done["t_ready"], 1)
                if i:
                    after("h1h_ready", i)
                    V.scalar_tensor_tensor(H1L[0:TT, i - 1, :], ps_of(f"h{i - 1}")[0:TT, :], 0.0, H1H[0:TT, i - 1, :].bitcast(F32),
                                           ALU.max, ALU.subtract).then_inc(done["h1l_ready"], 1)
            aggregate(2)
            dve.wait_ge(loads["b2"], 16)

            def layernorm_of(p):
                after("sqrt2_ready", p + 1)
                inverse_root(slice(2 * p, 2 * p + 2))
                for i in (2 * p, 2 * p + 1):
                    V.tensor_scalar(Y[0:TT, i, :], X[0:TT, i, :], mv[0:TT, i, 0:1], rstd[0:TT, 2, i:i + 1],
                                    ALU.subtract, ALU.mult).then_inc(done["y_ready"], 1)

            for i in range(NT):
                reads(dve, f"o{i}")
                ps = ps_of(f"o{i}")[0:TT, :]
                link(V.scalar_tensor_tensor(ps, bias[0:TT, :], degs[0:TT, i:i + 1], ps, ALU.mult, ALU.add))
                V.scalar_tensor_tensor(X[0:TT, i, :], ps, 0.0, X[0:TT, i, :], ALU.max, ALU.add).then_inc(done["x_final"], 1)
                after("x_final", i + 1)
                link(V.bn_stats(stat[0:TT, i, :], X[0:TT, i, :]))
                link(V.bn_aggr(mv[0:TT, i, :], stat[0:TT, i, :]))
                if i % 2 == 1:
                    variance(slice(i - 1, i + 1), "var2_ready")
                elif i >= 2:
                    layernorm_of(i // 2 - 1)
            layernorm_of(NT // 2 - 1)

            after("rconsts", 1)
            for r, s in enumerate(SHIFTS):
                V.tensor_scalar(ctab[:, r:r + 1], cb[:, 0:1], 15 if s else 7, s, ALU.bitwise_and, ALU.logical_shift_left)
            V.memset(pre[:, 0:1], 0)
            reads(dve, "logits")
            link(V.tensor_scalar(P8[t], ps_of("logits")[t, 0:NT * NE].rearrange("p (i e) -> p i e", e=NE), CLIP_EPS, None, ALU.max))
            for r in range(SINKHORN):
                V.tensor_reduce(s8[t, 0, :], P8[t].rearrange("p i e -> p e i"), AX, ALU.add).then_inc(done["p_ready"], 1)
                reads(dve, f"sink{r}")
                link(V.reciprocal(s8[t, 1, :], ps_of(f"sink{r}")[t, 0:NE]))
                link(V.tensor_tensor(P8[t], P8[t], s8[t, 1:2, :].broadcast_to([TT, NT, NE]), ALU.mult))
                link(V.tensor_reduce(s10[t, 0, :], P8[t], AX, ALU.add))
                link(V.reciprocal(s10[t, 1, :], s10[t, 0, :]))
                link(V.tensor_tensor(P8[t], P8[t], s10[t, 1, :].unsqueeze(2).broadcast_to([TT, NT, NE]), ALU.mult))
            V.tensor_copy(GREP[t].rearrange("p i (e c) -> p (i e) c", c=16),
                          P8[t].rearrange("p i e -> p (i e)").unsqueeze(2).broadcast_to([TT, NT * NE, 16])).then_inc(done["grep_ready"], 1)

            after("gt_ready", 3)
            for r, s in enumerate(SHIFTS):
                link(V.tensor_tensor(pre[:, 1:2], pre[:, 0:1], ctab[:, r:r + 1], ALU.bitwise_or))
                link(V.tensor_scalar(M_GT[:], GT[:], pre[:, 1:2].bitcast(F32), None, ALU.is_ge, ALU.add, accum_out=cnt[:, 0:1]))
                V.tensor_scalar(cnt[:, 1:2], cnt[:, 0:1], float(TOPK), None, ALU.is_ge).then_inc(done["ind_ready"], 1)
                reads(dve, f"rad{r}")
                twice = 1 if s else 2
                link(V.tensor_scalar(pre[:, 2:3], ps_of(f"rad{r}")[:, 0:1], float(2 ** s) / twice, -float(2 ** s), ALU.mult, ALU.add))
                V.tensor_tensor(pre[:, 0:1], pre[:, 0:1], pre[:, 2:3], ALU.bitwise_or).then_inc(done["prefix_ready"], 1)
                after("prefix_ready", r + 1)
            kth = pre[:, 0:1].bitcast(F32)
            V.tensor_scalar(M_GT[:], GT[:], kth, None, ALU.is_gt, ALU.add, accum_out=cnt[:, 2:3])
            link(V.tensor_scalar(M_EQ[:], GT[:], kth, None, ALU.is_equal))
            V.tensor_scalar(cnt[:, 3:4], cnt[:, 2:3], -1.0, float(TOPK), ALU.mult, ALU.add)
            link(V.tensor_tensor_scan(RANK[:], M_EQ[:], M_EQ[:], 0.0, ALU.add, ALU.max))
            link(V.scalar_tensor_tensor(M_TIE[:], RANK[:], cnt[:, 3:4], M_EQ[:], ALU.is_le, ALU.mult))
            V.tensor_tensor(M_SEL[:], M_GT[:], M_TIE[:], ALU.add).then_inc(done["msel_ready"], 1)

            V.tensor_scalar(tid[t, 1, :], tid[t, 0, :], 31, None, ALU.bitwise_and)
            reads(dve, "sel")
            link(V.tensor_tensor(w8[t, 0].rearrange("p e i -> p (e i)"), ps_of("sel")[t, 0:NT * NE],
                                 e1[t].rearrange("p i e -> p (i e)"), ALU.mult))
            taken = w8[t, 0].rearrange("p e i -> p (e i)").rearrange("p (i e) -> p i e", e=NE)
            link(V.tensor_reduce(s10[t, 0, :], taken, AX, ALU.max))
            last = w8[t, 1].rearrange("p e i -> p (e i)").rearrange("p (i e) -> p i e", e=NE)
            link(V.tensor_tensor(last, taken, s10[t, 0, :].unsqueeze(2).broadcast_to([TT, NT, NE]), ALU.is_equal))
            by_token = fin[t].rearrange("p e i -> p i e")
            link(V.scalar_tensor_tensor(by_token, taken, 0.0, last, ALU.is_gt, ALU.mult))
            link(V.tensor_tensor_scan(incl[t].rearrange("p e i -> p (e i)"), reset[t].rearrange("p e i -> p (e i)"),
                                      fin[t].rearrange("p e i -> p (e i)"), 0.0, ALU.mult, ALU.add))
            V.tensor_copy(s8[t, 1, :], incl[t, :, NT - 1]).then_inc(done["rowtot_ready"], 1)
            V.tensor_tensor(w8[t, 0], fin[t], P8[t].rearrange("p i e -> p e i"), ALU.mult)
            V.tensor_copy(vals[t, :, 1], tid[t, 1, :])
            link(V.tensor_tensor(vals[t, :, 0], tid[t, 0, :], tid[t, 1, :], ALU.subtract))
            link(V.tensor_reduce(s10[t, 1, :], w8[t, 0].rearrange("p e i -> p i e"), AX, ALU.add))
            link(V.tensor_copy(vals[t, :, 2], s10[t, 1, :]))
            link(V.tensor_tensor(s10[t, 2, :], s10[t, 1, :], vals[t, :, 2], ALU.subtract))
            link(V.tensor_copy(vals[t, :, 3], s10[t, 2, :]))
            V.tensor_tensor(vals[t, :, 4], s10[t, 2, :], vals[t, :, 3], ALU.subtract)
            V.memset(vals[t, :, 5], 0.0)
            reads(dve, "off")
            link(V.tensor_tensor(w8[t, 0], incl[t], ps_of("off")[t, 0:NE].unsqueeze(2).broadcast_to([TT, NE, NT]), ALU.add))
            link(V.tensor_tensor(w8[t, 1], w8[t, 0], e156[t].unsqueeze(2).broadcast_to([TT, NE, NT]), ALU.add))
            link(V.tensor_tensor(w8[t, 0], w8[t, 1], fin[t], ALU.mult))
            link(V.tensor_reduce(s10[t, 3, :], w8[t, 0].rearrange("p e i -> p i e"), AX, ALU.add))
            link(V.tensor_scalar(slot[t, :], s10[t, 3, :], -1.0, None, ALU.add))
            for i in range(NT):
                V.tensor_scalar(ROUTE[t, i, :], iota[t, 0:NS * SLOT], slot[t, i:i + 1], None, ALU.is_equal).then_inc(done["route_ready"], 1)
            reads(dve, "slots")
            u = slice(0, SLOT)
            ps = ps_of("slots")[u, 0:6 * NS].rearrange("p (j c) -> p j c", c=6)
            V.tensor_reduce(tokv[u, 1, :], ps[:, :, 2:5], AX, ALU.add)
            link(V.tensor_reduce(tokv[u, 0, :], ps[:, :, 0:2], AX, ALU.add))
            V.tensor_scalar(idx[u, 0, :], tokv[u, 0, :], -1.0, 0.0, ALU.add, ALU.max)
            link(V.tensor_scalar(tokv[u, 2, :], tokv[u, 0, :], 0.0, 8192.0, ALU.is_equal, ALU.mult))
            V.scalar_tensor_tensor(idx[u, 1, :], tokv[u, 0, :], -1.0, tokv[u, 2, :], ALU.add, ALU.add).then_inc(done["idx_ready"], 1)

            after("idx_ready", 1)
            for j in range(NS + 1):
                if j < NS:
                    after("fth_ready", j + 1)
                    V.tensor_tensor(FTL[:, j % 2, :, 0:SLOT], view(f"ft{j}")[:, :, 0:SLOT], FTH[:, j % 2, :, 0:SLOT].bitcast(F32),
                                    ALU.subtract).then_inc(done["ftl_ready"], 1)
                if j:
                    n = j - 1
                    reads(dve, f"fo{n}")
                    dve.wait_ge(gathered[n], 16)
                    if n >= 4:
                        dve.wait_ge(scattered[n % 4], 16 * (n // 4))
                    V.scalar_tensor_tensor(FO[u, n % 4, :], ps_of(f"fo{n}")[u, :], tokv[u, 1, n:n + 1], YX[u, n % 12, 1, :],
                                           ALU.mult, ALU.add).then_inc(done["fo_ready"], 1)
                    if j % 2 == 0 and 3 <= j // 2 + 1 < NE:
                        e = j // 2 + 1
                        after("w_hi", NW + e + 1)
                        V.tensor_tensor(WEL[e % 3][:], RAW_E[:], WEH[e % 3][:].bitcast(F32), ALU.subtract).then_inc(done["el_split"], 1)


_OUT = ((N, D), "float32")


def kernel(**inputs):
    import numpy as _np
    import concourse.bacc as _bacc
    from concourse import mybir as _mybir
    from concourse.bass_utils import run_bass_kernel_spmd as _run

    def tr(name):
        return _np.ascontiguousarray(_np.asarray(inputs[name]).T)

    def edges(name):
        return _np.ascontiguousarray(_np.asarray(inputs[name]).reshape(NE_T, ET).T)

    host = {
        "x": _np.asarray(inputs["x"]), "src_t": edges("src"), "dst_t": edges("dst"),
        "dst_rows": _np.asarray(inputs["dst"]).reshape(NE_T // 2, 2, ET),
        "gW1T": tr("L0_gnn_W1"), "gb1": _np.asarray(inputs["L0_gnn_b1"]),
        "gW2T": tr("L0_gnn_W2"), "gb2": _np.asarray(inputs["L0_gnn_b2"]),
        "WqT": tr("L0_mix_Wq"), "WkT": tr("L0_mix_Wk"), "Wv": _np.asarray(inputs["L0_mix_Wv"]),
        "mW1": _np.asarray(inputs["L0_mix_W1"]), "mW2T": tr("L0_mix_W2"),
        "gate": _np.asarray(inputs["L0_ffn_gate_weight"]), "experts": _np.asarray(inputs["L0_ffn_experts"]),
    }
    nc = _bacc.Bacc("TRN2", target_bir_lowering=False, num_devices=1)
    arrays, args = {}, []
    for name, a in host.items():
        a = _np.ascontiguousarray(a)
        arrays[f"in_{name}"] = a
        args.append(nc.dram_tensor(f"in_{name}", a.shape, _mybir.dt.from_np(a.dtype), kind="ExternalInput").ap())
    out = nc.dram_tensor("out_x", _OUT[0], _mybir.dt.float32, kind="ExternalOutput").ap()
    gps_block(nc, *args, out)
    r = _run(nc, [arrays], core_ids=[0])
    return r.results[0]["out_x"]
```

```python
from contextlib import ExitStack

import numpy as np

import concourse.bass as bass
from concourse import mybir

ALU = mybir.AluOpType
ACT = mybir.ActivationFunctionType
F32 = mybir.dt.float32
F32R = mybir.dt.float32r
BF16 = mybir.dt.bfloat16
F16 = mybir.dt.float16
I32 = mybir.dt.int32
U32 = mybir.dt.uint32
I8 = mybir.dt.int8
AX = mybir.AxisListType.X

N, D, E = 1250, 512, 20000
NE, TOPK = 8, 1250 // 8
TT = 125
NT = N // TT
C = D // 128
ET = 125
NE_T = E // ET
UN = 3
DB = 98
NB = -(-N // DB)
NPAD = NB * DB
SPANS = [(0, 4), (4, 8), (8, NB)]
PARTS = [(0, 2), (2, 6), (6, NT)]
EXACT = 4096.0
LN_EPS, CLIP_EPS, SINKHORN = 1e-5, 1e-6, 8
YP = 4
SLOT = TOPK // 2
NS = NE * 2
SHIFTS = [27, 23, 19, 15, 11, 7, 3, 0]
KB = 1024
BEHIND = ([[("context", 2 * b), ("context", 2 * b + 1)] for b in range(5)]
          + [[], [("values", 0)]]
          + [[("attend", i) for i in part] for part in ((0, 1), (2, 3), (4, 5), (6, 7), (8,), (9,))])


def psum_plan():
    uses, filled, readers, turn = {}, [0] * 8, [[] for _ in range(8)], {}

    def use(name, banks, *read_by):
        k = turn.get(banks, 0)
        turn[banks] = k + 1
        b = banks[k % len(banks)]
        uses[name] = (b, filled[b] + 1, readers[b])
        filled[b] += 1
        readers[b] = list(read_by)

    low, high = (0, 1, 2, 3), (4, 5, 6, 7)
    every = {1: (0, 1, 2, 3, 6, 7, 4, 5), 2: high + low}

    def turned(i):
        if i < NT:
            use(f"xt{i}", high, ("xth_ready", i + 1), ("xtl_ready", i + 1))

    turned(0)
    turned(1)
    for i in range(NT):
        if i == 4:
            use("bounds", (7,), ("blen_ready", 1))
        if i == 7:
            use("bases", (6,), ("tab_ready", 1))
        use(f"k{i}", low, ("k_stored", i + 1), ("kmax_step", i + 1))
        turned(i + 2)
    for i in range(NT):
        if i == 4:
            use("kmt", (4,), ("diag_ready", 1))
        if i == 7:
            use("kmb", (4,), ("k_shift", NT))
        use(f"q{i}", (5, 6, 7), ("rmax_ready", i + 1), ("q_exp", i + 1))
    for c in range(C):
        use(f"mp{c}", low, ("mph_ready", c + 1), ("mpl_ready", c + 1))
    for i in range(NT):
        use(f"xm{i}", low, ("xm_added", i + 1))
    for c in range(C):
        use(f"vp{c}", (7, 6, 5), ("vph_ready", c + 1), ("vpl_ready", c + 1))
    for c in range(C):
        use(f"tt{c}", low, ("th_ready", c + 1), ("tl_ready", c + 1))
    for b in high:
        uses[f"adj{b}"] = (b, None, readers[b])
        readers[b] = [("adj_hi", NB), ("adj_lo", NB)]
    use("ks", (0,), ("krs_ready", 1))
    for c in range(C):
        use(f"cp{c}", (1, 2, 3), ("cph_ready", c + 1), ("cpl_ready", c + 1))
    for i in range(NT):
        use(f"qt{i}", (0, 1), ("qth_ready", i + 1), ("qtl_ready", i + 1))
        use(f"qp{i}", (2, 3), ("qp_added", i + 1))
    for layer in (1, 2):
        for ch in range(3):
            for f in range(C):
                n = ((layer - 1) * 3 + ch) * C + f + 1
                use(f"z{layer}_{ch}_{f}", every[layer], ("zh_ready", n), ("zl_ready", n))
            if layer == 1:
                use(f"deg{ch}", every[layer], ("degrow_ready", ch + 1))
                if ch == 0:
                    use("flag", (7,), ("flag_ready", 1))
        if layer == 1:
            use("degt", (7,), ("deg_ready", 1))
            for i in range(NT):
                use(f"h{i}", low, ("h1h_ready", i + 1), ("h1l_ready", i + 1))
    for i in range(NT):
        use(f"o{i}", (3, 0, 1, 2), ("x_final", i + 1))
        use(f"yt{i}", (4, 5, 6), ("yt_ready", i + 1))
    use("logits", (7,), ("p_ready", 1))
    for r in range(SINKHORN):
        use(f"sink{r}", (3, 0), *([("p_ready", r + 2)] if r + 1 < SINKHORN else [("grep_ready", 1)]))
    for h in range(3):
        use(f"gt{h}", (1, 2, 3), ("gt_ready", h + 1))
    for r in range(len(SHIFTS)):
        use(f"rad{r}", (0,), ("prefix_ready", r + 1))
    use("sel", (1,), ("rowtot_ready", 1))
    use("off", (2,), ("route_ready", 1))
    use("slots", (3,), ("idx_ready", 1))
    for j in range(NS):
        use(f"ft{j}", (0, 1), ("fth_ready", j + 1), ("ftl_ready", j + 1))
        use(f"fo{j}", (2, 3), ("fo_ready", j + 1))
    return uses


def gps_block(nc, x_in, src_t, dst_t, dst_in, gW1T, gb1, gW2T, gb2, WqT, WkT, Wv, mW1, mW2T,
              gate_w, experts, out):
    plan = psum_plan()
    scratch = nc.dram_tensor("scratch", [N, 2 * D], F32).ap()

    with ExitStack() as ctx:
        base = nc.sbuf_base + (-nc.sbuf_base) % 32

        def at(name, shape, dt, off):
            return nc.alloc_sbuf_tensor_at(name, shape, dt, offset=base + int(off))

        areas = {"a": [int(162.5 * KB), 168 * KB], "b": [204 * KB, int(207.8 * KB)],
                 "c": [148 * KB, 160 * KB]}

        def small(name, shape, dt, area):
            size = int(np.prod(shape[1:])) * mybir.dt.size(dt)
            off = areas[area][0]
            areas[area][0] += size + (-size) % 32
            assert areas[area][0] <= areas[area][1], (name, areas[area])
            return at(name, shape, dt, off)

        def sem(name):
            return ctx.enter_context(nc.semaphore(name))

        X = at("X", [128, NT, D], F32, 0)
        XNH = at("XNH", [128, NT, D], F32R, 20 * KB)
        XNL = at("XNL", [128, NT, D], F32R, 40 * KB)
        H1H = at("H1H", [128, NT, D], F32R, 20 * KB)
        H1L = at("H1L", [128, NT, D], F32R, 40 * KB)
        XTH = at("XTH", [128, C, N], F32R, 60 * KB)
        XTL = at("XTL", [128, C, N], F32R, 80 * KB)
        EH = at("EH", [128, 4, D], F32R, 60 * KB)
        EL = at("EL", [128, 4, D], F32R, 68 * KB)
        TH = at("TH", [128, C, D], F32R, 60 * KB)
        TL = at("TL", [128, C, D], F32R, 68 * KB)
        QTH = at("QTH", [128, 2, C, TT + 3], F32R, 60 * KB)
        QTL = at("QTL", [128, 2, C, TT + 3], F32R, 64 * KB)
        VPH = at("VPH", [128, C, D], F32R, 76 * KB)
        VPL = at("VPL", [128, C, D], F32R, 84 * KB)
        HOT_S = at("HOT_S", [128, UN, N], BF16, 92 * KB)
        HOT_D = at("HOT_D", [128, UN, DB], BF16, 99.375 * KB)
        ZH = at("ZH", [128, C, N], F32R, 60 * KB)
        ZL = at("ZL", [128, C, N], F32R, 80 * KB)
        WKH = at("WKH", [128, C, D], F32R, 100 * KB)
        WKL = at("WKL", [128, C, D], F32R, 108 * KB)
        W1H = at("W1H", [128, C, D], F32R, 100 * KB)
        W1L = at("W1L", [128, C, D], F32R, 108 * KB)
        WVH = at("WVH", [128, C, D], F32R, 100 * KB)
        WVL = at("WVL", [128, C, D], F32R, 108 * KB)
        WQH = at("WQH", [128, C, D], F32R, 116 * KB)
        WQL = at("WQL", [128, C, D], F32R, 124 * KB)
        MPH = at("MPH", [128, C, D], F32R, 116 * KB)
        MPL = at("MPL", [128, C, D], F32R, 124 * KB)
        XF = at("XF", [128, NT, D], F32, 132 * KB)
        K = at("K", [128, NT, D], F32, 132 * KB)
        RAW_C = at("RAW_C", [128, C, D], F32, 152 * KB)
        AT = at("AT", [128, NB, NT, DB], F32R, 100 * KB)
        AL = at("AL", [128, NB, NT, DB], I8, 150 * KB)
        RAW_A = at("RAW_A", [128, C, D], F32, 168 * KB)
        RAW_B = at("RAW_B", [128, C, D], F32, 176 * KB)
        KMAX = at("KMAX", [128, D], F32, 186 * KB)
        Q = at("Q", [128, NT, D], F32, 168 * KB)
        W2H = at("W2H", [128, C, D], F32R, 188 * KB)
        W2L = at("W2L", [128, C, D], F32R, 196 * KB)
        CPH = at("CPH", [128, C, D], F32R, 188 * KB)
        CPL = at("CPL", [128, C, D], F32R, 196 * KB)
        DROW = at("DROW", [128, 2, ET], I32, 188 * KB)
        EDGE = at("EDGE", [128, 2, NE_T], I32, 189 * KB)
        grp = at("grp", [128, 2, 2], F32, 191 * KB)
        blk = at("blk", [128, 2], F32, 191 * KB + 32)
        blh = at("blh", [128, 7], F32, 191 * KB + 64)
        dg2 = at("dg2", [128, 2, NE_T], F32, 192 * KB)
        gio = at("gio", [128, 3, NE_T], F32, 194 * KB)
        bw = at("bw", [128, 4, NE_T], F32, 196 * KB)
        G1H = at("G1H", [128, C, D], F32R, 168 * KB)
        G1L = at("G1L", [128, C, D], F32R, 176 * KB)
        AC = at("AC", [128, 2, 5, DB], F32R, 184 * KB)
        G2H = at("G2H", [128, C, D], F32R, 188 * KB)
        G2L = at("G2L", [128, C, D], F32R, 196 * KB)
        RAW_G1 = at("RAW_G1", [128, C, D], F32, 188 * KB)
        drow = at("drow", [128, N], F32, 196 * KB)
        RAW_G2 = at("RAW_G2", [128, C, D], F32, 168 * KB)
        Y = at("Y", [128, NT, D], F32, 100 * KB)
        YT = at("YT", [128, 2, C, TT + 3], F32, 144 * KB)
        YX = at("YX", [128, 12, 2, D], F32, 60 * KB)
        FTH = at("FTH", [128, 2, C, SLOT + 2], F32R, 112 * KB)
        FTL = at("FTL", [128, 2, C, SLOT + 2], F32R, 115 * KB)
        FO = at("FO", [128, 4, D], F32, 52 * KB)
        WEH = [at(f"WEH{s}", [128, C, D], F32R, o * KB) for s, o in enumerate((20, 36, 120, 0))]
        WEL = [at(f"WEL{s}", [128, C, D], F32R, (o + 8) * KB) for s, o in enumerate((20, 36, 120, 0))]
        RAW_E = [at(f"RAW_E{s}", [128, C, D], F32, o * KB) for s, o in enumerate((136, 196))]
        GREP = at("GREP", [128, NT, 128], F32, 168 * KB)
        GT = at("GT", [128, N], F32, 173 * KB)
        RANK = at("RANK", [128, N], F32, 178 * KB)
        M_GT = at("M_GT", [128, N], BF16, 183 * KB)
        M_EQ = at("M_EQ", [128, N], BF16, 185.5 * KB)
        M_TIE = at("M_TIE", [128, N], BF16, 188 * KB)
        M_SEL = at("M_SEL", [128, N], BF16, 190.5 * KB)
        ROUTE = at("ROUTE", [128, NT, NS * SLOT], BF16, 168 * KB)

        ident = small("ident", [128, 128], F32, "a")
        ones = small("ones", [128, 128], F32, "a")
        tri = small("tri", [128, 128], F32, "a")
        iota = small("iota", [128, NPAD], F16, "a")
        srcf = small("srcf", [128, NE_T + UN], F32, "a")
        dstf = small("dstf", [128, NE_T + UN], F32, "a")
        diag = small("diag", [128, C, 128], F32, "b")
        ESUM = at("ESUM", [128, D], F32, 204 * KB)
        bias = at("bias", [128, D], F32, 204 * KB)
        stat = small("stat", [128, NT, 6], F32, "b")
        mv = small("mv", [128, NT, 2], F32, "b")
        rstd = small("rstd", [128, 4, NT], F32, "b")
        rmax = small("rmax", [128, NT], F32, "b")
        rsum = small("rsum", [128, 2, NT], F32, "b")
        kmt = small("kmt", [128, C], F32, "b")
        krs = small("krs", [128, 2, C], F32, "b")
        degs = small("degs", [128, NT], F32, "b")
        onesr = small("onesr", [128, 2], F32R, "b")
        odeg = small("odeg", [128, 2, NB], F32, "b")
        many = small("many", [128, 2], F32, "b")
        flag = small("flag", [128, 1], I32, "b")
        tab = small("tab", [128, 2, NB + 2], I32, "b")
        zero = small("zero", [128, TT + 3], BF16, "b")
        gw = small("gw", [128, C, NE], F32, "c")
        P8 = small("P8", [128, NT, NE], F32, "c")
        s8 = small("s8", [128, 2, NE], F32, "c")
        s10 = small("s10", [128, 4, NT], F32, "c")
        pick = small("pick", [128, NE], BF16, "c")
        blkones = small("blkones", [128, 128], BF16, "c")
        ctab = small("ctab", [128, len(SHIFTS)], I32, "c")
        cb = small("cb", [128, 2], I32, "c")
        pre = small("pre", [128, 4], I32, "c")
        cnt = small("cnt", [128, 4], F32, "c")
        reached = small("reached", [128, 2], BF16, "c")
        e1 = small("e1", [128, NT, NE], F32, "c")
        e156 = small("e156", [128, NE], F32, "c")
        fin = small("fin", [128, NE, NT], F32, "c")
        incl = small("incl", [128, NE, NT], F32, "c")
        reset = small("reset", [128, NE, NT], F32, "c")
        w8 = small("w8", [128, 2, NE, NT], F32, "c")
        tid = small("tid", [128, 2, NT], I32, "c")
        vals = small("vals", [128, NT, 6], BF16, "c")
        slot = small("slot", [128, NT], F32, "c")
        tokv = small("tokv", [128, 3, NS], F32, "c")
        idx = small("idx", [128, 2, NS], I32, "c")

        PS = [ctx.enter_context(nc.psum_tensor(f"ps{b}", [128, 512], F32)) for b in range(8)]

        def view(name, chunks=C):
            return PS[plan[name][0]].rearrange("p (c t) -> p c t", c=chunks)

        full = [sem(f"bank_full{b}") for b in range(8)]
        ld_x = [sem(f"ld_x{n}") for n in range(5)]
        loads = {n: sem(f"ld_{n}") for n in ("edges", "w1", "w2", "wk", "wq", "wv", "b1", "b2", "g1",
                                             "g2", "gate", "exp0", "exp1")}
        done = {n: sem(n) for n in (
            "consts rconsts w_hi w_lo el_split dve_chain pool_chain var_ready sqrt_ready xf_ready xnh_ready "
            "xnl_ready xth_ready xtl_ready grp_ready blen_ready tab_ready mph_ready mpl_ready "
            "k_stored kmax_step diag_ready rmax_ready q_exp q_ready k_shift k_exp eh_ready el_ready "
            "esum_ready krs_ready e_used xm_added vph_ready vpl_ready th_ready tl_ready cph_ready "
            "cpl_ready zero_ready adj_full adj_hi adj_lo qth_ready qtl_ready qp_added flag_in "
            "flag_ready zh_ready zl_ready ac_ready ac_used degrow_ready deg_ready t_ready h1h_ready "
            "h1l_ready x_final inv_ready inv2_ready y_ready ylast_ready var2_ready sqrt2_ready yt_ready yt_used p_ready grep_ready "
            "gt_ready ind_ready prefix_ready msel_ready rowtot_ready route_ready idx_ready st_scratch "
            "st_out fth_ready ftl_ready fo_ready").split()}
        gathered = [sem(f"gathered{j}") for j in range(NS)]
        scattered = [sem(f"scattered{s}") for s in range(4)]
        hot = [sem(f"hot{s}") for s in range(UN)]
        hot_used = [sem(f"hot_used{s}") for s in range(UN)]

        splits = [(RAW_A, WKH, WKL, "wk"), (RAW_B, WQH, WQL, "wq"), (RAW_C, W2H, W2L, "w2"),
                  (RAW_C, W1H, W1L, "w1"), (RAW_C, WVH, WVL, "wv"), (RAW_G1, G1H, G1L, "g1"),
                  (RAW_G2, G2H, G2L, "g2")]
        NW = len(splits)
        order = {s[3]: n + 1 for n, s in enumerate(splits)}

        def reads(eng, name):
            eng.wait_ge(full[plan[name][0]], plan[name][1])

        def reads_y(eng, i):
            if i < YP:
                eng.wait_ge(done["y_ready"], i + 1)
            else:
                eng.wait_ge(done["ylast_ready"], i - YP + 1)

        block = ctx.enter_context(nc.Block())

        @block.sync
        def _(sp):
            def rows(w):
                return w.rearrange("(c p) f -> p c f", p=128)

            def tiles(a, i, n=1):
                return a[TT * i:TT * (i + n), :].rearrange("(i p) f -> p i f", p=TT)

            for n in range(5):
                sp.dma_start(X[0:TT, 2 * n:2 * n + 2, :], tiles(x_in, 2 * n, 2)).then_inc(ld_x[n], 16)
                if n == 0:
                    sp.dma_start(RAW_A[:], rows(WkT)).then_inc(loads["wk"], 16)
            sp.dma_start(DROW[0:NE_T // 2], dst_in).then_inc(loads["edges"], 16)
            sp.dma_start(EDGE[0:ET, 0, :], src_t).then_inc(loads["edges"], 16)
            sp.dma_start(EDGE[0:ET, 1, :], dst_t).then_inc(loads["edges"], 16)
            sp.dma_start(RAW_B[:], rows(WqT)).then_inc(loads["wq"], 16)
            sp.dma_start(RAW_C[:], rows(mW2T)).then_inc(loads["w2"], 16)
            for last, name, w in (("w2", "w1", mW1), ("w1", "wv", Wv)):
                sp.wait_ge(done["w_hi"], order[last])
                sp.wait_ge(done["w_lo"], order[last])
                sp.dma_start(RAW_C[:], rows(w)).then_inc(loads[name], 16)
            sp.wait_ge(done["qp_added"], NT)
            sp.dma_start(RAW_G1[:], rows(gW1T)).then_inc(loads["g1"], 16)
            sp.dma_start(bias[0:TT, :], gb1.rearrange("(a f) -> a f", a=1).broadcast_to([TT, D])).then_inc(loads["b1"], 16)
            reads(sp, f"h{NT - 1}")
            sp.dma_start(RAW_G2[:], rows(gW2T)).then_inc(loads["g2"], 16)
            sp.wait_ge(done["t_ready"], NT)
            sp.dma_start(bias[0:TT, :], gb2.rearrange("(a f) -> a f", a=1).broadcast_to([TT, D])).then_inc(loads["b2"], 16)
            reads(sp, f"z2_2_{C - 1}")
            sp.dma_start(gw[:], rows(gate_w[0])).then_inc(loads["gate"], 16)
            sp.dma_start(RAW_E[0][:], rows(experts[0])).then_inc(loads["exp0"], 16)
            for i in range(NT):
                sp.wait_ge(done["x_final"], i + 1)
                sp.dma_start(tiles(out, i), X[0:TT, i:i + 1, :]).then_inc(done["st_out"], 16)
                sp.dma_start(tiles(scratch, i)[:, :, D:2 * D], X[0:TT, i:i + 1, :]).then_inc(done["st_scratch"], 16)
                if i >= 3:
                    reads_y(sp, i - 3)
                    sp.dma_start(tiles(scratch, i - 3)[:, :, 0:D], Y[0:TT, i - 3:i - 2, :]).then_inc(done["st_scratch"], 16)
            for i in range(NT - 3, NT):
                reads_y(sp, i)
                sp.dma_start(tiles(scratch, i)[:, :, 0:D], Y[0:TT, i:i + 1, :]).then_inc(done["st_scratch"], 16)
            for e in range(1, NE):
                if e >= 2:
                    sp.wait_ge(done["w_hi"], NW + e - 1)
                    if e - 2 < 4:
                        sp.wait_ge(done["w_lo"], NW + e - 1)
                    else:
                        sp.wait_ge(done["el_split"], e - 5)
                sp.dma_start(RAW_E[e % 2][:], rows(experts[e])).then_inc(loads[f"exp{e % 2}"], 16)
            sp.wait_ge(done["st_out"], 16 * NT)
            for s in range(4):
                sp.wait_ge(scattered[s], 16 * (NS // 4))

        @block.gpsimd
        def _(pool):
            count = [0]

            def link(ins):
                count[0] += 1
                ins.then_inc(done["pool_chain"], 1)
                pool.wait_ge(done["pool_chain"], count[0])

            link(nc.gpsimd.memset(ones[:], 1.0))
            link(nc.gpsimd.affine_select(out=ident[:], in_=ones[:], pattern=[[-1, 128]], compare_op=ALU.is_equal,
                                         fill=0.0, base=0, channel_multiplier=1))
            link(nc.gpsimd.affine_select(out=tri[:], in_=ones[:], pattern=[[1, 128]], compare_op=ALU.is_gt,
                                         fill=0.0, base=0, channel_multiplier=-1))
            for n, (step, base) in enumerate(((1, 1), (-1, NE_T))):
                link(nc.gpsimd.iota(gio[:, n, :].rearrange("p (h g) -> p h g", h=2), [[step, 2], [2 * step, NE_T // 2]],
                                    base=base, channel_multiplier=0, allow_small_or_imprecise_dtypes=True))
            link(nc.gpsimd.iota(gio[:, 2, :], [[UN, NE_T]], base=0, channel_multiplier=0,
                                allow_small_or_imprecise_dtypes=True))
            link(nc.gpsimd.iota(blk[:, 0:1], [[0, 1]], base=0, channel_multiplier=DB,
                                allow_small_or_imprecise_dtypes=True))
            link(nc.gpsimd.iota(blk[:, 1:2], [[0, 1]], base=DB - 1, channel_multiplier=DB,
                                allow_small_or_imprecise_dtypes=True))
            nc.gpsimd.iota(iota[:], [[1, NPAD]], base=0, channel_multiplier=0,
                           allow_small_or_imprecise_dtypes=True).then_inc(done["consts"], 1)

            def split_lo(n, raw, hi, lo):
                pool.wait_ge(done["w_hi"], n)
                nc.gpsimd.tensor_tensor(lo[:], raw[:], hi[:].bitcast(F32), ALU.subtract).then_inc(done["w_lo"], 1)

            for i in range(NT):
                if i == 0:
                    split_lo(order["wk"], *splits[0][:3])
                if i == 6:
                    split_lo(order["wq"], *splits[1][:3])
                pool.wait_ge(done["xnh_ready"], i + 1)
                nc.gpsimd.tensor_tensor(XNL[0:TT, i, :], XF[0:TT, i, :], XNH[0:TT, i, :].bitcast(F32),
                                        ALU.subtract).then_inc(done["xnl_ready"], 1)
            for n in (order["w2"], order["w1"], order["wv"]):
                split_lo(n, *splits[n - 1][:3])

            def add_exp(i):
                pool.wait_ge(done["k_exp"], i + 1)
                if i == 0:
                    link(nc.gpsimd.tensor_copy(ESUM[0:TT, :], K[0:TT, 0, :]))
                elif i < NT - 1:
                    link(nc.gpsimd.tensor_tensor(ESUM[0:TT, :], ESUM[0:TT, :], K[0:TT, i, :], ALU.add))
                else:
                    nc.gpsimd.tensor_tensor(ESUM[0:TT, :], ESUM[0:TT, :], K[0:TT, i, :],
                                            ALU.add).then_inc(done["esum_ready"], 1)

            for i in range(NT):
                add_exp(i)
            split_lo(6, *splits[5][:3])
            split_lo(7, *splits[6][:3])

            reads(pool, f"z2_2_{C - 1}")
            link(nc.gpsimd.affine_select(out=blkones[:].rearrange("p (e c) -> p e c", c=16),
                                         in_=ones[:].rearrange("p (e c) -> p e c", c=16),
                                         pattern=[[-16, NE], [0, 16]], compare_op=ALU.is_ge, fill=0.0,
                                         base=0, channel_multiplier=1))
            link(nc.gpsimd.affine_select(out=blkones[:].rearrange("p (e c) -> p e c", c=16),
                                         in_=blkones[:].rearrange("p (e c) -> p e c", c=16),
                                         pattern=[[16, NE], [0, 16]], compare_op=ALU.is_ge, fill=0.0,
                                         base=15, channel_multiplier=-1))
            link(nc.gpsimd.affine_select(out=pick[:], in_=ones[:, 0:NE], pattern=[[-16, NE]],
                                         compare_op=ALU.is_equal, fill=0.0, base=0, channel_multiplier=1))
            link(nc.gpsimd.iota(cb[:, 0:1], [[0, 1]], base=0, channel_multiplier=1))
            link(nc.gpsimd.iota(e1[:], [[0, NT], [1, NE]], base=1, channel_multiplier=0,
                                allow_small_or_imprecise_dtypes=True))
            link(nc.gpsimd.iota(e156[:], [[TOPK, NE]], base=0, channel_multiplier=0,
                                allow_small_or_imprecise_dtypes=True))
            link(nc.gpsimd.memset(reset[:], 1.0))
            link(nc.gpsimd.memset(reset[:, :, 0:1], 0.0))
            nc.gpsimd.iota(tid[:, 0, :], [[TT, NT]], base=1, channel_multiplier=1).then_inc(done["rconsts"], 1)

            for e in range(4):
                split_lo(NW + e + 1, RAW_E[e % 2], WEH[e], WEL[e])
                if e == 0:
                    for i in range(YP):
                        pool.wait_ge(done["inv2_ready"], i // 2 + 1)
                        nc.gpsimd.tensor_scalar(Y[0:TT, i, :], X[0:TT, i, :], mv[0:TT, i, 0:1], rstd[0:TT, 2, i:i + 1],
                                                ALU.subtract, ALU.mult).then_inc(done["y_ready"], 1)

            pool.wait_ge(done["st_scratch"], 2 * 16 * NT)
            pool.wait_ge(done["idx_ready"], 1)

            def gather(j):
                nc.gpsimd.indirect_dma_start(
                    out=YX[0:SLOT, j % 12].rearrange("p a f -> p (a f)"), out_offset=None, in_=scratch,
                    in_offset=bass.IndirectOffsetOnAxis(ap=idx[0:SLOT, 0, j:j + 1].bitcast(U32), axis=0)).then_inc(gathered[j], 16)

            for j in range(12):
                gather(j)
            pool.wait_ge(done["st_out"], 16 * NT)
            for j in range(NS):
                pool.wait_ge(done["fo_ready"], j + 1)
                nc.gpsimd.indirect_dma_start(
                    out=out, in_=FO[0:SLOT, j % 4, :], in_offset=None,
                    out_offset=bass.IndirectOffsetOnAxis(ap=idx[0:SLOT, 1, j:j + 1].bitcast(U32), axis=0),
                    bounds_check=N - 1, oob_is_err=False).then_inc(scattered[j % 4], 16)
                if j + 12 < NS:
                    gather(j + 12)

        @block.tensor
        def _(pe):
            def opens(name):
                for what, value in plan[name][2]:
                    pe.wait_ge(done[what], value)
                return PS[plan[name][0]]

            def closes(name, ins):
                ins.then_inc(full[plan[name][0]], 1)

            def product(name, ps, stationary, moving, chunks, between=None):
                pairs = [(a, b, c) for c in range(chunks) for a, b in ((0, 0), (0, 1), (1, 0))]
                for n, (a, b, c) in enumerate(pairs):
                    if n == 1 and between is not None:
                        between()
                    mm = pe.matmul(ps, stationary[a](c), moving[b](c), start=(n == 0), stop=(n == len(pairs) - 1))
                closes(name, mm)

            def block_of(t, f, w=128, off=0):
                return lambda c: t[:, c, f * w + off:(f + 1) * w + off]

            def rows_of(t):
                return lambda c: t[:, c, :]

            pe.wait_ge(done["consts"], 1)
            def turn_x(i):
                pe.wait_ge(done["xf_ready"], i + 1)
                opens(f"xt{i}")
                ps = view(f"xt{i}")
                for c in range(C):
                    mm = pe.transpose(ps[:, c, 0:TT], XF[0:TT, i, 128 * c:128 * (c + 1)], ident[0:TT, 0:TT])
                closes(f"xt{i}", mm)

            def tile_product(name, i, wh, wl):
                product(name, opens(name)[0:TT, :], (block_of(XTH, i, TT), block_of(XTL, i, TT)), (rows_of(wh), rows_of(wl)), C)

            for i in range(2):
                turn_x(i)
            for i in range(NT):
                if i == 4:
                    pe.wait_ge(done["grp_ready"], 1)
                    ps = opens("bounds")
                    for n in range(2):
                        mm = pe.matmul(ps[0:NB, NE_T * n:NE_T * (n + 1)], ones[0:NE_T // 2, 0:NB], dg2[0:NE_T // 2, n, :], start=True, stop=True)
                    closes("bounds", mm)
                if i == 7:
                    pe.wait_ge(done["blen_ready"], 1)
                    ps = opens("bases")
                    pe.matmul(ps[0:1, 0:NB + 1], blh[0:NB, 0:1], tri[0:NB, 0:NB + 1], start=True, stop=True)
                    closes("bases", pe.matmul(ps[0:1, 32:32 + NB], blh[0:NB, 1:2], ident[0:NB, 0:NB], start=True, stop=True))
                if i == 0:
                    pe.wait_ge(done["w_lo"], order["wk"])
                pe.wait_ge(done["xtl_ready"], i + 1)
                tile_product(f"k{i}", i, WKH, WKL)
                if i + 2 < NT:
                    turn_x(i + 2)
            pe.wait_ge(done["w_lo"], order["wq"])
            for i in range(NT):
                if i == 4:
                    pe.wait_ge(done["kmax_step"], NT)
                    opens("kmt")
                    for c in range(C):
                        mm = pe.transpose(view("kmt")[:, c, 0:TT], KMAX[0:TT, 128 * c:128 * (c + 1)], ident[0:TT, 0:TT])
                    closes("kmt", mm)
                if i == 7:
                    pe.wait_ge(done["diag_ready"], 1)
                    closes("kmb", pe.matmul(opens("kmb")[0:TT, :], ones[:, 0:TT], diag[:].rearrange("p c f -> p (c f)"),
                                            start=True, stop=True))
                tile_product(f"q{i}", i, WQH, WQL)
            pe.wait_ge(done["w_lo"], order["w1"])
            for c in range(C):
                ps = opens(f"mp{c}")
                product(f"mp{c}", ps[:], (block_of(W1H, c), block_of(W1L, c)), (rows_of(W2H), rows_of(W2L)), C,
                        between=lambda: pe.matmul(ps[:, 128 * c:128 * (c + 1)], ident[:], ident[:], start=False, stop=False))
            pe.wait_ge(done["mpl_ready"], C)
            for i in range(NT):
                tile_product(f"xm{i}", i, MPH, MPL)
            for s in range(UN):
                pe.sem_inc(hot_used[s], 1)
            pe.wait_ge(done["tab_ready"], 1)
            pe.wait_ge(done["zero_ready"], 1)
            _, starts = nc.values_load_multi_w_load_instructions(tab[0:1, 0, 0:NB + 1], engines=[mybir.EngineType.PE],
                                                                 min_val=0, max_val=NB * NE_T)
            pe.wait_ge(done["w_lo"], order["wv"])
            for c in range(C):
                product(f"vp{c}", opens(f"vp{c}")[:], (block_of(WVH, c), block_of(WVL, c)), (rows_of(MPH), rows_of(MPL)), C)
            def context(i):
                pe.wait_ge(done["el_ready"], i + 1)
                for c in range(C):
                    ps = opens(f"tt{c}") if i == 0 else PS[plan[f"tt{c}"][0]]
                    f = slice(128 * c, 128 * (c + 1))
                    pe.matmul(ps[:], XNH[0:TT, i, f], EH[0:TT, i % 4, :], start=(i == 0), stop=False)
                    pe.matmul(ps[:], XNH[0:TT, i, f], EL[0:TT, i % 4, :], start=False, stop=False)
                    mm = pe.matmul(ps[:], XNL[0:TT, i, f], EH[0:TT, i % 4, :], start=False, stop=(i == NT - 1))
                    if i == NT - 1:
                        closes(f"tt{c}", mm)
                    elif c == C - 1:
                        mm.then_inc(done["e_used"], 1)

            def values(_):
                pe.wait_ge(done["esum_ready"], 1)
                ps = opens("ks")
                for c in range(C):
                    mm = pe.matmul(ps[:, c:c + 1], ESUM[0:TT, 128 * c:128 * (c + 1)], ones[0:TT, 0:1], start=True, stop=True)
                closes("ks", mm)
                pe.wait_ge(done["tl_ready"], C)
                pe.wait_ge(done["vpl_ready"], C)
                for c in range(C):
                    product(f"cp{c}", opens(f"cp{c}")[:], (block_of(TH, c), block_of(TL, c)), (rows_of(VPH), rows_of(VPL)), C)
                turn_q(0)

            def turn_q(i):
                pe.wait_ge(done["q_ready"], i + 1)
                opens(f"qt{i}")
                for c in range(C):
                    mm = pe.transpose(view(f"qt{i}")[:, c, 0:TT], Q[0:TT, i, 128 * c:128 * (c + 1)], ident[0:TT, 0:TT])
                closes(f"qt{i}", mm)

            def attend(i):
                if i + 1 < NT:
                    turn_q(i + 1)
                pe.wait_ge(done["qtl_ready"], i + 1)
                if i == 0:
                    pe.wait_ge(done["cpl_ready"], C)
                product(f"qp{i}", opens(f"qp{i}")[0:TT, :],
                        (lambda c: QTH[:, i % 2, c, 0:TT], lambda c: QTL[:, i % 2, c, 0:TT]), (rows_of(CPH), rows_of(CPL)), C)

            for b in range(NB):
                if b < 2:
                    opens(f"adj{4 + 2 * b}")
                    opens(f"adj{5 + 2 * b}")
                if b >= 2:
                    pe.wait_ge(done["adj_hi"], b - 1)
                    pe.wait_ge(done["adj_lo"], b - 1)
                half = [PS[4 + 2 * (b % 2) + h] for h in range(2)]

                def add_zero(h, **flags):
                    return pe.matmul(half[h][0:TT, 0:5 * DB], zero[0:1, 0:TT], iota[0:1, 0:5 * DB], skip_group_check=True, **flags)

                for h in range(2):
                    add_zero(h, start=True, stop=False)
                with pe.Fori(starts[b], starts[b + 1]) as n:
                    for s in range(UN):
                        pe.wait_ge(hot[s], n + 1)
                        for k in range(NT):
                            mm = pe.matmul(half[k // 5][0:TT, (k % 5) * DB:(k % 5 + 1) * DB], HOT_S[0:ET, s, TT * k:TT * (k + 1)],
                                           HOT_D[0:ET, s, :], start=False, stop=False, skip_group_check=True)
                        mm.then_inc(hot_used[s], 1)
                for h in range(2):
                    mm = add_zero(h, start=False, stop=True)
                mm.then_inc(done["adj_full"], 1)
                for what, i in BEHIND[b]:
                    {"context": context, "values": values, "attend": attend}[what](i)

            large = []

            def aggregate(layer, hi, lo):
                for ch, (b0, b1) in enumerate(SPANS):
                    w = (b1 - b0) * DB
                    names = [f"z{layer}_{ch}_{f}" for f in range(C)] + ([f"deg{ch}"] if layer == 1 else [])

                    def operands(k, f):
                        if f == C:
                            return [onesr[0:TT, :]]
                        return [t[0:TT, k, 128 * f:128 * (f + 1)] for t in (hi, lo)]

                    def place(f):
                        return PS[plan[names[f]][0]][0:(2 if f == C else 128), 0:w]

                    def rows_ready(k):
                        if layer == 2 and ch == 0:
                            pe.wait_ge(done["h1l_ready"], k + 1)

                    for f, name in enumerate(names):
                        opens(name)
                        if layer == 1 and ch == 0 and f == 2:
                            pe.wait_ge(done["flag_in"], 1)
                            closes("flag", pe.matmul(opens("flag")[0:1, 0:1], many[0:TT, 1:2], ones[0:TT, 0:1], start=True, stop=True))
                        for k in range(NT - 1):
                            if f == 0:
                                rows_ready(k)
                            for n, a in enumerate(operands(k, f)):
                                pe.matmul(place(f), a, AT[0:TT, b0:b1, k, :], start=(k == 0 and n == 0), stop=False)
                    rows_ready(NT - 1)
                    if layer == 1 and ch == 0:
                        pe.wait_ge(done["flag_ready"], 1)
                        large.append(pe.value_load(flag[0:1, 0:1], min_val=0, max_val=1))
                    with pe.If(large[0] > 0):
                        for k in range(NT):
                            pe.wait_ge(done["ac_ready"], ((layer - 1) * 3 + ch) * NT + k + 1)
                            for f in range(len(names)):
                                for a in operands(k, f):
                                    mm = pe.matmul(place(f), a, AC[0:TT, k % 2, 0:b1 - b0, :], start=False, stop=False)
                            mm.then_inc(done["ac_used"], 1)
                    with pe.Else():
                        pe.nop()
                    for f, name in enumerate(names):
                        last = operands(NT - 1, f)
                        for n, a in enumerate(last):
                            mm = pe.matmul(place(f), a, AT[0:TT, b0:b1, NT - 1, :], start=False, stop=(n == len(last) - 1))
                        closes(name, mm)

            def dense(layer, name, i, wh, wl):
                span = min(ch for ch, (_, b1) in enumerate(SPANS) if b1 * DB >= TT * (i + 1))
                pe.wait_ge(done["zl_ready"], ((layer - 1) * 3 + span + 1) * C)
                product(name, opens(name)[0:TT, :], (block_of(ZH, i, TT), block_of(ZL, i, TT)), (rows_of(wh), rows_of(wl)), C)

            aggregate(1, XNH, XNL)
            pe.wait_ge(done["w_lo"], order["g1"])
            for i in range(NT):
                dense(1, f"h{i}", i, G1H, G1L)
                if i == 1:
                    pe.wait_ge(done["degrow_ready"], 3)
                    ps = opens("degt")
                    for k in range(NT):
                        mm = pe.matmul(ps[0:TT, k:k + 1], drow[0:1, TT * k:TT * (k + 1)], ones[0:1, 0:1], start=True, stop=True)
                    closes("degt", mm)
            aggregate(2, H1H, H1L)
            pe.wait_ge(done["w_lo"], order["g2"])

            def turn_y(i):
                reads_y(pe, i)
                opens(f"yt{i}")
                for c in range(C):
                    mm = pe.transpose(view(f"yt{i}")[:, c, 0:TT], Y[0:TT, i, 128 * c:128 * (c + 1)], ident[0:TT, 0:TT])
                closes(f"yt{i}", mm)

            def logits(i):
                pe.wait_ge(done["yt_ready"], i + 1)
                for c in range(C):
                    mm = pe.matmul(PS[plan["logits"][0]][0:TT, NE * i:NE * (i + 1)], YT[:, i % 2, c, 0:TT], gw[:, c, :],
                                   start=(c == 0), stop=(c == C - 1))
                if i == NT - 1:
                    closes("logits", mm)
                else:
                    mm.then_inc(done["yt_used"], 1)

            for i in range(NT + 5):
                if i < NT:
                    dense(2, f"o{i}", i, G2H, G2L)
                if 4 <= i < NT + 4:
                    turn_y(i - 4)
                if i == 5:
                    opens("logits")
                    pe.wait_ge(loads["gate"], 16)
                if i >= 5:
                    logits(i - 5)

            for r in range(SINKHORN):
                pe.wait_ge(done["p_ready"], r + 1)
                closes(f"sink{r}", pe.matmul(opens(f"sink{r}")[0:TT, 0:NE], ones[0:TT, 0:TT], s8[0:TT, 0, :],
                                             start=True, stop=True))
            pe.wait_ge(done["grep_ready"], 1)
            for h in range(3):
                opens(f"gt{h}")
                for i in range(4 * h, min(4 * h + 4, NT)):
                    mm = pe.transpose(view(f"gt{h}")[:, i % 4, 0:TT], GREP[0:TT, i, :], ident[0:TT, 0:TT])
                closes(f"gt{h}", mm)
            pe.wait_ge(done["rconsts"], 1)
            for r in range(len(SHIFTS)):
                pe.wait_ge(done["ind_ready"], r + 1)
                closes(f"rad{r}", pe.matmul(opens(f"rad{r}")[:, 0:1], blkones[:], reached[:, 0:1], start=True, stop=True))
            pe.wait_ge(done["msel_ready"], 1)
            ps = opens("sel")
            for i in range(NT):
                mm = pe.matmul(ps[0:TT, NE * i:NE * (i + 1)], M_SEL[:, TT * i:TT * (i + 1)], pick[:], start=True, stop=True)
            closes("sel", mm)
            pe.wait_ge(done["rowtot_ready"], 1)
            closes("off", pe.matmul(opens("off")[0:TT, 0:NE], tri[0:TT, 0:TT], s8[0:TT, 1, :], start=True, stop=True))
            ps = opens("slots")

            def slots_zero(**flags):
                return pe.matmul(ps[0:SLOT, 0:6 * NS], zero[0:1, 0:SLOT], iota[0:1, 0:6 * NS], skip_group_check=True, **flags)

            slots_zero(start=True, stop=False)
            for i in range(NT):
                pe.wait_ge(done["route_ready"], i + 1)
                for j in range(NS):
                    pe.matmul(ps[0:SLOT, 6 * j:6 * (j + 1)], ROUTE[0:TT, i, SLOT * j:SLOT * (j + 1)], vals[0:TT, i, :],
                              start=False, stop=False, skip_group_check=True)
            closes("slots", slots_zero(start=False, stop=True))

            for j in range(NS + 1):
                if j < NS:
                    pe.wait_ge(gathered[j], 16)
                    opens(f"ft{j}")
                    for c in range(C):
                        mm = pe.transpose(view(f"ft{j}")[:, c, 0:SLOT], YX[0:SLOT, j % 12, 0, 128 * c:128 * (c + 1)], ident[0:SLOT, 0:SLOT])
                    closes(f"ft{j}", mm)
                if j:
                    t = j - 1
                    e = t // 2
                    if e < 4:
                        pe.wait_ge(done["w_lo"], NW + e + 1)
                    else:
                        pe.wait_ge(done["el_split"], e - 3)
                    pe.wait_ge(done["ftl_ready"], t + 1)
                    product(f"fo{t}", opens(f"fo{t}")[0:SLOT, :],
                            (lambda c: FTH[:, t % 2, c, 0:SLOT], lambda c: FTL[:, t % 2, c, 0:SLOT]),
                            (rows_of(WEH[e % 4]), rows_of(WEL[e % 4])), C)

        @block.scalar
        def _(act):
            def copy(o, i, **kw):
                return nc.scalar.activation(o, i, ACT.Copy, **kw)

            def split_hi(n, raw, hi, load, value=16):
                act.wait_ge(loads[load], value)
                copy(hi[:], raw[:]).then_inc(done["w_hi"], 1)

            def split_named(name):
                n = order[name] - 1
                split_hi(n, splits[n][0], splits[n][1], name)

            def root(p):
                w = slice(*PARTS[p])
                act.wait_ge(done["var_ready"], p + 1)
                nc.scalar.activation(rstd[0:TT, 1, w], rstd[0:TT, 0, w], ACT.Sqrt).then_inc(done["sqrt_ready"], 1)

            root(0)
            split_named("wk")
            def round_x(i):
                act.wait_ge(done["xf_ready"], i + 1)
                copy(XNH[0:TT, i, :], XF[0:TT, i, :]).then_inc(done["xnh_ready"], 1)
                reads(act, f"xt{i}")
                copy(XTH[:, :, TT * i:TT * (i + 1)], view(f"xt{i}")[:, :, 0:TT]).then_inc(done["xth_ready"], 1)

            round_x(0)
            round_x(1)
            root(1)
            for i in range(NT):
                if i == 3:
                    split_named("wq")
                if i == 7:
                    reads(act, "bases")
                    split_named("w2")
                reads(act, f"k{i}")
                act.wait_ge(done["xnl_ready"], i + 1)
                ps = PS[plan[f"k{i}"][0]]
                copy(K[0:TT, i, :], ps[0:TT, :]).then_inc(done["k_stored"], 1)
                if i + 2 < NT:
                    round_x(i + 2)
                if i == 0:
                    root(2)
            for i in range(NT):
                if i == 3:
                    split_named("w1")
                ps = PS[plan[f"q{i}"][0]]
                act.wait_ge(done["rmax_ready"], i + 1)
                if i == 0:
                    act.wait_ge(done["w_lo"], order["wq"])
                nc.scalar.activation(Q[0:TT, i, :], ps[0:TT, :], ACT.Exp, bias=rmax[0:TT, i:i + 1],
                                     accum_out=rsum[0:TT, 0, i:i + 1]).then_inc(done["q_exp"], 1)
            for c in range(C):
                reads(act, f"mp{c}")
                copy(MPH[:, c, :], PS[plan[f"mp{c}"][0]][:]).then_inc(done["mph_ready"], 1)
            split_named("wv")
            for i in range(NT):
                act.wait_ge(done["k_shift"], i + 1)
                nc.scalar.activation(K[0:TT, i, :], K[0:TT, i, :], ACT.Exp).then_inc(done["k_exp"], 1)
            def round_exp(i):
                act.wait_ge(done["k_exp"], i + 1)
                if i >= 4:
                    act.wait_ge(done["e_used"], i - 3)
                copy(EH[0:TT, i % 4, :], K[0:TT, i, :]).then_inc(done["eh_ready"], 1)

            def block_counts(b):
                act.wait_ge(done["adj_full"], b + 1)
                for h in range(2):
                    src = PS[4 + 2 * (b % 2) + h][0:TT, 0:5 * DB]
                    ins = nc.scalar.activation(AT[0:TT, b, 5 * h:5 * h + 5, :].rearrange("p k d -> p (k d)"), src, ACT.Copy,
                                               accum_out=odeg[0:TT, h, b:b + 1])
                ins.then_inc(done["adj_hi"], 1)

            def round_q(i):
                reads(act, f"qt{i}")
                if i >= 2:
                    reads(act, f"qp{i - 2}")
                copy(QTH[:, i % 2, :, 0:TT], view(f"qt{i}")[:, :, 0:TT]).then_inc(done["qth_ready"], 1)

            for c in range(C):
                reads(act, f"vp{c}")
                copy(VPH[:, c, :], PS[plan[f"vp{c}"][0]][:]).then_inc(done["vph_ready"], 1)
                round_exp(c)
            for b in range(NB):
                if b >= 1:
                    block_counts(b - 1)
                if 1 <= b < 4:
                    round_exp(2 * b + 2)
                    round_exp(2 * b + 3)
                if b == 5:
                    reads(act, f"tt{C - 1}")
                    for c in range(C):
                        reads(act, f"tt{c}")
                        copy(TH[:, c, :], PS[plan[f"tt{c}"][0]][:]).then_inc(done["th_ready"], 1)
                if b == 6:
                    act.wait_ge(done["krs_ready"], 1)
                    for c in range(C):
                        reads(act, f"cp{c}")
                        copy(CPH[:, c, :], PS[plan[f"cp{c}"][0]][:], scale=krs[:, 1, c:c + 1]).then_inc(done["cph_ready"], 1)
                    round_q(0)
                for what, i in BEHIND[b]:
                    if what == "attend" and i + 1 < NT:
                        round_q(i + 1)
            block_counts(NB - 1)
            reads(act, f"qp{NT - 1}")
            split_named("g1")

            def z_hi(layer):
                for ch, (b0, b1) in enumerate(SPANS):
                    c0, w = b0 * DB, min(b1 * DB, N) - b0 * DB
                    for f in range(C):
                        name = f"z{layer}_{ch}_{f}"
                        reads(act, name)
                        if layer == 2 and ch == f == 0:
                            reads(act, f"h{NT - 1}")
                        copy(ZH[:, f, c0:c0 + w], PS[plan[name][0]][:, 0:w]).then_inc(done["zh_ready"], 1)

            z_hi(1)
            for i in range(NT):
                act.wait_ge(done["t_ready"], i + 1)
                nc.scalar.activation(H1H[0:TT, i, :], PS[plan[f"h{i}"][0]][0:TT, :], ACT.Relu).then_inc(done["h1h_ready"], 1)
            act.wait_ge(done["w_lo"], order["g1"])
            split_named("g2")
            z_hi(2)

            def split_expert(e):
                if e == 3:
                    act.wait_ge(done["st_out"], 16 * NT)
                    act.wait_ge(done["st_scratch"], 2 * 16 * NT)
                if e >= 4:
                    reads(act, f"fo{2 * (e - 4) + 1}")
                split_hi(NW + e, RAW_E[e % 2], WEH[e % 4], f"exp{e % 2}", 16 * (e // 2 + 1))

            def copy_yt(i):
                reads(act, f"yt{i}")
                if i >= 2:
                    act.wait_ge(done["yt_used"], i - 1)
                copy(YT[:, i % 2, :, 0:TT], view(f"yt{i}")[:, :, 0:TT]).then_inc(done["yt_ready"], 1)

            split_expert(0)
            for i in range(NT + 4):
                if i < NT and i % 2 == 1:
                    p = i // 2
                    act.wait_ge(done["var2_ready"], p + 1)
                    nc.scalar.activation(rstd[0:TT, 1, 2 * p:2 * p + 2], rstd[0:TT, 0, 2 * p:2 * p + 2],
                                         ACT.Sqrt).then_inc(done["sqrt2_ready"], 1)
                if i >= 4:
                    copy_yt(i - 4)
            split_expert(1)
            split_expert(2)
            split_expert(3)
            for h in range(3):
                reads(act, f"gt{h}")
                n = min(4, NT - 4 * h)
                copy(GT[:, TT * 4 * h:TT * (4 * h + n)].rearrange("p (i t) -> p i t", i=n),
                     view(f"gt{h}")[:, 0:n, 0:TT]).then_inc(done["gt_ready"], 1)
            for j in range(NS):
                reads(act, f"ft{j}")
                if j >= 2:
                    reads(act, f"fo{j - 2}")
                copy(FTH[:, j % 2, :, 0:SLOT], view(f"ft{j}")[:, :, 0:SLOT]).then_inc(done["fth_ready"], 1)
                if j % 2 == 1 and 4 <= (j + 5) // 2 < NE:
                    split_expert((j + 5) // 2)

        @block.vector
        def _(dve):
            V = nc.vector
            count = [0]

            def link(ins):
                count[0] += 1
                ins.then_inc(done["dve_chain"], 1)
                dve.wait_ge(done["dve_chain"], count[0])

            def after(name, value):
                dve.wait_ge(done[name], value)

            def ps_of(name):
                return PS[plan[name][0]]

            t = slice(0, TT)

            def variance(w, signal):
                V.tensor_scalar(rstd[t, 0, w], mv[t, w, 1], LN_EPS, None, ALU.add).then_inc(done[signal], 1)

            def inverse_root(w, signal):
                link(V.reciprocal(rstd[t, 2, w], rstd[t, 1, w]))
                link(V.tensor_tensor(rstd[t, 3, w], rstd[t, 2, w], rstd[t, 2, w], ALU.mult))
                link(V.tensor_tensor(rstd[t, 3, w], rstd[t, 3, w], rstd[t, 0, w], ALU.mult))
                link(V.tensor_scalar(rstd[t, 3, w], rstd[t, 3, w], -0.5, 1.5, ALU.mult, ALU.add))
                V.tensor_tensor(rstd[t, 2, w], rstd[t, 2, w], rstd[t, 3, w], ALU.mult).then_inc(done[signal], 1)

            def moments(p):
                for i in range(*PARTS[p]):
                    if i % 2 == 0:
                        dve.wait_ge(ld_x[i // 2], 16)
                    ins = V.bn_stats(stat[0:TT, i, :], X[0:TT, i, :])
                link(ins)
                for i in range(*PARTS[p]):
                    ins = V.bn_aggr(mv[0:TT, i, :], stat[0:TT, i, :])
                link(ins)
                variance(slice(*PARTS[p]), "var_ready")

            def normalise(p):
                after("sqrt_ready", p + 1)
                inverse_root(slice(*PARTS[p]), "inv_ready")
                after("inv_ready", p + 1)
                for i in range(*PARTS[p]):
                    V.tensor_scalar(XF[0:TT, i, :], X[0:TT, i, :], mv[0:TT, i, 0:1], rstd[0:TT, 2, i:i + 1],
                                    ALU.subtract, ALU.mult).then_inc(done["xf_ready"], 1)

            def x_left(i):
                after("xth_ready", i + 1)
                V.tensor_tensor(XTL[:, :, TT * i:TT * (i + 1)], view(f"xt{i}")[:, :, 0:TT],
                                XTH[:, :, TT * i:TT * (i + 1)].bitcast(F32), ALU.subtract).then_inc(done["xtl_ready"], 1)

            moments(0)
            normalise(0)
            moments(1)
            x_left(0)
            normalise(1)
            x_left(1)
            moments(2)
            x_left(2)
            normalise(2)
            x_left(3)

            G = NE_T // 2
            dve.wait_ge(loads["edges"], 48)
            V.tensor_reduce(grp[0:G, 0, :], DROW[0:G], AX, ALU.min)
            link(V.tensor_reduce(grp[0:G, 1, :], DROW[0:G], AX, ALU.max))
            after("consts", 1)
            V.tensor_copy(onesr[:], ones[:, 0:2])
            V.memset(zero[:], 0.0).then_inc(done["zero_ready"], 1)
            for n in range(2):
                for h in range(2):
                    ins = V.tensor_scalar(dg2[0:G, n, G * h:G * (h + 1)], ident[0:G, 0:G], grp[0:G, n, h:h + 1], None, ALU.mult)
            ins.then_inc(done["grp_ready"], 1)
            V.memset(srcf[0:ET, NE_T:NE_T + UN], -1.0)
            V.memset(dstf[0:ET, NE_T:NE_T + UN], -1.0)
            V.tensor_copy(srcf[0:ET, 0:NE_T], EDGE[0:ET, 0, :])
            V.tensor_copy(dstf[0:ET, 0:NE_T], EDGE[0:ET, 1, :])
            for i in range(NT):
                if i == 4:
                    reads(dve, "bounds")
                    ps = ps_of("bounds")
                    b_ = slice(0, NB)
                    link(V.tensor_scalar(bw[b_, 0, :], ps[b_, 0:NE_T], blk[b_, 1:2], None, ALU.is_le))
                    link(V.scalar_tensor_tensor(bw[b_, 1, :], ps[b_, NE_T:2 * NE_T], blk[b_, 0:1], bw[b_, 0, :], ALU.is_ge, ALU.mult))
                    V.tensor_tensor(bw[b_, 2, :], bw[b_, 1, :], gio[b_, 0, :], ALU.mult)
                    link(V.tensor_tensor(bw[b_, 3, :], bw[b_, 1, :], gio[b_, 1, :], ALU.mult))
                    V.tensor_reduce(blh[b_, 2:3], bw[b_, 2, :], AX, ALU.max)
                    link(V.tensor_reduce(blh[b_, 3:4], bw[b_, 3, :], AX, ALU.max))
                    link(V.tensor_scalar(blh[b_, 4:5], blh[b_, 3:4], -1.0, float(NE_T), ALU.mult, ALU.add))
                    link(V.tensor_scalar(blh[b_, 1:2], blh[b_, 4:5], float(NE_T - 1), None, ALU.min))
                    link(V.scalar_tensor_tensor(blh[b_, 5:6], blh[b_, 1:2], 1.0, blh[b_, 2:3], ALU.add, ALU.max))
                    link(V.tensor_tensor(blh[b_, 6:7], blh[b_, 5:6], blh[b_, 1:2], ALU.subtract))
                    V.tensor_scalar(bw[b_, 0, :], gio[b_, 2, :], blh[b_, 6:7], None, ALU.is_lt, ALU.add,
                                    accum_out=blh[b_, 0:1]).then_inc(done["blen_ready"], 1)
                if 4 <= i + 2 < NT:
                    x_left(i + 2)
                if i == 7:
                    reads(dve, "bases")
                    ps = ps_of("bases")
                    link(V.tensor_copy(tab[0:1, 0, 0:NB + 1], ps[0:1, 0:NB + 1]))
                    V.scalar_tensor_tensor(tab[0:1, 1, 0:NB], tab[0:1, 0, 0:NB], -float(UN), ps[0:1, 32:32 + NB], ALU.mult,
                                           ALU.add).then_inc(done["tab_ready"], 1)
                    after("tab_ready", 1)
                after("k_stored", i + 1)
                ps = ps_of(f"k{i}")[0:TT, :]
                if i == 0:
                    V.tensor_copy(KMAX[0:TT, :], ps).then_inc(done["kmax_step"], 1)
                else:
                    after("kmax_step", i)
                    V.tensor_tensor(KMAX[0:TT, :], ps, KMAX[0:TT, :], ALU.max).then_inc(done["kmax_step"], 1)

            def q_scale(i):
                after("q_exp", i + 1)
                link(V.reciprocal(rsum[0:TT, 1, i:i + 1], rsum[0:TT, 0, i:i + 1]))
                V.tensor_scalar(Q[0:TT, i, :], Q[0:TT, i, :], rsum[0:TT, 1, i:i + 1], None, ALU.mult).then_inc(done["q_ready"], 1)

            def shift(i):
                if i == 0:
                    reads(dve, "kmb")
                after("k_stored", i + 1)
                V.tensor_tensor(K[0:TT, i, :], K[0:TT, i, :], ps_of("kmb")[0:TT, :], ALU.subtract).then_inc(done["k_shift"], 1)

            for i in range(NT):
                reads(dve, f"q{i}")
                V.tensor_reduce(rmax[0:TT, i:i + 1], ps_of(f"q{i}")[0:TT, :], AX, ALU.max, negate=True).then_inc(done["rmax_ready"], 1)
                if i == 3:
                    reads(dve, "kmt")
                    link(V.tensor_reduce(kmt[:], view("kmt")[:, :, 0:TT], AX, ALU.max))
                    for c in range(C):
                        ins = V.tensor_scalar(diag[:, c, :], ident[:], kmt[:, c:c + 1], None, ALU.mult)
                    ins.then_inc(done["diag_ready"], 1)
                if i >= 1:
                    q_scale(i - 1)
                if i >= 8:
                    shift(i - 8)
            q_scale(NT - 1)
            for c in range(C):
                after("mph_ready", c + 1)
                V.tensor_tensor(MPL[:, c, :], ps_of(f"mp{c}")[:], MPH[:, c, :].bitcast(F32), ALU.subtract).then_inc(done["mpl_ready"], 1)
            for i in range(NT):
                if i + 2 < NT:
                    shift(i + 2)
                reads(dve, f"xm{i}")
                after("xf_ready", i + 1)
                V.tensor_tensor(X[0:TT, i, :], ps_of(f"xm{i}")[0:TT, :], X[0:TT, i, :], ALU.add).then_inc(done["xm_added"], 1)
            def exp_left(i):
                after("eh_ready", i + 1)
                V.tensor_tensor(EL[0:TT, i % 4, :], K[0:TT, i, :], EH[0:TT, i % 4, :].bitcast(F32), ALU.subtract).then_inc(done["el_ready"], 1)

            _, starts = nc.values_load_multi_w_load_instructions(tab[0:1, 0, 0:NB + 1], engines=[mybir.EngineType.DVE],
                                                                 min_val=0, max_val=NB * NE_T)
            _, behind = nc.values_load_multi_w_load_instructions(tab[0:1, 1, 0:NB], engines=[mybir.EngineType.DVE],
                                                                 min_val=-UN * NB * NE_T, max_val=NE_T)

            def values_left(c):
                after("vph_ready", c + 1)
                V.tensor_tensor(VPL[:, c, :], ps_of(f"vp{c}")[:], VPH[:, c, :].bitcast(F32), ALU.subtract).then_inc(done["vpl_ready"], 1)

            values_left(0)
            exp_left(0)
            values_left(1)
            exp_left(1)
            values_left(2)


            def counts_left(b):
                after("adj_hi", b + 1)
                for h in range(2):
                    src = PS[4 + 2 * (b % 2) + h][0:TT, 0:5 * DB].rearrange("p (k d) -> p k d", k=5)
                    ins = V.tensor_tensor(AL[0:TT, NB - 1 - b, 5 * h:5 * h + 5, :], src,
                                          AT[0:TT, b, 5 * h:5 * h + 5, :].bitcast(F32), ALU.subtract)
                ins.then_inc(done["adj_lo"], 1)

            def add_attention(i):
                reads(dve, f"qp{i}")
                V.tensor_tensor(X[0:TT, i, :], ps_of(f"qp{i}")[0:TT, :], X[0:TT, i, :], ALU.add).then_inc(done["qp_added"], 1)

            def context_left(c):
                after("cph_ready", c + 1)
                V.scalar_tensor_tensor(CPL[:, c, :], ps_of(f"cp{c}")[:], krs[:, 1, c:c + 1], CPH[:, c, :].bitcast(F32),
                                       ALU.mult, ALU.subtract).then_inc(done["cpl_ready"], 1)

            def q_left(i):
                after("qth_ready", i + 1)
                V.tensor_tensor(QTL[:, i % 2, :, 0:TT], view(f"qt{i}")[:, :, 0:TT], QTH[:, i % 2, :, 0:TT].bitcast(F32),
                                ALU.subtract).then_inc(done["qtl_ready"], 1)

            after("xm_added", NT)
            for b in range(NB):
                with dve.Fori(starts[b], starts[b + 1]) as n:
                    for s in range(UN):
                        col = nc.s_assert_within(UN * n + behind[b] + s, 0, NE_T + UN - 1,
                                                 skip_runtime_bounds_check_because="lo + UN (n - first) < hi + UN")
                        dve.wait_ge(hot_used[s], n + 1)
                        V.tensor_scalar(HOT_D[0:ET, s, :], iota[0:ET, DB * b:DB * (b + 1)], dstf[0:ET, bass.ds(col, 1)], None,
                                        ALU.is_equal)
                        V.tensor_scalar(HOT_S[0:ET, s, :], iota[0:ET, 0:N], srcf[0:ET, bass.ds(col, 1)], None,
                                        ALU.is_equal).then_inc(hot[s], 1)
                if b == 6:
                    for c in range(C):
                        after("th_ready", c + 1)
                        V.tensor_tensor(TL[:, c, :], ps_of(f"tt{c}")[:], TH[:, c, :].bitcast(F32), ALU.subtract).then_inc(done["tl_ready"], 1)
                if b >= 1:
                    counts_left(b - 1)
                if b == 0:
                    values_left(3)
                if b < 4:
                    exp_left(2 * b + 2)
                    exp_left(2 * b + 3)
                if b == 6:
                    reads(dve, "ks")
                    link(V.reciprocal(krs[:, 0, :], ps_of("ks")[:, 0:C]))
                    V.tensor_scalar(krs[:, 1, :], krs[:, 0, :], float(D) ** -0.5, None, ALU.mult).then_inc(done["krs_ready"], 1)
                    for c in range(C - 1):
                        context_left(c)
                if b == 7:
                    context_left(C - 1)
                    q_left(0)
                for what, i in BEHIND[b]:
                    if what == "attend":
                        if i + 1 < NT:
                            q_left(i + 1)
                        if i >= 1:
                            add_attention(i - 1)
            counts_left(NB - 1)
            add_attention(NT - 1)

            link(V.tensor_reduce(many[0:TT, 0:1], odeg[0:TT], mybir.AxisListType.XY, ALU.add))
            V.tensor_scalar(many[0:TT, 1:2], many[0:TT, 0:1], EXACT, None, ALU.is_gt).then_inc(done["flag_in"], 1)
            reads(dve, "flag")
            V.tensor_scalar(flag[0:1, 0:1], ps_of("flag")[0:1, 0:1], 0.5, None, ALU.is_gt).then_inc(done["flag_ready"], 1)
            after("flag_ready", 1)
            large = dve.value_load(flag[0:1, 0:1], min_val=0, max_val=1)

            def aggregate(layer):
                for ch, (b0, b1) in enumerate(SPANS):
                    c0, w = b0 * DB, min(b1 * DB, N) - b0 * DB
                    with dve.If(large > 0):
                        for k in range(NT):
                            n = ((layer - 1) * 3 + ch) * NT + k
                            if n >= 2:
                                after("ac_used", n - 1)
                            for b in range(b0, b1):
                                ins = V.tensor_copy(AC[0:TT, k % 2, b - b0, :], AL[0:TT, NB - 1 - b, k, :])
                            ins.then_inc(done["ac_ready"], 1)
                    with dve.Else():
                        dve.nop()
                    for f in range(C):
                        n = ((layer - 1) * 3 + ch) * C + f + 1
                        after("zh_ready", n)
                        V.tensor_tensor(ZL[:, f, c0:c0 + w], ps_of(f"z{layer}_{ch}_{f}")[:, 0:w], ZH[:, f, c0:c0 + w].bitcast(F32),
                                        ALU.subtract).then_inc(done["zl_ready"], 1)
                    if layer == 1:
                        reads(dve, f"deg{ch}")
                        V.tensor_copy(drow[0:1, c0:c0 + w], ps_of(f"deg{ch}")[0:1, 0:w]).then_inc(done["degrow_ready"], 1)

            aggregate(1)
            reads(dve, "degt")
            V.tensor_copy(degs[0:TT, :], ps_of("degt")[0:TT, 0:NT]).then_inc(done["deg_ready"], 1)
            after("deg_ready", 1)
            dve.wait_ge(loads["b1"], 16)
            for i in range(NT + 1):
                if i < NT:
                    reads(dve, f"h{i}")
                    ps = ps_of(f"h{i}")[0:TT, :]
                    V.scalar_tensor_tensor(ps, bias[0:TT, :], degs[0:TT, i:i + 1], ps, ALU.mult, ALU.add).then_inc(done["t_ready"], 1)
                if i:
                    after("h1h_ready", i)
                    V.scalar_tensor_tensor(H1L[0:TT, i - 1, :], ps_of(f"h{i - 1}")[0:TT, :], 0.0, H1H[0:TT, i - 1, :].bitcast(F32),
                                           ALU.max, ALU.subtract).then_inc(done["h1l_ready"], 1)
            aggregate(2)
            dve.wait_ge(loads["b2"], 16)

            def layernorm_of(p):
                after("sqrt2_ready", p + 1)
                inverse_root(slice(2 * p, 2 * p + 2), "inv2_ready")
                if 2 * p >= YP:
                    after("inv2_ready", p + 1)
                    for i in (2 * p, 2 * p + 1):
                        V.tensor_scalar(Y[0:TT, i, :], X[0:TT, i, :], mv[0:TT, i, 0:1], rstd[0:TT, 2, i:i + 1],
                                        ALU.subtract, ALU.mult).then_inc(done["ylast_ready"], 1)

            for i in range(NT):
                reads(dve, f"o{i}")
                ps = ps_of(f"o{i}")[0:TT, :]
                link(V.scalar_tensor_tensor(ps, bias[0:TT, :], degs[0:TT, i:i + 1], ps, ALU.mult, ALU.add))
                V.scalar_tensor_tensor(X[0:TT, i, :], ps, 0.0, X[0:TT, i, :], ALU.max, ALU.add).then_inc(done["x_final"], 1)
                after("x_final", i + 1)
                link(V.bn_stats(stat[0:TT, i, :], X[0:TT, i, :]))
                link(V.bn_aggr(mv[0:TT, i, :], stat[0:TT, i, :]))
                if i % 2 == 1:
                    variance(slice(i - 1, i + 1), "var2_ready")
                elif i >= 2:
                    layernorm_of(i // 2 - 1)
            layernorm_of(NT // 2 - 1)

            after("rconsts", 1)
            for r, s in enumerate(SHIFTS):
                V.tensor_scalar(ctab[:, r:r + 1], cb[:, 0:1], 15 if s else 7, s, ALU.bitwise_and, ALU.logical_shift_left)
            V.memset(pre[:, 0:1], 0)
            V.tensor_scalar(pre[:, 1:2], cb[:, 0:1], 15, SHIFTS[0], ALU.bitwise_and, ALU.logical_shift_left)
            reads(dve, "logits")
            link(V.tensor_scalar(P8[t], ps_of("logits")[t, 0:NT * NE].rearrange("p (i e) -> p i e", e=NE), CLIP_EPS, None, ALU.max))
            for r in range(SINKHORN):
                V.tensor_reduce(s8[t, 0, :], P8[t].rearrange("p i e -> p e i"), AX, ALU.add).then_inc(done["p_ready"], 1)
                reads(dve, f"sink{r}")
                link(V.reciprocal(s8[t, 1, :], ps_of(f"sink{r}")[t, 0:NE]))
                link(V.tensor_tensor(P8[t], P8[t], s8[t, 1:2, :].broadcast_to([TT, NT, NE]), ALU.mult))
                link(V.tensor_reduce(s10[t, 0, :], P8[t], AX, ALU.add))
                link(V.reciprocal(s10[t, 1, :], s10[t, 0, :]))
                link(V.tensor_tensor(P8[t], P8[t], s10[t, 1, :].unsqueeze(2).broadcast_to([TT, NT, NE]), ALU.mult))
            V.tensor_copy(GREP[t].rearrange("p i (e c) -> p (i e) c", c=16),
                          P8[t].rearrange("p i e -> p (i e)").unsqueeze(2).broadcast_to([TT, NT * NE, 16])).then_inc(done["grep_ready"], 1)

            after("gt_ready", 3)
            for r, s in enumerate(SHIFTS):
                link(V.tensor_scalar(M_GT[:], GT[:], pre[:, 1:2].bitcast(F32), None, ALU.is_ge, ALU.add, accum_out=cnt[:, 0:1]))
                V.tensor_scalar(reached[:, 0:1], cnt[:, 0:1], float(TOPK), None, ALU.is_ge).then_inc(done["ind_ready"], 1)
                reads(dve, f"rad{r}")
                twice = 1 if s else 2
                link(V.tensor_scalar(pre[:, 2:3], ps_of(f"rad{r}")[:, 0:1], float(2 ** s) / twice, -float(2 ** s), ALU.mult, ALU.add))
                if s:
                    V.scalar_tensor_tensor(pre[:, 1:2], pre[:, 2:3], pre[:, 0:1], ctab[:, r + 1:r + 2], ALU.bitwise_or,
                                           ALU.bitwise_or)
                V.tensor_tensor(pre[:, 0:1], pre[:, 0:1], pre[:, 2:3], ALU.bitwise_or).then_inc(done["prefix_ready"], 1)
                after("prefix_ready", r + 1)
            kth = pre[:, 0:1].bitcast(F32)
            V.tensor_scalar(M_GT[:], GT[:], kth, None, ALU.is_gt, ALU.add, accum_out=cnt[:, 2:3])
            link(V.tensor_scalar(M_EQ[:], GT[:], kth, None, ALU.is_equal))
            V.tensor_scalar(cnt[:, 3:4], cnt[:, 2:3], -1.0, float(TOPK), ALU.mult, ALU.add)
            link(V.tensor_tensor_scan(RANK[:], M_EQ[:], M_EQ[:], 0.0, ALU.add, ALU.max))
            link(V.scalar_tensor_tensor(M_TIE[:], RANK[:], cnt[:, 3:4], M_EQ[:], ALU.is_le, ALU.mult))
            V.tensor_tensor(M_SEL[:], M_GT[:], M_TIE[:], ALU.add).then_inc(done["msel_ready"], 1)

            V.tensor_scalar(tid[t, 1, :], tid[t, 0, :], 31, None, ALU.bitwise_and)
            reads(dve, "sel")
            link(V.tensor_tensor(w8[t, 0].rearrange("p e i -> p (e i)"), ps_of("sel")[t, 0:NT * NE],
                                 e1[t].rearrange("p i e -> p (i e)"), ALU.mult))
            taken = w8[t, 0].rearrange("p e i -> p (e i)").rearrange("p (i e) -> p i e", e=NE)
            link(V.tensor_reduce(s10[t, 0, :], taken, AX, ALU.max))
            last = w8[t, 1].rearrange("p e i -> p (e i)").rearrange("p (i e) -> p i e", e=NE)
            link(V.tensor_tensor(last, taken, s10[t, 0, :].unsqueeze(2).broadcast_to([TT, NT, NE]), ALU.is_equal))
            by_token = fin[t].rearrange("p e i -> p i e")
            link(V.scalar_tensor_tensor(by_token, taken, 0.0, last, ALU.is_gt, ALU.mult))
            link(V.tensor_tensor_scan(incl[t].rearrange("p e i -> p (e i)"), reset[t].rearrange("p e i -> p (e i)"),
                                      fin[t].rearrange("p e i -> p (e i)"), 0.0, ALU.mult, ALU.add))
            V.tensor_copy(s8[t, 1, :], incl[t, :, NT - 1]).then_inc(done["rowtot_ready"], 1)
            V.tensor_tensor(w8[t, 0], fin[t], P8[t].rearrange("p i e -> p e i"), ALU.mult)
            V.tensor_copy(vals[t, :, 1], tid[t, 1, :])
            link(V.tensor_tensor(vals[t, :, 0], tid[t, 0, :], tid[t, 1, :], ALU.subtract))
            link(V.tensor_reduce(s10[t, 1, :], w8[t, 0].rearrange("p e i -> p i e"), AX, ALU.add))
            link(V.tensor_copy(vals[t, :, 2], s10[t, 1, :]))
            link(V.tensor_tensor(s10[t, 2, :], s10[t, 1, :], vals[t, :, 2], ALU.subtract))
            link(V.tensor_copy(vals[t, :, 3], s10[t, 2, :]))
            V.tensor_tensor(vals[t, :, 4], s10[t, 2, :], vals[t, :, 3], ALU.subtract)
            V.memset(vals[t, :, 5], 0.0)
            reads(dve, "off")
            link(V.tensor_tensor(w8[t, 0], incl[t], ps_of("off")[t, 0:NE].unsqueeze(2).broadcast_to([TT, NE, NT]), ALU.add))
            link(V.tensor_tensor(w8[t, 1], w8[t, 0], e156[t].unsqueeze(2).broadcast_to([TT, NE, NT]), ALU.add))
            link(V.tensor_tensor(w8[t, 0], w8[t, 1], fin[t], ALU.mult))
            link(V.tensor_reduce(s10[t, 3, :], w8[t, 0].rearrange("p e i -> p i e"), AX, ALU.add))
            link(V.tensor_scalar(slot[t, :], s10[t, 3, :], -1.0, None, ALU.add))
            for i in range(NT):
                V.tensor_scalar(ROUTE[t, i, :], iota[t, 0:NS * SLOT], slot[t, i:i + 1], None, ALU.is_equal).then_inc(done["route_ready"], 1)
            reads(dve, "slots")
            u = slice(0, SLOT)
            ps = ps_of("slots")[u, 0:6 * NS].rearrange("p (j c) -> p j c", c=6)
            V.tensor_reduce(tokv[u, 1, :], ps[:, :, 2:5], AX, ALU.add)
            link(V.tensor_reduce(tokv[u, 0, :], ps[:, :, 0:2], AX, ALU.add))
            V.tensor_scalar(idx[u, 0, :], tokv[u, 0, :], -1.0, 0.0, ALU.add, ALU.max)
            link(V.tensor_scalar(tokv[u, 2, :], tokv[u, 0, :], 0.0, 8192.0, ALU.is_equal, ALU.mult))
            V.scalar_tensor_tensor(idx[u, 1, :], tokv[u, 0, :], -1.0, tokv[u, 2, :], ALU.add, ALU.add).then_inc(done["idx_ready"], 1)

            after("idx_ready", 1)
            for j in range(NS + 1):
                if j < NS:
                    after("fth_ready", j + 1)
                    V.tensor_tensor(FTL[:, j % 2, :, 0:SLOT], view(f"ft{j}")[:, :, 0:SLOT], FTH[:, j % 2, :, 0:SLOT].bitcast(F32),
                                    ALU.subtract).then_inc(done["ftl_ready"], 1)
                if j:
                    n = j - 1
                    reads(dve, f"fo{n}")
                    dve.wait_ge(gathered[n], 16)
                    if n >= 4:
                        dve.wait_ge(scattered[n % 4], 16 * (n // 4))
                    V.scalar_tensor_tensor(FO[u, n % 4, :], ps_of(f"fo{n}")[u, :], tokv[u, 1, n:n + 1], YX[u, n % 12, 1, :],
                                           ALU.mult, ALU.add).then_inc(done["fo_ready"], 1)
                    e = j // 2 + 2
                    if 4 <= e < NE:
                        after("w_hi", NW + e + 1)
                        half = slice(C // 2 * (j % 2), C // 2 * (j % 2 + 1))
                        ins = V.tensor_tensor(WEL[e % 4][:, half, :], RAW_E[e % 2][:, half, :], WEH[e % 4][:, half, :].bitcast(F32),
                                              ALU.subtract)
                        if j % 2 == 1:
                            ins.then_inc(done["el_split"], 1)



_OUT = ((N, D), "float32")


def kernel(**inputs):
    import numpy as _np
    import concourse.bacc as _bacc
    from concourse import mybir as _mybir
    from concourse.bass_utils import run_bass_kernel_spmd as _run

    def tr(name):
        return _np.ascontiguousarray(_np.asarray(inputs[name]).T)

    def edges(name):
        return _np.ascontiguousarray(_np.asarray(inputs[name]).reshape(NE_T, ET).T)

    host = {
        "x": _np.asarray(inputs["x"]), "src_t": edges("src"), "dst_t": edges("dst"),
        "dst_rows": _np.asarray(inputs["dst"]).reshape(NE_T // 2, 2, ET),
        "gW1T": tr("L0_gnn_W1"), "gb1": _np.asarray(inputs["L0_gnn_b1"]),
        "gW2T": tr("L0_gnn_W2"), "gb2": _np.asarray(inputs["L0_gnn_b2"]),
        "WqT": tr("L0_mix_Wq"), "WkT": tr("L0_mix_Wk"), "Wv": _np.asarray(inputs["L0_mix_Wv"]),
        "mW1": _np.asarray(inputs["L0_mix_W1"]), "mW2T": tr("L0_mix_W2"),
        "gate": _np.asarray(inputs["L0_ffn_gate_weight"]), "experts": _np.asarray(inputs["L0_ffn_experts"]),
    }
    nc = _bacc.Bacc("TRN2", target_bir_lowering=False, num_devices=1)
    arrays, args = {}, []
    for name, a in host.items():
        a = _np.ascontiguousarray(a)
        arrays[f"in_{name}"] = a
        args.append(nc.dram_tensor(f"in_{name}", a.shape, _mybir.dt.from_np(a.dtype), kind="ExternalInput").ap())
    out = nc.dram_tensor("out_x", _OUT[0], _mybir.dt.float32, kind="ExternalOutput").ap()
    gps_block(nc, *args, out)
    r = _run(nc, [arrays], core_ids=[0])
    return r.results[0]["out_x"]
```
